# Optimizing a Trainium2 kernel written in Bass

```python
import numpy as np
import jax
import jax.numpy as jnp

def _softmax(x, axis=-1):
    return jax.nn.softmax(x, axis=axis)

def _gelu(x):
    return jax.nn.gelu(x, approximate=True)

def _silu(x):
    return jax.nn.silu(x)

def _sigmoid(x):
    return jax.nn.sigmoid(x)

def _layernorm(x, axis=-1, eps=1e-05):
    m = jnp.mean(x, axis=axis, keepdims=True)
    v = jnp.var(x, axis=axis, keepdims=True)
    return (x - m) / jnp.sqrt(v + eps)

def _scatter_add(tgt, idx, src, axis=0):
    return tgt.at[idx].add(src)

def _segment_sum(src, seg, n):
    return jax.ops.segment_sum(src, seg, n)
kernel_name = 'mk_sandwich_d2_jaxref_r8_6d8de4'

def setup_inputs(seed: int=0):
    np.random.seed(seed)
    _w = jnp.asarray

    def _L0_attn_setup():
        import jax, jax.numpy as jnp
        import numpy as np
        B_, L_, D_, N_ = (16, 128, 128, 8)

        def soft_clamp(x, mn, mx, sharp):
            c = (mx + mn) / 2.0
            r = (mx - mn) / 2.0
            xn = (x - c) / (r + 1e-08)
            return jnp.tanh(xn * sharp) / sharp * r + c

        def _forward(x, W_dt, b_dt, W_B, W_C, A_log, D_param):
            Bb, L, D = x.shape
            N = W_B.shape[0]
            dt = soft_clamp(jax.nn.softplus(jnp.einsum('bld,ed->ble', x, W_dt) + b_dt), 0.001, 0.1, 0.5)
            Bp = jnp.einsum('bld,nd->bln', x, W_B)
            Cp = jnp.einsum('bld,nd->bln', x, W_C)
            A = -jnp.exp(soft_clamp(A_log, -5.0, 5.0, 0.5))

            def step(h, inp):
                t, x_t, dt_t, B_t, C_t = inp
                dA = jnp.exp(soft_clamp(dt_t[:, :, None] * A[None], -8.0, 8.0, 0.5))
                h = h * dA + (dt_t * x_t)[:, :, None] * B_t[:, None, :]
                hnorm = jnp.sqrt(jnp.sum(h.astype(jnp.float32) ** 2, axis=(1, 2), keepdims=True))
                scale = jnp.minimum(20.0 / (hnorm + 1e-08), 1.0).astype(h.dtype)
                h = jnp.where(t % 10 == 0, h * scale, h)
                y = jnp.einsum('bdn,bn->bd', h, C_t) + D_param * x_t
                return (h, y)
            h0 = jnp.zeros((Bb, D, N), dtype=x.dtype)
            ts = jnp.arange(L)
            xs = (ts, jnp.swapaxes(x, 0, 1), jnp.swapaxes(dt, 0, 1), jnp.swapaxes(Bp, 0, 1), jnp.swapaxes(Cp, 0, 1))
            _, ys = jax.lax.scan(step, h0, xs)
            return jnp.swapaxes(ys, 0, 1)
        key = jax.random.key(seed)
        ks = jax.random.split(key, 6)
        x = jax.random.normal(ks[0], (B_, L_, D_), dtype=jnp.float32)
        W_dt = jax.random.normal(ks[1], (D_, D_), dtype=jnp.float32) * 0.02
        b_dt = jnp.full((D_,), -2.0, dtype=jnp.float32)
        W_B = jax.random.normal(ks[2], (N_, D_), dtype=jnp.float32) * (1.0 / np.sqrt(D_))
        W_C = jax.random.normal(ks[3], (N_, D_), dtype=jnp.float32) * (1.0 / np.sqrt(D_))
        A_log = jax.random.normal(ks[4], (D_, N_), dtype=jnp.float32) * 0.1
        D_param = jnp.full((D_,), 0.1, dtype=jnp.float32)
        return {'x': x, 'W_dt': W_dt, 'b_dt': b_dt, 'W_B': W_B, 'W_C': W_C, 'A_log': A_log, 'D_param': D_param}
    _L0_attn_in = _L0_attn_setup()

    def _L0_ffn_setup():
        import jax, jax.numpy as jnp
        import numpy as np
        DIM = 128
        DEPTH = 2
        HEADS = 8
        DIM_HEAD = 64
        WINDOW = 64
        INNER = HEADS * DIM_HEAD
        HID = int(DIM * 4 * 2 / 3)
        B, N = (2, 1024)
        QK_SCALE = 8.0

        def shift_token(t):
            t1, t2 = jnp.split(t, 2, axis=-1)
            t2 = jnp.pad(t2, ((0, 0), (1, 0), (0, 0)))[:, :-1]
            return jnp.concatenate([t1, t2], axis=-1)

        def l2norm(t):
            return t / jnp.clip(jnp.linalg.norm(t, axis=-1, keepdims=True), 1e-12)

        def rotate_half(x):
            x1, x2 = jnp.split(x, 2, axis=-1)
            return jnp.concatenate([-x2, x1], axis=-1)

        def rotary_xpos(q, k):
            n = q.shape[-2]
            half_idx = jnp.arange(0, DIM_HEAD, 2, dtype=jnp.float32)
            inv_freq = 1.0 / 10000.0 ** (half_idx / DIM_HEAD)
            t = jnp.arange(n, dtype=jnp.float32)
            freqs = t[:, None] * inv_freq[None, :]
            freqs = jnp.concatenate([freqs, freqs], axis=-1)
            base = (half_idx + 0.4 * DIM_HEAD) / (1.4 * DIM_HEAD)
            power = (t - n // 2) / float(WINDOW // 2)
            scale = base[None, :] ** power[:, None]
            scale = jnp.concatenate([scale, scale], axis=-1)
            cos, sin = (jnp.cos(freqs), jnp.sin(freqs))
            q = q * cos * scale + rotate_half(q) * sin * scale
            k = k * cos / scale + rotate_half(k) * sin / scale
            return (q, k)

        def local_attention(q, k, v):
            b, h, n, d = q.shape
            w = n // WINDOW
            bq = q.reshape(b, h, w, WINDOW, d) * QK_SCALE
            bk = k.reshape(b, h, w, WINDOW, d)
            bv = v.reshape(b, h, w, WINDOW, d)

            def look_around(t):
                p = jnp.pad(t, ((0, 0), (0, 0), (1, 0), (0, 0), (0, 0)))
                return jnp.concatenate([p[:, :, :w], p[:, :, 1:]], axis=3)
            bk, bv = (look_around(bk), look_around(bv))
            bt = jnp.arange(n).reshape(w, WINDOW)
            btp = jnp.pad(bt, ((1, 0), (0, 0)), constant_values=-1)
            btk = jnp.concatenate([btp[:w], btp[1:]], axis=1)
            sim = jnp.einsum('bhwid,bhwjd->bhwij', bq, bk)
            i = bt[:, :, None]
            j = btk[:, None, :]
            mask = (i < j) | (i > j + WINDOW) | (j == -1)
            sim = jnp.where(mask, -jnp.finfo(sim.dtype).max, sim)
            attn = jax.nn.softmax(sim, axis=-1)
            out = jnp.einsum('bhwij,bhwjd->bhwid', attn, bv)
            return out.reshape(b, h, n, d)

        def _layer(x, wqkv, qs, ksc, wo, lg, lb, w1, b1, w2, b2):
            b, n, _ = x.shape
            h = shift_token(x)
            qkv = h @ wqkv
            q, k, v = jnp.split(qkv, 3, axis=-1)
            to_heads = lambda t: t.reshape(b, n, HEADS, DIM_HEAD).transpose(0, 2, 1, 3)
            q, k, v = (to_heads(q), to_heads(k), to_heads(v))
            q = l2norm(q) * qs
            k = l2norm(k) * ksc
            q, k = rotary_xpos(q, k)
            o = local_attention(q, k, v)
            o = o.transpose(0, 2, 1, 3).reshape(b, n, INNER)
            x = x + o @ wo
            h = shift_token(x)
            mu = h.mean(-1, keepdims=True)
            var = h.var(-1, keepdims=True)
            h = (h - mu) / jnp.sqrt(var + 1e-05) * lg + lb
            h = h @ w1 + b1
            a, g = jnp.split(h, 2, axis=-1)
            h = a * jax.nn.gelu(g, approximate=False)
            x = x + h @ w2 + b2
            return x
        key = jax.random.key(seed)
        ks = jax.random.split(key, 6)
        return {'x': jax.random.normal(ks[0], (B, N, DIM), jnp.float32), 'wqkv': jax.random.normal(ks[1], (DEPTH, DIM, 3 * INNER), jnp.float32) * 0.02, 'q_scale': jnp.ones((DEPTH, DIM_HEAD), jnp.float32), 'k_scale': jnp.ones((DEPTH, DIM_HEAD), jnp.float32), 'wo': jax.random.normal(ks[2], (DEPTH, INNER, DIM), jnp.float32) * 0.02, 'ln_g': jnp.ones((DEPTH, DIM), jnp.float32), 'ln_b': jnp.zeros((DEPTH, DIM), jnp.float32), 'w1': jax.random.normal(ks[3], (DEPTH, DIM, 2 * HID), jnp.float32) * 0.02, 'b1': jnp.zeros((DEPTH, 2 * HID), jnp.float32), 'w2': jax.random.normal(ks[4], (DEPTH, HID, DIM), jnp.float32) * 0.02, 'b2': jnp.zeros((DEPTH, DIM), jnp.float32)}
    _L0_ffn_in = _L0_ffn_setup()

    def _L1_attn_setup():
        import jax, jax.numpy as jnp
        import numpy as np
        BATCH, SEQ, D_MODEL = (4, 256, 128)
        D_STATE, D_CONV, EXPAND, HEADDIM = (64, 4, 2, 64)
        D_INNER = EXPAND * D_MODEL
        NHEADS = D_INNER // HEADDIM
        CONV_DIM = D_INNER + 2 * D_STATE
        D_IN_PROJ = 2 * D_INNER + 2 * D_STATE + NHEADS
        EPS = 1e-05

        def mamba2(X, W_in, conv_w, conv_b, dt_bias, A_log, D, norm_w, W_out):
            b, l, _ = X.shape
            zxbcdt = X @ W_in.T
            z, xBC, dt = jnp.split(zxbcdt, [D_INNER, D_INNER + CONV_DIM], axis=-1)
            dt = jax.nn.softplus(dt + dt_bias)
            xBC_t = xBC.transpose(0, 2, 1)
            ker = conv_w[:, None, :]
            xBC_c = jax.lax.conv_general_dilated(xBC_t, ker, window_strides=(1,), padding=[(D_CONV - 1, 0)], feature_group_count=CONV_DIM)
            xBC = jax.nn.silu(xBC_c.transpose(0, 2, 1) + conv_b)
            x, Bm, Cm = jnp.split(xBC, [D_INNER, D_INNER + D_STATE], axis=-1)
            xh = x.reshape(b, l, NHEADS, HEADDIM)
            A = -jnp.exp(A_log)
            dA = jnp.exp(dt * A)
            dBx = jnp.einsum('blh,bln,blhp->blhpn', dt, Bm, xh)

            def step(h, inp):
                dA_t, dBx_t, C_t = inp
                h = h * dA_t[:, :, None, None] + dBx_t
                y = jnp.einsum('bhpn,bn->bhp', h, C_t)
                return (h, y)
            h0 = jnp.zeros((b, NHEADS, HEADDIM, D_STATE), X.dtype)
            _, ys = jax.lax.scan(step, h0, (dA.transpose(1, 0, 2), dBx.transpose(1, 0, 2, 3, 4), Cm.transpose(1, 0, 2)))
            y = ys.transpose(1, 0, 2, 3) + D[None, None, :, None] * xh
            y = y.reshape(b, l, D_INNER)
            y = y * jax.nn.silu(z)
            y = y * jax.lax.rsqrt(jnp.mean(y * y, axis=-1, keepdims=True) + EPS) * norm_w
            return y @ W_out.T
        key = jax.random.key(seed)
        ks = jax.random.split(key, 6)
        s = 0.02
        return {'X': jax.random.normal(ks[0], (BATCH, SEQ, D_MODEL), jnp.float32), 'W_in': jax.random.normal(ks[1], (D_IN_PROJ, D_MODEL), jnp.float32) * s, 'conv_w': jax.random.normal(ks[2], (CONV_DIM, D_CONV), jnp.float32) * s, 'conv_b': jnp.zeros((CONV_DIM,), jnp.float32), 'dt_bias': jax.random.uniform(ks[3], (NHEADS,), jnp.float32), 'A_log': jnp.log(jax.random.uniform(ks[4], (NHEADS,), jnp.float32, minval=1.0, maxval=16.0)), 'D': jnp.ones((NHEADS,), jnp.float32), 'norm_w': jnp.ones((D_INNER,), jnp.float32), 'W_out': jax.random.normal(ks[5], (D_MODEL, D_INNER), jnp.float32) * s}
    _L1_attn_in = _L1_attn_setup()

    def _L1_ffn_setup():
        import jax, jax.numpy as jnp
        import numpy as np
        B, S, D, F, E = (8, 128, 128, 512, 8)
        EPS = 1e-05
        key = jax.random.key(seed)
        ks = jax.random.split(key, 4)
        s = 0.02
        return {'input_features': jax.random.normal(ks[0], (B, S, D), jnp.float32), 'centroids': jax.random.normal(ks[1], (E, D), jnp.float32) * 0.1, 'ln_g': jnp.ones((E, D), jnp.float32), 'ln_b': jnp.zeros((E, D), jnp.float32), 'w1': jax.random.normal(ks[2], (E, D, F), jnp.float32) * s, 'b1': jnp.zeros((E, F), jnp.float32), 'w2': jax.random.normal(ks[3], (E, F, D), jnp.float32) * s, 'b2': jnp.zeros((E, D), jnp.float32)}
    _L1_ffn_in = _L1_ffn_setup()
    _d = {'L0_attn_x': _L0_attn_in['x'], 'L0_attn_W_dt': _L0_attn_in['W_dt'], 'L0_attn_b_dt': _L0_attn_in['b_dt'], 'L0_attn_W_B': _L0_attn_in['W_B'], 'L0_attn_W_C': _L0_attn_in['W_C'], 'L0_attn_A_log': _L0_attn_in['A_log'], 'L0_attn_D_param': _L0_attn_in['D_param'], 'L0_ffn_wqkv': _L0_ffn_in['wqkv'], 'L0_ffn_q_scale': _L0_ffn_in['q_scale'], 'L0_ffn_k_scale': _L0_ffn_in['k_scale'], 'L0_ffn_wo': _L0_ffn_in['wo'], 'L0_ffn_ln_g': _L0_ffn_in['ln_g'], 'L0_ffn_ln_b': _L0_ffn_in['ln_b'], 'L0_ffn_w1': _L0_ffn_in['w1'], 'L0_ffn_b1': _L0_ffn_in['b1'], 'L0_ffn_w2': _L0_ffn_in['w2'], 'L0_ffn_b2': _L0_ffn_in['b2'], 'L1_attn_W_in': _L1_attn_in['W_in'], 'L1_attn_conv_w': _L1_attn_in['conv_w'], 'L1_attn_conv_b': _L1_attn_in['conv_b'], 'L1_attn_dt_bias': _L1_attn_in['dt_bias'], 'L1_attn_A_log': _L1_attn_in['A_log'], 'L1_attn_D': _L1_attn_in['D'], 'L1_attn_norm_w': _L1_attn_in['norm_w'], 'L1_attn_W_out': _L1_attn_in['W_out'], 'L1_ffn_centroids': _L1_ffn_in['centroids'], 'L1_ffn_ln_g': _L1_ffn_in['ln_g'], 'L1_ffn_ln_b': _L1_ffn_in['ln_b'], 'L1_ffn_w1': _L1_ffn_in['w1'], 'L1_ffn_b1': _L1_ffn_in['b1'], 'L1_ffn_w2': _L1_ffn_in['w2'], 'L1_ffn_b2': _L1_ffn_in['b2']}
    _x0 = _d['L0_attn_x']
    _d['L0_attn_x'] = jax.random.normal(jax.random.fold_in(jax.random.key(seed), 1), (8, 512, 128), dtype=_x0.dtype)
    del _x0
    return _d

def reference(L0_attn_x, L0_attn_W_dt, L0_attn_b_dt, L0_attn_W_B, L0_attn_W_C, L0_attn_A_log, L0_attn_D_param, L0_ffn_wqkv, L0_ffn_q_scale, L0_ffn_k_scale, L0_ffn_wo, L0_ffn_ln_g, L0_ffn_ln_b, L0_ffn_w1, L0_ffn_b1, L0_ffn_w2, L0_ffn_b2, L1_attn_W_in, L1_attn_conv_w, L1_attn_conv_b, L1_attn_dt_bias, L1_attn_A_log, L1_attn_D, L1_attn_norm_w, L1_attn_W_out, L1_ffn_centroids, L1_ffn_ln_g, L1_ffn_ln_b, L1_ffn_w1, L1_ffn_b1, L1_ffn_w2, L1_ffn_b2):

    def _L0_attn_ref(x, W_dt, b_dt, W_B, W_C, A_log, D_param):
        import jax, jax.numpy as jnp
        import numpy as np
        B_, L_, D_, N_ = (16, 128, 128, 8)

        def soft_clamp(x, mn, mx, sharp):
            c = (mx + mn) / 2.0
            r = (mx - mn) / 2.0
            xn = (x - c) / (r + 1e-08)
            return jnp.tanh(xn * sharp) / sharp * r + c

        def _forward(x, W_dt, b_dt, W_B, W_C, A_log, D_param):
            Bb, L, D = x.shape
            N = W_B.shape[0]
            dt = soft_clamp(jax.nn.softplus(jnp.einsum('bld,ed->ble', x, W_dt) + b_dt), 0.001, 0.1, 0.5)
            Bp = jnp.einsum('bld,nd->bln', x, W_B)
            Cp = jnp.einsum('bld,nd->bln', x, W_C)
            A = -jnp.exp(soft_clamp(A_log, -5.0, 5.0, 0.5))

            def step(h, inp):
                t, x_t, dt_t, B_t, C_t = inp
                dA = jnp.exp(soft_clamp(dt_t[:, :, None] * A[None], -8.0, 8.0, 0.5))
                h = h * dA + (dt_t * x_t)[:, :, None] * B_t[:, None, :]
                hnorm = jnp.sqrt(jnp.sum(h.astype(jnp.float32) ** 2, axis=(1, 2), keepdims=True))
                scale = jnp.minimum(20.0 / (hnorm + 1e-08), 1.0).astype(h.dtype)
                h = jnp.where(t % 10 == 0, h * scale, h)
                y = jnp.einsum('bdn,bn->bd', h, C_t) + D_param * x_t
                return (h, y)
            h0 = jnp.zeros((Bb, D, N), dtype=x.dtype)
            ts = jnp.arange(L)
            xs = (ts, jnp.swapaxes(x, 0, 1), jnp.swapaxes(dt, 0, 1), jnp.swapaxes(Bp, 0, 1), jnp.swapaxes(Cp, 0, 1))
            _, ys = jax.lax.scan(step, h0, xs)
            return jnp.swapaxes(ys, 0, 1)
        return _forward(x, W_dt, b_dt, W_B, W_C, A_log, D_param)

    def _L0_ffn_ref(x, wqkv, q_scale, k_scale, wo, ln_g, ln_b, w1, b1, w2, b2):
        import jax, jax.numpy as jnp
        import numpy as np
        DIM = 128
        DEPTH = 2
        HEADS = 8
        DIM_HEAD = 64
        WINDOW = 64
        INNER = HEADS * DIM_HEAD
        HID = int(DIM * 4 * 2 / 3)
        B, N = (2, 1024)
        QK_SCALE = 8.0

        def shift_token(t):
            t1, t2 = jnp.split(t, 2, axis=-1)
            t2 = jnp.pad(t2, ((0, 0), (1, 0), (0, 0)))[:, :-1]
            return jnp.concatenate([t1, t2], axis=-1)

        def l2norm(t):
            return t / jnp.clip(jnp.linalg.norm(t, axis=-1, keepdims=True), 1e-12)

        def rotate_half(x):
            x1, x2 = jnp.split(x, 2, axis=-1)
            return jnp.concatenate([-x2, x1], axis=-1)

        def rotary_xpos(q, k):
            n = q.shape[-2]
            half_idx = jnp.arange(0, DIM_HEAD, 2, dtype=jnp.float32)
            inv_freq = 1.0 / 10000.0 ** (half_idx / DIM_HEAD)
            t = jnp.arange(n, dtype=jnp.float32)
            freqs = t[:, None] * inv_freq[None, :]
            freqs = jnp.concatenate([freqs, freqs], axis=-1)
            base = (half_idx + 0.4 * DIM_HEAD) / (1.4 * DIM_HEAD)
            power = (t - n // 2) / float(WINDOW // 2)
            scale = base[None, :] ** power[:, None]
            scale = jnp.concatenate([scale, scale], axis=-1)
            cos, sin = (jnp.cos(freqs), jnp.sin(freqs))
            q = q * cos * scale + rotate_half(q) * sin * scale
            k = k * cos / scale + rotate_half(k) * sin / scale
            return (q, k)

        def local_attention(q, k, v):
            b, h, n, d = q.shape
            w = n // WINDOW
            bq = q.reshape(b, h, w, WINDOW, d) * QK_SCALE
            bk = k.reshape(b, h, w, WINDOW, d)
            bv = v.reshape(b, h, w, WINDOW, d)

            def look_around(t):
                p = jnp.pad(t, ((0, 0), (0, 0), (1, 0), (0, 0), (0, 0)))
                return jnp.concatenate([p[:, :, :w], p[:, :, 1:]], axis=3)
            bk, bv = (look_around(bk), look_around(bv))
            bt = jnp.arange(n).reshape(w, WINDOW)
            btp = jnp.pad(bt, ((1, 0), (0, 0)), constant_values=-1)
            btk = jnp.concatenate([btp[:w], btp[1:]], axis=1)
            sim = jnp.einsum('bhwid,bhwjd->bhwij', bq, bk)
            i = bt[:, :, None]
            j = btk[:, None, :]
            mask = (i < j) | (i > j + WINDOW) | (j == -1)
            sim = jnp.where(mask, -jnp.finfo(sim.dtype).max, sim)
            attn = jax.nn.softmax(sim, axis=-1)
            out = jnp.einsum('bhwij,bhwjd->bhwid', attn, bv)
            return out.reshape(b, h, n, d)

        def _layer(x, wqkv, qs, ksc, wo, lg, lb, w1, b1, w2, b2):
            b, n, _ = x.shape
            h = shift_token(x)
            qkv = h @ wqkv
            q, k, v = jnp.split(qkv, 3, axis=-1)
            to_heads = lambda t: t.reshape(b, n, HEADS, DIM_HEAD).transpose(0, 2, 1, 3)
            q, k, v = (to_heads(q), to_heads(k), to_heads(v))
            q = l2norm(q) * qs
            k = l2norm(k) * ksc
            q, k = rotary_xpos(q, k)
            o = local_attention(q, k, v)
            o = o.transpose(0, 2, 1, 3).reshape(b, n, INNER)
            x = x + o @ wo
            h = shift_token(x)
            mu = h.mean(-1, keepdims=True)
            var = h.var(-1, keepdims=True)
            h = (h - mu) / jnp.sqrt(var + 1e-05) * lg + lb
            h = h @ w1 + b1
            a, g = jnp.split(h, 2, axis=-1)
            h = a * jax.nn.gelu(g, approximate=False)
            x = x + h @ w2 + b2
            return x
        for l in range(DEPTH):
            x = _layer(x, wqkv[l], q_scale[l], k_scale[l], wo[l], ln_g[l], ln_b[l], w1[l], b1[l], w2[l], b2[l])
        return x

    def _L1_attn_ref(X, W_in, conv_w, conv_b, dt_bias, A_log, D, norm_w, W_out):
        import jax, jax.numpy as jnp
        import numpy as np
        BATCH, SEQ, D_MODEL = (4, 256, 128)
        D_STATE, D_CONV, EXPAND, HEADDIM = (64, 4, 2, 64)
        D_INNER = EXPAND * D_MODEL
        NHEADS = D_INNER // HEADDIM
        CONV_DIM = D_INNER + 2 * D_STATE
        D_IN_PROJ = 2 * D_INNER + 2 * D_STATE + NHEADS
        EPS = 1e-05

        def mamba2(X, W_in, conv_w, conv_b, dt_bias, A_log, D, norm_w, W_out):
            b, l, _ = X.shape
            zxbcdt = X @ W_in.T
            z, xBC, dt = jnp.split(zxbcdt, [D_INNER, D_INNER + CONV_DIM], axis=-1)
            dt = jax.nn.softplus(dt + dt_bias)
            xBC_t = xBC.transpose(0, 2, 1)
            ker = conv_w[:, None, :]
            xBC_c = jax.lax.conv_general_dilated(xBC_t, ker, window_strides=(1,), padding=[(D_CONV - 1, 0)], feature_group_count=CONV_DIM)
            xBC = jax.nn.silu(xBC_c.transpose(0, 2, 1) + conv_b)
            x, Bm, Cm = jnp.split(xBC, [D_INNER, D_INNER + D_STATE], axis=-1)
            xh = x.reshape(b, l, NHEADS, HEADDIM)
            A = -jnp.exp(A_log)
            dA = jnp.exp(dt * A)
            dBx = jnp.einsum('blh,bln,blhp->blhpn', dt, Bm, xh)

            def step(h, inp):
                dA_t, dBx_t, C_t = inp
                h = h * dA_t[:, :, None, None] + dBx_t
                y = jnp.einsum('bhpn,bn->bhp', h, C_t)
                return (h, y)
            h0 = jnp.zeros((b, NHEADS, HEADDIM, D_STATE), X.dtype)
            _, ys = jax.lax.scan(step, h0, (dA.transpose(1, 0, 2), dBx.transpose(1, 0, 2, 3, 4), Cm.transpose(1, 0, 2)))
            y = ys.transpose(1, 0, 2, 3) + D[None, None, :, None] * xh
            y = y.reshape(b, l, D_INNER)
            y = y * jax.nn.silu(z)
            y = y * jax.lax.rsqrt(jnp.mean(y * y, axis=-1, keepdims=True) + EPS) * norm_w
            return y @ W_out.T
        return mamba2(X, W_in, conv_w, conv_b, dt_bias, A_log, D, norm_w, W_out) + X

    def _L1_ffn_ref(input_features, centroids, ln_g, ln_b, w1, b1, w2, b2):
        import jax, jax.numpy as jnp
        import numpy as np
        B, S, D, F, E = (8, 128, 128, 512, 8)
        EPS = 1e-05
        x = input_features.reshape(-1, D)
        aff = jax.lax.stop_gradient(x @ centroids.T)
        eid = jnp.argmax(aff, axis=-1)
        alpha = jax.nn.sigmoid(jnp.sum(x * centroids[eid], axis=-1, keepdims=True))
        mu = jnp.mean(x, axis=-1, keepdims=True)
        var = jnp.mean((x - mu) ** 2, axis=-1, keepdims=True)
        xn = (x - mu) * jax.lax.rsqrt(var + EPS)
        xln = xn * ln_g[eid] + ln_b[eid]
        onehot = jax.nn.one_hot(eid, E, dtype=x.dtype)
        ffn = jnp.zeros_like(x)
        for e in range(E):
            h = jax.nn.relu(xln @ w1[e] + b1[e])
            ffn = ffn + onehot[:, e:e + 1] * (h @ w2[e] + b2[e])
        out = x + alpha * ffn
        return out.reshape(input_features.shape)
    x = L0_attn_x
    x = x + _layernorm(_L0_attn_ref(_layernorm(x, axis=-1), L0_attn_W_dt, L0_attn_b_dt, L0_attn_W_B, L0_attn_W_C, L0_attn_A_log, L0_attn_D_param), axis=-1)
    x = x + _layernorm(_L0_ffn_ref(_layernorm(x, axis=-1), L0_ffn_wqkv, L0_ffn_q_scale, L0_ffn_k_scale, L0_ffn_wo, L0_ffn_ln_g, L0_ffn_ln_b, L0_ffn_w1, L0_ffn_b1, L0_ffn_w2, L0_ffn_b2), axis=-1)
    x = x + _layernorm(_L1_attn_ref(_layernorm(x, axis=-1), L1_attn_W_in, L1_attn_conv_w, L1_attn_conv_b, L1_attn_dt_bias, L1_attn_A_log, L1_attn_D, L1_attn_norm_w, L1_attn_W_out), axis=-1)
    x = x + _layernorm(_L1_ffn_ref(_layernorm(x, axis=-1), L1_ffn_centroids, L1_ffn_ln_g, L1_ffn_ln_b, L1_ffn_w1, L1_ffn_b1, L1_ffn_w2, L1_ffn_b2), axis=-1)
    return x

_drawn_inputs = setup_inputs


def setup_inputs(seed=0):
    import zlib

    import numpy as np

    out = dict(_drawn_inputs(seed))
    spreads = {'L0_attn_b_dt': (-2.0, 0.2),
     'L0_attn_D_param': (0.10000000149011612, 0.584),
     'L0_ffn_q_scale': (1.0, 0.6),
     'L0_ffn_k_scale': (1.0, 0.6),
     'L0_ffn_ln_g': (1.0, 0.6),
     'L0_ffn_ln_b': (0.0, 0.8),
     'L0_ffn_b1': (0.0, 0.8),
     'L0_ffn_b2': (0.0, 0.1),
     'L1_attn_conv_b': (0.0, 0.1),
     'L1_attn_D': (1.0, 0.6),
     'L1_attn_norm_w': (1.0, 0.6),
     'L1_ffn_ln_g': (1.0, 0.6),
     'L1_ffn_ln_b': (0.0, 0.8),
     'L1_ffn_b1': (0.0, 0.8),
     'L1_ffn_b2': (0.0, 0.425)}
    factors = {'L0_ffn_wqkv': 4.501,
     'L0_ffn_wo': 4.504,
     'L0_ffn_w1': 7.567,
     'L0_ffn_w2': 7.405,
     'L1_attn_conv_w': 6.822,
     'L1_attn_dt_bias': 8.0,
     'L1_attn_A_log': 8.0,
     'L1_ffn_w1': 4.869,
     'L1_ffn_w2': 3.839}
    for name, (base, spread) in spreads.items():
        noise = np.random.default_rng([zlib.crc32(name.encode()), seed]).standard_normal(out[name].shape)
        drawn = base * np.exp(spread * noise) if base else spread * noise
        out[name] = jnp.asarray(drawn.astype(out[name].dtype))
    for name, factor in factors.items():
        out[name] = (out[name] * factor).astype(out[name].dtype)
    return out
```

```python
import concourse.bass as bass
from concourse import mybir
from collections import namedtuple
from contextlib import ExitStack

F32 = mybir.dt.float32
BF16 = mybir.dt.bfloat16
ALU = mybir.AluOpType
ACT = mybir.ActivationFunctionType
AX = mybir.AxisListType

P = 128
BATCH, SEQ, D = 8, 512, 128
TILES = SEQ // P
EPS = 1e-5
STAGES = 4
FIRST = 0


def semaphores(nc, ctx, prefix, names):
    sems = [nc.alloc_semaphore(name=f"{prefix}_{n}") for n in names.split()]

    def clear():
        nc.clear_and_free_semaphores(sems)
        nc.all_engine_barrier()

    ctx.callback(clear)
    return namedtuple("Semaphores", names)(*sems)


def lead(eng, sem, n):
    for _ in range(n):
        eng.nop().then_inc(sem, 1)


def step(eng, ins, sem, count):
    ins.then_inc(sem, 1)
    eng.wait_ge(sem, count)


class Order:

    def __init__(self, eng, sem, per=0, base=0):
        self.eng, self.sem, self.per, self.base, self.turn, self.n = eng, sem, per, base, 0, 0

    def start(self, turn):
        self.turn, self.n = turn, 0

    def __call__(self, ins):
        self.n += 1
        step(self.eng, ins, self.sem, self.turn * self.per + (self.base + self.n))

    def end(self):
        assert self.n == self.per, (self.n, self.per)


def spread(ap, axis, n):
    ap = ap.unsqueeze(axis)
    return ap.to_broadcast([n if k == axis else m for k, m in enumerate(ap.shape)])


NT = BATCH * TILES


def stage_sequences(sp, src, buf, used, staged):
    with sp.Fori(0, BATCH // 2) as i:
        for q in range(2):
            sp.wait_ge(used, 2 * i + (q + 1))
            sp.dma_start(buf[:, q, :, :], src[:, bass.ds((2 * i + q) * TILES, TILES), :]).then_inc(staged[q], 16)


def transpose_sequences(pe, buf, ps, con, staged, copied, done):
    lead(pe, done, 2)
    with pe.Fori(0, BATCH // 2) as i:
        for q in range(2):
            pe.wait_ge(copied, 2 * i + (q + 1))
            pe.wait_ge(staged[q], i * 16 + 16)
            for j in range(TILES):
                last = pe.transpose(ps[:, q, j * P:(j + 1) * P], buf[:, q, j, :], con["ident"])
            last.then_inc(done, 1)


MOMENTS = 6


def moments(dve, own, stats, mean, diff, var):
    own(dve.tensor_tensor(mean[:, :], stats[:, :, 1], stats[:, :, 4], ALU.add))
    own(dve.tensor_scalar(mean[:, :], mean[:, :], 0.5, None, ALU.mult))
    own(dve.tensor_tensor(diff[:, :], stats[:, :, 1], stats[:, :, 4], ALU.subtract))
    own(dve.scalar_tensor_tensor(out=diff[:, :], in0=diff[:, :], scalar=0.25, in1=diff[:, :], op0=ALU.mult, op1=ALU.mult))
    own(dve.tensor_tensor(var[:, :], stats[:, :, 2], stats[:, :, 5], ALU.add))
    own(dve.scalar_tensor_tensor(out=var[:, :], in0=var[:, :], scalar=1.0 / D, in1=diff[:, :], op0=ALU.mult, op1=ALU.add))


def normalize(nc, tag, con, src, dst, add_to=None):
    with ExitStack() as ctx:
        sb = lambda n, s: ctx.enter_context(nc.sbuf_tensor(f"{tag}_{n}", s, F32))
        S = semaphores(nc, ctx, tag, "stats own veps rstd")
        stats = sb("stats", [P, NT, 6])
        mean, diff, var, rstd = (sb(n, [P, NT]) for n in ("mean", "diff", "var", "rstd"))
        block = ctx.enter_context(nc.Block())

        @block.vector
        def _(dve):
            with dve.Fori(0, NT // 4) as i:
                for j in range(4):
                    t = 4 * i + j
                    dve.bn_stats(stats[:, bass.ds(t, 1), :].squeeze(1), src[:, bass.ds(t, 1), :].squeeze(1)).then_inc(S.stats, 1)
            dve.wait_ge(S.stats, NT)
            own = Order(dve, S.own)
            moments(dve, own, stats, mean, diff, var)
            dve.tensor_scalar(var[:, :], var[:, :], EPS, None, ALU.add).then_inc(S.veps, 1)
            dve.wait_ge(S.rstd, 1)
            n0 = own.n
            with dve.Fori(0, NT // 4) as i:
                for j in range(4):
                    t = 4 * i + j
                    dve.tensor_scalar(dst[:, bass.ds(t, 1), :].squeeze(1), src[:, bass.ds(t, 1), :].squeeze(1),
                                      mean[:, bass.ds(t, 1)], rstd[:, bass.ds(t, 1)], ALU.subtract, ALU.mult).then_inc(S.own, 1)
            if add_to is not None:
                dve.wait_ge(S.own, n0 + NT)
                dve.tensor_tensor(add_to[:, :, :], add_to[:, :, :], dst[:, :, :], ALU.add).then_inc(S.own, 1)

        @block.gpsimd
        def _(pool):
            pool.wait_ge(S.veps, 1)
            pool.tensor_tensor(rstd[:, :], var[:, :], con["mhalf"][:, 0:NT], ALU.pow).then_inc(S.rstd, 1)


N_STATE = 8
STEPS = 10
CHUNKS = -(-SEQ // STEPS)
CW = BATCH * STEPS
HALF = N_STATE // 2 * CW
COLS0 = CHUNKS * CW


def stage0_project(nc, xn_tok, w, con, xnT, dt, dtx):
    with ExitStack() as ctx:
        sb = lambda n, s: ctx.enter_context(nc.sbuf_tensor(n, s, F32))
        S = semaphores(nc, ctx, "p0", "staged0 staged1 xt xT xT_part proj u absu ex ln sp th pad dt dtx")
        xn = sb("p0_xn", [P, 2, TILES, D])
        u, a = sb("p0_u", [P, COLS0]), sb("p0_a", [P, COLS0])
        ps_t = ctx.enter_context(nc.psum_tensor("p0_ps_t", [P, 2, SEQ], F32))
        ps_p = ctx.enter_context(nc.psum_tensor("p0_ps_p", [P, 2, SEQ], F32))
        GROUPS, GW = 10, COLS0 // 10
        c, r = (0.1 + 0.001) / 2, (0.1 - 0.001) / 2
        block = ctx.enter_context(nc.Block())

        @block.sync
        def _(sp):
            stage_sequences(sp, xn_tok, xn, S.xt, (S.staged0, S.staged1))

        @block.vector
        def _(dve):
            dve.memset(xnT[:, (CHUNKS - 1) * CW:], 0.0).then_inc(S.pad, 1)
            dve.wait_ge(S.u, 2 + GROUPS)
            dve.scalar_tensor_tensor(out=a[:, :], in0=u[:, :], scalar=-1.0, in1=u[:, :], op0=ALU.mult,
                                     op1=ALU.max).then_inc(S.absu, 1)
            dve.wait_ge(S.ln, 1)
            dve.scalar_tensor_tensor(out=u[:, :], in0=u[:, :], scalar=0.0, in1=a[:, :], op0=ALU.max,
                                     op1=ALU.add).then_inc(S.sp, 1)
            dve.wait_ge(S.th, 1)
            step(dve, dve.tensor_scalar(dt[:, :], u[:, :], r / 0.5, c, ALU.mult, ALU.add), S.dt, 1)
            dve.wait_ge(S.xT, 2 + BATCH)
            step(dve, dve.tensor_tensor(dtx[:, :], dt[:, :], xnT[:, :], ALU.mult), S.dtx, 1)

        @block.tensor
        def _(pe):
            transpose_sequences(pe, xn, ps_t, con, (S.staged0, S.staged1), S.xT, S.xt)
            pe.wait_ge(S.xT, 2 + BATCH)
            pe.wait_ge(S.pad, 1)
            with pe.Fori(0, GROUPS // 2) as i:
                for q in range(2):
                    pe.wait_ge(S.u, 2 * i + (q + 1))
                    pe.matmul(ps_p[:, q, 0:GW], w["W_dtT"], xnT[:, bass.ds((2 * i + q) * GW, GW)],
                              start=True, stop=True).then_inc(S.proj, 1)

        @block.scalar
        def _(act):
            lead(act, S.xT, 2)
            lead(act, S.u, 2)
            full = (CHUNKS - 1) * STEPS
            cols = xnT[:, :].rearrange("p (k b t) -> p k b t", b=BATCH, t=STEPS)
            act.wait_ge(S.pad, 1)
            with act.Fori(0, BATCH // 2) as i:
                for q in range(2):
                    act.wait_ge(S.xt, 2 * i + (q + 3))
                    b = 2 * i + q
                    act.copy(cols[:, 0:CHUNKS - 1, bass.ds(b, 1), :],
                             ps_t[:, q, 0:full].rearrange("p (k t) -> p k t", t=STEPS).unsqueeze(2)).then_inc(S.xT_part, 1)
                    act.wait_ge(S.xT_part, 2 * i + (q + 1))
                    act.copy(cols[:, CHUNKS - 1, bass.ds(b, 1), 0:SEQ - full],
                             ps_t[:, q, full:SEQ].unsqueeze(1)).then_inc(S.xT, 1)
            with act.Fori(0, GROUPS // 2) as i:
                for q in range(2):
                    act.wait_ge(S.proj, 2 * i + (q + 1))
                    act.activation(u[:, bass.ds((2 * i + q) * GW, GW)], ps_p[:, q, 0:GW], ACT.Identity,
                                   bias=w["b_dt"]).then_inc(S.u, 1)
            act.wait_ge(S.absu, 1)
            step(act, act.activation(a[:, :], a[:, :], ACT.Exp, scale=-1.0), S.ex, 1)
            step(act, act.activation(a[:, :], a[:, :], ACT.Ln, bias=1.0), S.ln, 1)
            act.wait_ge(S.sp, 1)
            act.activation(u[:, :], u[:, :], ACT.Tanh, scale=0.5 / (r + 1e-8), bias=con["clamp_dt"]).then_inc(S.th, 1)


def chunk_turns(eng, turn):
    turn(0, 0)
    with eng.Fori(0, (CHUNKS - 2) // 2) as i:
        turn(2 * i + 1, 1)
        turn(2 * i + 2, 0)
    turn(CHUNKS - 1, 1)


def is_at(k, chunk):
    return isinstance(k, int) and k == chunk


def stage0_scan(nc, w, con, xnT, dt, dtx, y):
    with ExitStack() as ctx:
        sb = lambda n, s: ctx.enter_context(nc.sbuf_tensor(n, s, F32))
        pb = lambda n, s: ctx.enter_context(nc.psum_tensor(n, s, F32))
        S = semaphores(nc, ctx, "s0", "arg tanh dA B C dBx sq ones ss root h hC Y out own zero")
        W, ROWS = N_STATE * CW, N_STATE * BATCH
        arg = sb("s0_arg", [P, 2, W])
        dA = sb("s0_dA", [P, 2, W])
        dBx = sb("s0_dBx", [P, 2, W])
        h = sb("s0_h", [P, 2, W])
        hC = sb("s0_hC", [P, 2, W])
        first = sb("s0_first", [P, ROWS])
        sq = sb("s0_sq", [P, ROWS])
        ss, root, scale = sb("s0_ss", [P, BATCH]), sb("s0_root", [P, BATCH]), sb("s0_scale", [P, BATCH])
        psB, psC = pb("s0_psB", [P, 2, 512]), pb("s0_psC", [P, 2, 512])
        psS = pb("s0_psS", [P, 512])
        psY = pb("s0_psY", [P, 2, 512])
        block = ctx.enter_context(nc.Block())
        step_of = lambda t, s: t.rearrange("p (r t) -> p r t", t=STEPS)[:, :, s]
        halves = lambda t: t.rearrange("p (a n c) -> p a n c", a=2, n=N_STATE // 2)
        banks = lambda t: t[:, :, 0:HALF].rearrange("p a (n c) -> p a n c", n=N_STATE // 2)

        @block.gpsimd
        def _(pool):
            def decay_argument(k, q):
                pool.wait_ge(S.dA, k + 1)
                pool.tensor_tensor(arg[:, q, :].rearrange("p (n c) -> p n c", n=N_STATE),
                                   spread(dt[:, bass.ds(k * CW, CW)], 1, N_STATE),
                                   spread(w["A16"], 2, CW), ALU.mult).then_inc(S.arg, 1)

            def turn(k, q):
                pool.wait_ge(S.ss, k + 1)
                pool.tensor_tensor(root[:, :], ss[:, :], con["half"][:, 0:BATCH], ALU.pow).then_inc(S.root, 1)
                if not is_at(k, CHUNKS - 1):
                    decay_argument(k + 1, 1 - q)

            decay_argument(0, 0)
            chunk_turns(pool, turn)

        @block.scalar
        def _(act):
            lead(act, S.dA, 2)
            lead(act, S.out, 2)

            def decay(k, q):
                act.wait_ge(S.arg, k + 1)
                step(act, act.activation(arg[:, q, :], arg[:, q, :], ACT.Tanh), S.tanh, k + 1)
                act.wait_ge(S.h, k + 1)
                act.activation(dA[:, q, :], arg[:, q, :], ACT.Exp, scale=16.0).then_inc(S.dA, 1)

            def copy_out(k, q):
                act.wait_ge(S.Y, k + 3)
                act.copy(y[:, :, bass.ds(k * STEPS, STEPS)],
                         psY[:, q, 0:CW].rearrange("p (b t) -> p b t", b=BATCH)).then_inc(S.out, 1)

            def turn(k, q):
                if not is_at(k, CHUNKS - 1):
                    decay(k + 1, 1 - q)
                if not is_at(k, 0):
                    copy_out(k - 1, 1 - q)

            decay(0, 0)
            chunk_turns(act, turn)
            copy_out(CHUNKS - 1, 1)

        @block.tensor
        def _(pe):
            def rows_of(ps, weights, k, used, count, ready):
                pe.wait_ge(used, count)
                for n in range(N_STATE):
                    o = n % 4 * CW
                    last = pe.matmul(ps[:, n // 4, o:o + CW], weights[:, n, :], xnT[:, bass.ds(k * CW, CW)],
                                     start=True, stop=True)
                last.then_inc(ready, 1)

            def sum_states(k, q):
                pe.wait_ge(S.hC, k + 2)
                pe.wait_ge(S.out, k + 1)
                pe.matmul(psY[:, q, 0:CW], w["diagD"], xnT[:, bass.ds(k * CW, CW)], start=True, stop=False)
                for n in range(N_STATE):
                    last = pe.matmul(psY[:, q, 0:CW], con["ident"], hC[:, q, n * CW:(n + 1) * CW],
                                     start=False, stop=n == N_STATE - 1)
                last.then_inc(S.Y, 1)

            def turn(k, q):
                pe.wait_ge(S.sq, k + 1)
                pe.matmul(psS[:, 0:ROWS], con["ones"], sq[:, :], start=True, stop=True).then_inc(S.ones, 1)
                if not is_at(k, CHUNKS - 1):
                    rows_of(psB, w["WB_rep"], k + 1, S.dBx, k + 2, S.B)
                if not is_at(k, 0):
                    sum_states(k - 1, 1 - q)
                rows_of(psC, w["WC_rep"], k, S.hC, k + 1, S.C)

            lead(pe, S.Y, 2)
            rows_of(psB, w["WB_rep"], 0, S.dBx, 1, S.B)
            chunk_turns(pe, turn)
            sum_states(CHUNKS - 1, 1)

        @block.vector
        def _(dve):
            OWN = 7
            own = Order(dve, S.own, OWN)

            def inputs(k, q):
                dve.wait_ge(S.B, k + 1)
                dve.tensor_tensor(halves(dBx[:, q, :]), banks(psB),
                                  spread(dtx[:, bass.ds(k * CW, CW)], 1, N_STATE).rearrange("p (a n) c -> p a n c", a=2),
                                  ALU.mult).then_inc(S.dBx, 1)

            def outputs(k, q):
                dve.wait_ge(S.C, k + 1)
                dve.wait_ge(S.Y, k + 1)
                dve.tensor_tensor(halves(hC[:, q, :]), banks(psC), halves(h[:, q, :]), ALU.mult).then_inc(S.hC, 1)

            lead(dve, S.h, 2)
            lead(dve, S.dBx, 1)
            lead(dve, S.hC, 1)
            step(dve, dve.memset(h[:, :, :], 0.0), S.zero, 1)
            inputs(0, 0)

            def turn(k, q):
                own.start(k)
                dve.wait_ge(S.dBx, k + 2)
                dve.wait_ge(S.dA, k + 3)
                own(dve.tensor_tensor(first[:, :], step_of(dA[:, q, :], 0), step_of(h[:, 1 - q, :], STEPS - 1), ALU.mult))
                own(dve.tensor_tensor(first[:, :], first[:, :], step_of(dBx[:, q, :], 0), ALU.add))
                step(dve, dve.tensor_tensor(sq[:, :], first[:, :], first[:, :], ALU.mult), S.sq, k + 1)
                own(dve.memset(step_of(dA[:, q, :], 0), 0.0))
                dve.wait_ge(S.ones, k + 1)
                step(dve, dve.tensor_reduce(ss[:, :], psS[:, 0:ROWS].rearrange("p (n b) -> p b n", b=BATCH), AX.X,
                                            ALU.add), S.ss, k + 1)
                if not is_at(k, 0):
                    outputs(k - 1, 1 - q)
                if not is_at(k, CHUNKS - 1):
                    inputs(k + 1, 1 - q)
                dve.wait_ge(S.root, k + 1)
                own(dve.tensor_scalar(scale[:, :], root[:, :], 1e-8, None, ALU.add))
                own(dve.reciprocal(scale[:, :], scale[:, :]))
                own(dve.tensor_scalar(scale[:, :], scale[:, :], 20.0, 1.0, ALU.mult, ALU.min))
                own(dve.tensor_tensor(step_of(dBx[:, q, :], 0).rearrange("p (n b) -> p n b", b=BATCH),
                                      first[:, :].rearrange("p (n b) -> p n b", b=BATCH),
                                      spread(scale[:, :], 1, N_STATE), ALU.mult))
                step(dve, dve.tensor_tensor_scan(h[:, q, :], dA[:, q, :], dBx[:, q, :], 0.0, ALU.mult, ALU.add),
                     S.h, k + 3)
                own.end()

            chunk_turns(dve, turn)
            outputs(CHUNKS - 1, 1)


def stage0_output(nc, y, con, y_tok):
    with ExitStack() as ctx:
        S = semaphores(nc, ctx, "o0", "staged0 staged1 yt y_tok")
        buf = ctx.enter_context(nc.sbuf_tensor("o0_buf", [P, 2, TILES, P], F32))
        ps = ctx.enter_context(nc.psum_tensor("o0_ps", [P, 2, SEQ], F32))
        block = ctx.enter_context(nc.Block())

        @block.sync
        def _(sp):
            with sp.Fori(0, BATCH // 2) as i:
                for q in range(2):
                    sp.wait_ge(S.yt, 2 * i + (q + 1))
                    sp.dma_start(buf[:, q, :, :].rearrange("p j t -> p (j t)"),
                                 y[:, bass.ds(2 * i + q, 1), 0:SEQ].squeeze(1)).then_inc((S.staged0, S.staged1)[q], 16)

        @block.tensor
        def _(pe):
            transpose_sequences(pe, buf, ps, con, (S.staged0, S.staged1), S.y_tok, S.yt)

        @block.scalar
        def _(act):
            lead(act, S.y_tok, 2)
            with act.Fori(0, BATCH // 2) as i:
                for q in range(2):
                    act.wait_ge(S.yt, 2 * i + (q + 3))
                    act.copy(y_tok[:, bass.ds((2 * i + q) * TILES, TILES), :],
                             ps[:, q, :].rearrange("p (j d) -> p j d", j=TILES)).then_inc(S.y_tok, 1)


def stage0(nc, mem, xn_tok, y_tok, con, weights):
    with ExitStack() as ctx:
        sb = lambda n, s: ctx.enter_context(nc.sbuf_tensor(n, s, F32))
        W0 = 2 * D + 2 * N_STATE + N_STATE + 2
        raw = sb("w0_raw", [P, W0])
        wdt, wb, wc = raw[:, 0:D], raw[:, D:D + N_STATE], raw[:, D + N_STATE:D + 2 * N_STATE]
        alog, bdt, dpar = (raw[:, D + 2 * N_STATE:D + 3 * N_STATE], raw[:, D + 3 * N_STATE:D + 3 * N_STATE + 1],
                           raw[:, D + 3 * N_STATE + 1:D + 3 * N_STATE + 2])
        WBr, WCr = sb("w0_WB", [P, N_STATE, P]), sb("w0_WC", [P, N_STATE, P])
        A16, diagD = sb("w0_A16", [P, N_STATE]), sb("w0_diagD", [P, P])
        S = semaphores(nc, ctx, "w0", "load th ex own")
        with nc.Block() as block:
            @block.sync
            def _(sp):
                sp.dma_start(raw[:, 0:D + 3 * N_STATE + 2], weights).then_inc(S.load, 16)

            @block.scalar
            def _(act):
                act.wait_ge(S.load, 16)
                step(act, act.activation(A16[:, :], alog, ACT.Tanh, scale=0.5 / (5.0 + 1e-8)), S.th, 1)
                act.activation(A16[:, :], A16[:, :], ACT.Exp, scale=10.0).then_inc(S.ex, 1)

            @block.vector
            def _(dve):
                dve.wait_ge(S.load, 16)
                dve.tensor_copy(WBr[:, :, :], spread(wb, 2, P)).then_inc(S.own, 1)
                dve.tensor_copy(WCr[:, :, :], spread(wc, 2, P)).then_inc(S.own, 1)
                dve.tensor_scalar(diagD[:, :], con["ident"], dpar, None, ALU.mult).then_inc(S.own, 1)
                dve.wait_ge(S.ex, 1)
                dve.tensor_scalar(A16[:, :], A16[:, :], -0.5 / (8.0 + 1e-8), None, ALU.mult).then_inc(S.own, 1)

        w = dict(W_dtT=wdt, b_dt=bdt, WB_rep=WBr, WC_rep=WCr, A16=A16[:, :], diagD=diagD[:, :])
        xnT, dt, dtx = (sb(f"s0_{n}", [P, COLS0]) for n in ("xnT", "dt", "dtx"))
        y = sb("s0_y", [P, BATCH, CHUNKS * STEPS])
        stage0_project(nc, xn_tok, w, con, xnT, dt, dtx)
        stage0_scan(nc, w, con, xnT, dt, dtx, y)
        stage0_output(nc, y, con, y_tok)



LAYERS, HEADS, DH, WINDOW = 2, 8, 64, 64
PAIRS = HEADS // 2
HIDDEN = int(D * 4 * 2 / 3)
KH = -(-HIDDEN // P)
W1C = 2 * KH * P
UPC = W1C + 2 * KH + 2
MASKED = -1e30


def stage1(nc, xn_tok, y_tok, con, dram):
    with ExitStack() as ctx:
        sb = lambda n, s, t=F32: ctx.enter_context(nc.sbuf_tensor(f"s1_{n}", s, t))
        S = semaphores(nc, ctx, "s1", "load own prep z_in z_out up_in zT hT qkv sq ss rn v rotC rot qkn qkt qkT sim0 sim1 max0 max1 "
                  "exp0 exp1 rin0 rin1 pn0 pn1 pt0 pt1 PT0 PT1 av oT wo z_att ft fT fb fst fvar frs fn fnt fnT up gelu hid "
                  "down z_ffn hT_half fT_half")
        wqkv = sb("wqkv", [P, LAYERS, 3 * HEADS * DH])
        wo = sb("wo", [P, LAYERS, PAIRS, D])
        w2 = sb("w2", [P, LAYERS, KH, D])
        b2 = sb("b2", [1, LAYERS, D])
        up = sb("up", [P, UPC])
        rot_base = sb("rot_base", [P, 2, TILES, 2, DH])
        qk_gain = sb("qk_gain", [P, LAYERS, 2, 2, DH])
        rot_tab = sb("rot_tab", [P, LAYERS, 2, TILES, 2, DH])
        mask_f = sb("mask_f", [P, TILES * P])
        mask = sb("mask", [P, TILES * P], BF16)
        ident16 = sb("ident16", [P, P], BF16)
        z = sb("z", [P, TILES, D])
        hT = sb("hT", [P, WINDOW + 1 + SEQ])
        fT = sb("fT", [P, 1 + SEQ])
        sq = sb("sq", [P, TILES, 4 * DH])
        ss, rn = sb("ss", [P, 4 * TILES]), sb("rn", [P, 4 * TILES])
        qk = sb("qk", [P, 2, TILES, 4 * DH])
        rs = sb("rs", [P, TILES, 4 * DH])
        v = sb("v", [P, 2, TILES, 2, P])
        qkT = sb("qkT", [P, 2, SEQ])
        nmax, rsum, rinv = (sb(n, [P, 2, TILES]) for n in ("nmax", "rsum", "rinv"))
        prob = sb("prob", [P, 2, TILES, P])
        probT = sb("probT", [P, 2, SEQ])
        oT = sb("oT", [P, PAIRS, SEQ])
        fstats = sb("fstats", [P, TILES, 6])
        fmean, fdiff, frstd = (sb(n, [P, TILES]) for n in ("fmean", "fdiff", "frstd"))
        fn, fnT = sb("fn", [P, TILES, D]), sb("fnT", [P, SEQ])
        gl, hid = sb("gl", [P, KH, SEQ]), sb("hid", [P, KH, SEQ])

        with nc.Block() as block:
            @block.sync
            def _(sp):
                for dst, name in ((wqkv, "wqkv"), (wo, "wo"), (w2, "w2"), (b2, "b2"), (rot_base, "rot_base"),
                                  (qk_gain, "qk_gain"), (mask_f, "mask")):
                    sp.dma_start(dst[tuple([slice(None)] * len(dst.shape))], dram[name]).then_inc(S.load, 16)

            @block.vector
            def _(dve):
                dve.memset(hT[:, 0:WINDOW + 1], 0.0).then_inc(S.prep, 1)
                dve.memset(fT[:, 0:1], 0.0).then_inc(S.prep, 1)
                dve.wait_ge(S.load, 7 * 16)
                for l in range(LAYERS):
                    for cs in range(2):
                        dve.tensor_tensor(rot_tab[:, l, cs, :, :, :].rearrange("p j c d -> p j (c d)"),
                                          rot_base[:, cs, :, :, :].rearrange("p j c d -> p j (c d)"),
                                          spread(qk_gain[:, l, cs, :, :].rearrange("p c d -> p (c d)"), 1, TILES),
                                          ALU.mult).then_inc(S.prep, 1)
                dve.tensor_copy(mask[:, :], mask_f[:, :]).then_inc(S.prep, 1)
                dve.tensor_copy(ident16[:, :], con["ident"]).then_inc(S.prep, 1)

        psQ = ctx.enter_context(nc.psum_tensor("s1_psQ", [P, TILES, 512], F32))
        psT = ctx.enter_context(nc.psum_tensor("s1_psT", [P, 2, 512], F32))
        psS = ctx.enter_context(nc.psum_tensor("s1_psS", [P, 2, 512], F32))
        psO, psW = psS[:, 0, :], psS[:, 1, :]
        block = ctx.enter_context(nc.Block())
        sim, mx, ex, rin, pn, pt, PT = ((S.sim0, S.sim1), (S.max0, S.max1), (S.exp0, S.exp1), (S.rin0, S.rin1),
                                        (S.pn0, S.pn1), (S.pt0, S.pt1), (S.PT0, S.PT1))

        def passes(eng, turn, after=None):
            with eng.Fori(0, BATCH) as b:
                with eng.Fori(0, LAYERS) as l:
                    turn(b, l, 2 * b + l)
                if after is not None:
                    after(b)

        @block.sync
        def _(sp):
            sp.nop().then_inc(S.z_out, 16)
            with sp.Fori(0, BATCH) as b:
                tile = sp.snap(b * TILES, min_val=0, max_val=NT - TILES)
                sp.wait_ge(S.z_out, b * 16 + 16)
                sp.dma_start(z[:, :, :], xn_tok[:, bass.ds(tile, TILES), :]).then_inc(S.z_in, 16)
                with sp.Fori(0, LAYERS) as l:
                    n = 2 * b + l
                    sp.wait_ge(S.z_ffn, n + 1)
                    sp.dma_start(up[:, :], dram["up"][:, bass.ds(l, 1), :].squeeze(1)).then_inc(S.up_in, 16)
            sp.wait_ge(S.z_out, BATCH * 16 + 16)

        @block.tensor
        def _(pe):
            def transposes(bank, src):
                for j in range(TILES):
                    last = pe.transpose(bank[:, j * P:(j + 1) * P], src(j), con["ident"])
                return last

            def project(n, l, hp):
                k = n * PAIRS + hp
                if hp == 0:
                    pe.wait_ge(S.hT, n + 1)
                else:
                    pe.wait_ge(S.rot, k)
                for j in range(TILES):
                    w = wqkv[:, bass.ds(l, 1), :].squeeze(1).rearrange("p (c f) -> p c f", c=3)[:, :, hp * P:(hp + 1) * P]
                    o = WINDOW + j * P
                    pe.matmul(psQ[:, j, 0:3 * P], hT[:, o:o + P], w, start=True, stop=True)
                    last = pe.matmul(psQ[:, j, 3 * P:4 * P], hT[:, o - WINDOW:o - WINDOW + P], w[:, 2, :],
                                     start=True, stop=True, skip_group_check=True)
                last.then_inc(S.qkv, 1)

            def scores(n, hp, h):
                k = n * PAIRS + hp
                if h == 0:
                    pe.wait_ge(S.oT, k + 1)
                pe.matmul(psS[:, h, :], ident16[:, :], mask[:, :], start=True, stop=False, skip_group_check=True)
                r = slice(h * DH, (h + 1) * DH)
                for j in range(TILES):
                    o = j * P
                    lo = 0 if j else WINDOW
                    pe.matmul(psS[0:64, h, o + lo:o + P], qkT[r, 0, o:o + WINDOW],
                              qkT[r, 1, o - WINDOW + lo:o + WINDOW], start=False, stop=True, skip_group_check=True)
                    last = pe.matmul(psS[64:128, h, o:o + P], qkT[r, 0, o + WINDOW:o + P],
                                     qkT[r, 1, o:o + P], start=False, stop=True, skip_group_check=True)
                last.then_inc(sim[h], 1)

            def turn(b, l, n):
                pe.wait_ge(S.z_in, b * 16 + 16)
                pe.wait_ge(S.z_ffn, n + 1)
                transposes(psT[:, 0, :], lambda j: z[:, j, :]).then_inc(S.zT, 1)
                project(n, l, 0)
                for hp in range(PAIRS):
                    k = n * PAIRS + hp
                    if hp + 1 < PAIRS:
                        project(n, l, hp + 1)
                    pe.wait_ge(S.qkn, k + 2)
                    pe.wait_ge(S.PT0, k + 1)
                    pe.wait_ge(S.PT1, k + 1)
                    for c in range(2):
                        last = transposes(psT[:, c, :], lambda j: qk[:, hp % 2, j, c * P:(c + 1) * P])
                    last.then_inc(S.qkt, 1)
                    pe.wait_ge(S.qkT, k + 1)
                    for h in range(2):
                        scores(n, hp, h)
                    for h in range(2):
                        pe.wait_ge(pn[h], k + 1)
                        transposes(psT[:, h, :], lambda j: prob[:, h, j, :]).then_inc(pt[h], 1)
                    for h in range(2):
                        pe.wait_ge(PT[h], k + 2)
                        if h == 0:
                            pe.wait_ge(S.v, k + 1)
                        r = slice(h * DH, (h + 1) * DH)
                        for j in range(TILES):
                            for odd in range(2):
                                o = j * P + odd * WINDOW
                                last = pe.matmul(psO[r, o:o + WINDOW], v[:, hp % 2, j, 1 - odd, r],
                                                 probT[:, h, o:o + WINDOW], start=True, stop=True, skip_group_check=True)
                    last.then_inc(S.av, 1)
                pe.wait_ge(S.oT, (n + 1) * PAIRS + 1)
                for j in range(TILES):
                    for hp in range(PAIRS):
                        last = pe.matmul(psW[:, j * P:(j + 1) * P], oT[:, hp, j * P:(j + 1) * P],
                                         wo[:, bass.ds(l, 1), hp, :].squeeze(1), start=hp == 0, stop=hp == PAIRS - 1)
                last.then_inc(S.wo, 1)
                pe.wait_ge(S.z_att, n + 1)
                transposes(psQ[:, 0, :], lambda j: z[:, j, :]).then_inc(S.ft, 1)
                pe.wait_ge(S.fT, n + 1)
                transposes(psQ[:, 1, :], lambda j: fT[:, j * P:(j + 1) * P]).then_inc(S.fb, 1)
                pe.wait_ge(S.fn, n + 1)
                transposes(psQ[:, 2, :], lambda j: fn[:, j, :]).then_inc(S.fnt, 1)
                pe.wait_ge(S.fnT, n + 1)
                pe.wait_ge(S.up_in, n * 16 + 16)
                for c in range(KH):
                    if c >= 2:
                        pe.wait_ge(S.hid, n * KH + (c - 1))
                    for g in range(2):
                        o = (g * KH + c) * P
                        last = pe.matmul(psQ[:, c % 2 * 2 + g, :], up[:, o:o + P], fnT[:, :], start=True, stop=True)
                    last.then_inc(S.up, 1)
                pe.wait_ge(S.hid, (n + 1) * KH)
                for j in range(TILES):
                    for c in range(KH):
                        pe.matmul(psT[:, 0, j * P:(j + 1) * P], hid[:, c, j * P:(j + 1) * P],
                                  w2[:, bass.ds(l, 1), c, :].squeeze(1), start=c == 0, stop=False)
                    last = pe.matmul(psT[:, 0, j * P:(j + 1) * P], con["ones"][0:1, :], b2[:, bass.ds(l, 1), :].squeeze(1),
                                     start=False, stop=True)
                last.then_inc(S.down, 1)

            lead(pe, S.qkt, 2)
            passes(pe, turn)

        @block.scalar
        def _(act):
            def square(n, hp):
                k = n * PAIRS + hp
                act.wait_ge(S.qkv, k + 1)
                act.wait_ge(S.ss, k + 1)
                act.activation(sq[:, :, :], psQ[:, :, 0:4 * DH], ACT.Square).then_inc(S.sq, 1)

            def turn(b, l, n):
                act.wait_ge(S.zT, n + 1)
                act.copy(hT[0:64, WINDOW:WINDOW + SEQ], psT[0:64, 0, :]).then_inc(S.hT_half, 1)
                act.copy(hT[64:128, WINDOW + 1:WINDOW + 1 + SEQ], psT[64:128, 0, :]).then_inc(S.hT, 1)
                square(n, 0)
                for hp in range(PAIRS):
                    k = n * PAIRS + hp
                    if hp + 1 < PAIRS:
                        square(n, hp + 1)
                    act.wait_ge(S.qkt, k + 3)
                    act.copy(qkT[:, :, :], psT[:, :, :]).then_inc(S.qkT, 1)
                    for h in range(2):
                        act.wait_ge(mx[h], k + 1)
                        for j in range(TILES):
                            last = act.activation(prob[:, h, j, :], psS[:, h, j * P:(j + 1) * P], ACT.Exp,
                                                  bias=nmax[:, h, j:j + 1], accum_out=rsum[:, h, j:j + 1])
                        last.then_inc(ex[h], 1)
                    for h in range(2):
                        act.wait_ge(pt[h], k + 1)
                        act.copy(probT[:, h, :], psT[:, h, :]).then_inc(PT[h], 1)
                    act.wait_ge(S.av, k + 1)
                    act.copy(oT[:, hp, :], psO).then_inc(S.oT, 1)
                act.wait_ge(S.ft, n + 1)
                act.copy(fT[0:64, 0:SEQ], psQ[0:64, 0, :]).then_inc(S.fT_half, 1)
                act.copy(fT[64:128, 1:1 + SEQ], psQ[64:128, 0, :]).then_inc(S.fT, 1)
                act.wait_ge(S.fnt, n + 1)
                act.wait_ge(S.up_in, n * 16 + 16)
                act.activation(fnT[:, :], psQ[:, 2, :], ACT.Identity, bias=up[:, UPC - 1:UPC],
                               scale=up[:, UPC - 2:UPC - 1]).then_inc(S.fnT, 1)
                for c in range(KH):
                    act.wait_ge(S.up, n * KH + (c + 1))
                    act.activation(gl[:, c, :], psQ[:, c % 2 * 2 + 1, :], ACT.Gelu,
                                   bias=up[:, W1C + KH + c:W1C + KH + c + 1]).then_inc(S.gelu, 1)

            lead(act, S.PT0, 1)
            lead(act, S.PT1, 1)
            lead(act, S.oT, 1)
            def store(b):
                act.wait_ge(S.z_ffn, 2 * b + 3)
                act.dma_start(y_tok[:, bass.ds(b * TILES, TILES), :], z[:, :, :]).then_inc(S.z_out, 16)

            passes(act, turn, store)

        @block.gpsimd
        def _(pool):
            def root(n, hp):
                k = n * PAIRS + hp
                pool.wait_ge(S.ss, k + 2)
                pool.wait_ge(S.qkn, k + 1)
                pool.tensor_tensor(rn[:, :], ss[:, :], con["mhalf"][:, 0:4 * TILES], ALU.pow).then_inc(S.rn, 1)

            def scale_qk(n, hp):
                k = n * PAIRS + hp
                pool.wait_ge(S.rot, k + 1)
                pool.wait_ge(S.rn, k + 2)
                t = qk[:, hp % 2, :, :].rearrange("p j (r d) -> p (j r) d", d=DH)
                pool.tensor_tensor(t, t, spread(rn[:, :], 2, DH), ALU.mult).then_inc(S.qkn, 1)

            def turn(b, l, n):
                root(n, 0)
                scale_qk(n, 0)
                for hp in range(PAIRS):
                    k = n * PAIRS + hp
                    if hp + 1 < PAIRS:
                        root(n, hp + 1)
                    for h in range(2):
                        pool.wait_ge(rin[h], k + 1)
                        pool.tensor_tensor(prob[:, h, :, :], prob[:, h, :, :], spread(rinv[:, h, :], 2, P),
                                           ALU.mult).then_inc(pn[h], 1)
                    if hp + 1 < PAIRS:
                        scale_qk(n, hp + 1)
                pool.wait_ge(S.fvar, n + 1)
                pool.tensor_tensor(frstd[:, :], frstd[:, :], con["mhalf"][:, 0:TILES], ALU.pow).then_inc(S.frs, 1)

            lead(pool, S.rn, 1)
            lead(pool, S.qkn, 1)
            passes(pool, turn)

        @block.vector
        def _(dve):
            own = Order(dve, S.own, PAIRS + MOMENTS)

            def sums(n, hp):
                k = n * PAIRS + hp
                dve.wait_ge(S.sq, k + 1)
                dve.wait_ge(S.rn, k + 1)
                own(dve.tensor_reduce(ss[:, :], sq[:, :, :].rearrange("p j (r d) -> p (j r) d", d=DH), AX.X, ALU.add))
                dve.tensor_scalar(ss[:, :], ss[:, :], 1e-24, None, ALU.max).then_inc(S.ss, 1)
                dve.tensor_copy(v[:, hp % 2, :, :, :].rearrange("p j a f -> p j (a f)"), psQ[:, :, 2 * P:4 * P]).then_inc(S.v, 1)

            def rotate(l, n, hp):
                k = n * PAIRS + hp
                heads = lambda t: t.rearrange("p j (c h d) -> p h j c d", c=2, h=2)
                out, out_s, src = heads(qk[:, hp % 2, :, :]), heads(rs[:, :, :]), heads(psQ[:, :, 0:4 * DH])
                tab = rot_tab[:, bass.ds(l, 1), :, :, :, :].squeeze(1)
                dve.wait_ge(S.qkt, k + 1)
                for h in range(2):
                    dve.tensor_tensor(out[:, h], src[:, h], tab[:, 0], ALU.mult).then_inc(S.rotC, 1)
                    for u in range(2):
                        a, c = slice(u * 32, u * 32 + 32), slice((1 - u) * 32, (1 - u) * 32 + 32)
                        dve.tensor_tensor(out_s[:, h, :, :, a], src[:, h, :, :, c], tab[:, 1, :, :, a], ALU.mult).then_inc(S.rotC, 1)
                dve.wait_ge(S.rotC, k * 6 + 6)
                dve.tensor_tensor(qk[:, hp % 2, :, :], qk[:, hp % 2, :, :], rs[:, :, :], ALU.add).then_inc(S.rot, 1)
                dve.wait_ge(S.rot, k + 1)

            def turn(b, l, n):
                own.start(n)
                sums(n, 0)
                rotate(l, n, 0)
                for hp in range(PAIRS):
                    k = n * PAIRS + hp
                    if hp + 1 < PAIRS:
                        sums(n, hp + 1)
                    for h in range(2):
                        dve.wait_ge(sim[h], k + 1)
                        dve.tensor_reduce(nmax[:, h, :], psS[:, h, :].rearrange("p (j c) -> p j c", j=TILES), AX.X,
                                          ALU.max, negate=True).then_inc(mx[h], 1)
                    if hp + 1 < PAIRS:
                        rotate(l, n, hp + 1)
                    for h in range(2):
                        dve.wait_ge(ex[h], k + 1)
                        dve.reciprocal(rinv[:, h, :], rsum[:, h, :]).then_inc(rin[h], 1)
                dve.wait_ge(S.wo, n + 1)
                step(dve, dve.tensor_tensor(z[:, :, :].rearrange("p j d -> p (j d)"), z[:, :, :].rearrange("p j d -> p (j d)"),
                                            psW, ALU.add), S.z_att, n + 1)
                dve.wait_ge(S.fb, n + 1)
                for j in range(TILES):
                    dve.bn_stats(fstats[:, j, :], psQ[:, 1, j * P:(j + 1) * P]).then_inc(S.fst, 1)
                dve.wait_ge(S.fst, n * TILES + TILES)
                moments(dve, own, fstats, fmean, fdiff, frstd)
                dve.tensor_scalar(frstd[:, :], frstd[:, :], EPS, None, ALU.add).then_inc(S.fvar, 1)
                dve.wait_ge(S.frs, n + 1)
                for j in range(TILES):
                    last = dve.tensor_scalar(fn[:, j, :], psQ[:, 1, j * P:(j + 1) * P], fmean[:, j:j + 1], frstd[:, j:j + 1],
                                             ALU.subtract, ALU.mult)
                last.then_inc(S.fn, 1)
                for c in range(KH):
                    dve.wait_ge(S.gelu, n * KH + (c + 1))
                    dve.scalar_tensor_tensor(out=hid[:, c, :], in0=psQ[:, c % 2 * 2, :], scalar=up[:, W1C + c:W1C + c + 1],
                                             in1=gl[:, c, :], op0=ALU.add, op1=ALU.mult).then_inc(S.hid, 1)
                dve.wait_ge(S.down, n + 1)
                step(dve, dve.tensor_tensor(z[:, :, :].rearrange("p j d -> p (j d)"), z[:, :, :].rearrange("p j d -> p (j d)"),
                                            psT[:, 0, :], ALU.add), S.z_ffn, n + 2)
                own.end()

            lead(dve, S.ss, 1)
            lead(dve, S.z_ffn, 1)
            passes(dve, turn)


def layout1(a, np):
    f = np.float32
    pad = lambda w, n: np.concatenate([w, np.zeros(w.shape[:-1] + (n - w.shape[-1],), f)], -1)
    two = lambda w: np.concatenate([pad(w[..., :HIDDEN], KH * P), pad(w[..., HIDDEN:], KH * P)], -1)
    w1, b1 = two(a["L0_ffn_w1"]), two(a["L0_ffn_b1"])
    w2 = np.concatenate([a["L0_ffn_w2"], np.zeros((LAYERS, KH * P - HIDDEN, D), f)], 1)
    half = np.arange(0, DH, 2, dtype=f)
    inv = (1.0 / 10000.0 ** (half / f(DH))).astype(f)
    t = np.arange(SEQ, dtype=f)
    freqs = t[:, None] * inv[None, :]
    base = ((half + f(0.4 * DH)) / f(1.4 * DH)).astype(f)
    decay = base[None, :] ** ((t - SEQ // 2) / f(WINDOW // 2))[:, None]
    freqs, decay = np.concatenate([freqs, freqs], 1), np.concatenate([decay, decay], 1)
    sign = np.concatenate([-np.ones(DH // 2, f), np.ones(DH // 2, f)])
    cos, sin = np.cos(freqs), np.sin(freqs) * sign
    tab = np.stack([np.stack([cos * decay * 8, cos / decay], 1), np.stack([sin * decay * 8, sin / decay], 1)])
    tab = tab.astype(f).reshape(2, TILES, P, 2, DH).transpose(2, 0, 1, 3, 4)
    gain = np.stack([a["L0_ffn_q_scale"], a["L0_ffn_k_scale"]], 1)
    gain = np.stack([gain, np.roll(gain, DH // 2, -1)], 1)
    i, c = np.arange(P)[:, None] % WINDOW, np.arange(P)[None, :]
    mask = np.where((c >= i) & (c <= i + WINDOW), 0, MASKED).astype(f)
    mask = np.tile(mask, (1, TILES))
    mask[:WINDOW, :WINDOW] = MASKED
    return {
        "wqkv": a["L0_ffn_wqkv"].transpose(1, 0, 2),
        "wo": a["L0_ffn_wo"].reshape(LAYERS, PAIRS, P, D).transpose(2, 0, 1, 3),
        "w2": w2.reshape(LAYERS, KH, P, D).transpose(2, 0, 1, 3),
        "b2": a["L0_ffn_b2"][None],
        "up": np.concatenate([w1.transpose(1, 0, 2), b1.reshape(LAYERS, 2 * KH, P).transpose(2, 0, 1),
                              a["L0_ffn_ln_g"].T[:, :, None], a["L0_ffn_ln_b"].T[:, :, None]], 2),
        "rot_base": tab,
        "qk_gain": np.tile(gain[None], (P, 1, 1, 1, 1)),
        "mask": mask,
    }


INNER, SSTATE, SHEADS, HD, TAPS = 2 * D, 64, 4, 64, 4
GROUPS2 = 4


def sequence_turns(eng, turn):
    turn(0, 0)
    with eng.Fori(0, (BATCH - 2) // 2) as i:
        turn(2 * i + 1, 1)
        turn(2 * i + 2, 0)
    turn(BATCH - 1, 1)


def stage2(nc, xn_tok, y_tok, con, dram):
    with ExitStack() as ctx:
        sb = lambda n, s: ctx.enter_context(nc.sbuf_tensor(f"s2_{n}", s, F32))
        S = semaphores(nc, ctx, "s2", "load prep xin0 xin1 xt xT dtp u absu ex ln dt a prod evac taps conv silu "
                  "xtok Xdt Btok R seg cum G E dec Gm M Cdec Xs Y St decayed state skip yg sqr ms rv rs out y")
        WC = 2 * INNER + 2 * SSTATE + SHEADS
        win = sb("win", [P, WC])
        small = sb("small", [P, GROUPS2 * (TAPS + 1) + 2 * SHEADS + 2 + 2])
        cw = small[:, 0:GROUPS2 * (TAPS + 1)].rearrange("p (g t) -> p g t", g=GROUPS2)
        o = GROUPS2 * (TAPS + 1)
        dt_bias, Alog, Dcol, norm_w = (small[:, o:o + 4], small[:, o + 4:o + 8], small[:, o + 8:o + 10], small[:, o + 10:o + 12])
        wout = sb("wout", [P, 2, D])
        tri, strict = sb("tri", [P, P]), sb("strict", [P, P])
        A = sb("A", [P, SHEADS])
        xin = sb("xin", [P, 2, TILES, D])
        xT = sb("xT", [P, SEQ])
        craw = sb("craw", [P, GROUPS2, TAPS - 1 + SEQ])
        acc = sb("acc", [P, GROUPS2, SEQ])
        xc = sb("xc", [P, 2, GROUPS2, SEQ])
        zs = sb("zs", [P, 2, 2, SEQ])
        u, au = sb("u", [P, TILES, SHEADS]), sb("au", [P, TILES, SHEADS])
        dt, a = sb("dt", [P, 2, TILES, SHEADS]), sb("a", [P, 2, TILES, SHEADS])
        Xdt, Xs = sb("Xdt", [P, SHEADS, HD]), sb("Xs", [P, SHEADS, HD])
        Btok = sb("Btok", [P, SSTATE])
        R, E, M = (sb(n, [P, SHEADS, P]) for n in ("R", "E", "M"))
        Gm = sb("Gm", [P, P])
        dec, Cdec = sb("dec", [64, SHEADS, P]), sb("Cdec", [64, SHEADS, P])
        state = sb("state", [64, 2, SHEADS, HD])
        yg, ysq = sb("yg", [P, 2, SEQ]), sb("ysq", [P, 2, SEQ])
        rs = sb("rs", [P, TILES])

        with nc.Block() as block:
            @block.sync
            def _(sp):
                for dst, name in ((win[:, :], "m_in"), (small[:, :], "m_small"), (wout[:, :, :], "m_out"),
                                  (tri[:, :], "m_tri"), (strict[:, :], "m_strict")):
                    sp.dma_start(dst, dram[name]).then_inc(S.load, 16)

            @block.scalar
            def _(act):
                act.wait_ge(S.load, 5 * 16)
                act.activation(A[:, :], Alog, ACT.Exp).then_inc(S.prep, 1)

            @block.vector
            def _(dve):
                dve.memset(craw[:, :, 0:TAPS - 1], 0.0).then_inc(S.decayed, 1)
                dve.wait_ge(S.load, 5 * 16)
                for h in range(2):
                    dve.tensor_scalar(wout[:, h, :], wout[:, h, :], norm_w[:, h:h + 1], None, ALU.mult).then_inc(S.decayed, 1)
                dve.wait_ge(S.prep, 1)
                dve.tensor_scalar(A[:, :], A[:, :], -1.0, None, ALU.mult).then_inc(S.decayed, 1)

        pb = lambda n, s: ctx.enter_context(nc.psum_tensor(f"s2_{n}", s, F32))
        psA = pb("psA", [P, 2, 512])
        psX = pb("psX", [P, 512])
        psG = pb("psG", [P, 512])
        psE, psC = pb("psE", [P, 512]), pb("psC", [P, 512])
        psY = pb("psY", [P, 2, 512])
        ST0 = P
        psO = psE
        block = ctx.enter_context(nc.Block())
        PROD = [(2 * INNER, 64), (2 * INNER + SSTATE, 64), (INNER, P), (INNER + P, P), (0, P), (P, P)]
        rows = lambda g: slice(0, PROD[g][1])
        xins = S.xin0, S.xin1

        @block.sync
        def _(sp):
            with sp.Fori(0, BATCH // 2) as i:
                for q in range(2):
                    b = 2 * i + q
                    sp.wait_ge(S.y, b + 1)
                    sp.dma_start(xin[:, q, :, :], xn_tok[:, bass.ds(b * TILES, TILES), :]).then_inc(xins[q], 16)

        @block.tensor
        def _(pe):
            def front(b, q, half_b):
                pe.wait_ge(xins[q], half_b * 16 + 16)
                pe.wait_ge(S.evac, b * 6 + 1)
                for j in range(TILES):
                    last = pe.transpose(psA[:, 0, j * P:(j + 1) * P], xin[:, q, j, :], con["ident"])
                last.then_inc(S.xt, 1)
                pe.wait_ge(S.xT, b + 1)
                pe.wait_ge(S.evac, b * 6 + 2)
                for j in range(TILES):
                    last = pe.matmul(psA[:, 1, j * SHEADS:(j + 1) * SHEADS], xT[:, j * P:(j + 1) * P],
                                     win[:, WC - SHEADS:WC], start=True, stop=True, skip_group_check=True)
                last.then_inc(S.dtp, 1)
                for g, (col, m) in enumerate(PROD):
                    pe.wait_ge(S.evac, b * 6 + (g + 1))
                    if g == 1:
                        pe.wait_ge(S.u, b + 1)
                    pe.matmul(psA[0:m, g % 2, :], win[:, col:col + m], xT[:, :], start=True, stop=True).then_inc(S.prod, 1)

            def back(b, q):
                for c in range(TILES):
                    k = b * TILES + c
                    t = slice(c * P, (c + 1) * P)
                    if c == 0:
                        pe.wait_ge(S.silu, b * 4 + 8)
                    pe.wait_ge(S.Xdt, k + 1)
                    pe.wait_ge(S.Btok, k + 1)
                    for h in range(2):
                        pe.transpose(psX[:, h * P:(h + 1) * P], xc[:, q, 2 + h, t], con["ident"])
                    pe.transpose(psX[:, 2 * P:2 * P + SSTATE], xc[0:64, q, 0, t], con["ident"][0:64, 0:64]).then_inc(S.xtok, 1)
                    pe.wait_ge(S.state, k + 1)
                    pe.matmul(psG[:, 0:P], xc[0:64, q, 0, t], xc[0:64, q, 1, t], start=True, stop=True,
                              skip_group_check=True).then_inc(S.G, 1)
                    pe.wait_ge(S.R, k + 1)
                    pe.wait_ge(S.E, k + 1)
                    if c == 0:
                        pe.wait_ge(S.y, b + 2)
                    pe.matmul(psE[:, :], strict[:, :], R[:, :, :], start=True, stop=True).then_inc(S.seg, 1)
                    pe.wait_ge(S.dec, k + 1)
                    if c == 0:
                        pe.wait_ge(S.rv, b + 1)
                    pe.matmul(psC[0:64, :], con["ones"][:, 0:64], R[:, :, :], start=True, stop=True).then_inc(S.cum, 1)
                    if c < TILES - 1:
                        pe.wait_ge(S.Xs, k + 2)
                        pe.wait_ge(S.Btok, k + 2)
                        pe.matmul(psG[0:64, ST0:ST0 + SHEADS * HD], Btok[:, :], Xs[:, :, :], start=True, stop=True,
                                  skip_group_check=True).then_inc(S.St, 1)
                    else:
                        pe.nop().then_inc(S.St, 1)
                    pe.wait_ge(S.M, k + 1)
                    pe.wait_ge(S.Cdec, k + 2)
                    if c == 0:
                        pe.wait_ge(S.yg, b + 1)
                    for h in range(SHEADS):
                        out = psY[h % 2 * 64:h % 2 * 64 + 64, h // 2, t]
                        last = pe.matmul(out, Xdt[:, h, :], M[:, h, :], start=True, stop=c == 0, skip_group_check=True)
                        if c:
                            last = pe.matmul(out, state[:, (c - 1) % 2, h, :], Cdec[:, h, :], start=False, stop=True, skip_group_check=True)
                    last.then_inc(S.Y, 1)
                pe.wait_ge(S.sqr, b + 1)
                for j in range(TILES):
                    for h in range(2):
                        last = pe.matmul(psC[:, j:j + 1], ysq[:, h, j * P:(j + 1) * P], con["ones"][:, 0:1],
                                         start=h == 0, stop=h == 1, skip_group_check=True)
                last.then_inc(S.ms, 1)
                pe.wait_ge(S.E, b * TILES + TILES + 1)
                for j in range(TILES):
                    for h in range(2):
                        last = pe.matmul(psO[:, j * P:(j + 1) * P], yg[:, h, j * P:(j + 1) * P], wout[:, h, :],
                                         start=h == 0, stop=h == 1)
                last.then_inc(S.out, 1)

            def turn(b, q):
                if not is_at(b, BATCH - 1):
                    front(b + 1, 1 - q, (b + 1 - (1 - q)) // 2 if isinstance(b, int) else (b + q) >> 1)
                back(b, q)

            lead(pe, S.cum, 1)
            lead(pe, S.St, 1)
            lead(pe, S.Y, 1)
            front(0, 0, 0)
            sequence_turns(pe, turn)

        @block.scalar
        def _(act):
            def front(b, q):
                act.wait_ge(S.xt, b + 1)
                act.copy(xT[:, :], psA[:, 0, :]).then_inc(S.xT, 1)
                act.wait_ge(S.absu, b + 1)
                step(act, act.activation(au[:, :, :], au[:, :, :], ACT.Exp, scale=-1.0), S.ex, b + 1)
                act.activation(au[:, :, :], au[:, :, :], ACT.Ln, bias=1.0).then_inc(S.ln, 1)
                for g in range(6):
                    act.wait_ge(S.prod, b * 6 + (g + 1))
                    if g < GROUPS2:
                        act.copy(craw[rows(g), g, TAPS - 1:], psA[rows(g), g % 2, :]).then_inc(S.evac, 1)
                    else:
                        act.activation(zs[:, q, g - 4, :], psA[:, g % 2, :], ACT.Silu).then_inc(S.evac, 1)
                for g in range(GROUPS2):
                    act.wait_ge(S.conv, b * 4 + (g + 1))
                    act.activation(xc[rows(g), q, g, :], acc[rows(g), g, :], ACT.Silu).then_inc(S.silu, 1)

            def back(b, q):
                for c in range(TILES):
                    k = b * TILES + c
                    act.wait_ge(S.seg, k + 1)
                    act.wait_ge(S.Xs, k + 1)
                    act.activation(E[:, :, :], psE[:, :].rearrange("p (h i) -> p h i", h=SHEADS), ACT.Exp).then_inc(S.E, 1)
                    act.wait_ge(S.cum, k + 2)
                    act.wait_ge(S.Cdec, k + 1)
                    act.wait_ge(S.state, k + 1)
                    act.activation(dec[:, :, :], psC[0:64, :].rearrange("p (h i) -> p h i", h=SHEADS), ACT.Exp).then_inc(S.dec, 1)
                act.wait_ge(S.yg, b + 2)
                act.activation(ysq[:, :, :], yg[:, :, :], ACT.Square).then_inc(S.sqr, 1)

            lead(act, S.evac, 2)
            lead(act, S.E, 1)
            lead(act, S.dec, 1)
            lead(act, S.silu, 4)
            front(0, 0)
            sequence_turns(act, lambda b, q: (None if is_at(b, BATCH - 1) else front(b + 1, 1 - q), back(b, q)))

        @block.gpsimd
        def _(pool):
            def back(b, q):
                for c in range(TILES):
                    k = b * TILES + c
                    if c == 0:
                        pool.wait_ge(S.a, b + 1)
                        pool.wait_ge(S.silu, b * 4 + 8)
                    pool.wait_ge(S.cum, k + 1)
                    pool.tensor_tensor(R[:, :, :], spread(tri[:, :], 1, SHEADS), spread(a[:, q, c, :], 2, P),
                                       ALU.mult).then_inc(S.R, 1)
                    pool.wait_ge(S.dec, k + 2)
                    pool.wait_ge(S.Y, k + 1)
                    pool.tensor_tensor(Cdec[:, :, :], dec[:, :, :], spread(xc[0:64, q, 1, c * P:(c + 1) * P], 1, SHEADS),
                                       ALU.mult).then_inc(S.Cdec, 1)
                pool.wait_ge(S.rv, b + 2)
                pool.tensor_tensor(rs[:, :], rs[:, :], con["mhalf"][:, 0:TILES], ALU.pow).then_inc(S.rs, 1)

            lead(pool, S.Cdec, 1)
            sequence_turns(pool, back)

        @block.vector
        def _(dve):
            def front(b, q):
                dve.wait_ge(S.dtp, b + 1)
                step(dve, dve.tensor_tensor(u[:, :, :], psA[:, 1, 0:TILES * SHEADS].rearrange("p (j h) -> p j h", h=SHEADS),
                                            spread(dt_bias, 1, TILES), ALU.add), S.u, b + 1)
                dve.scalar_tensor_tensor(out=au[:, :, :], in0=u[:, :, :], scalar=-1.0, in1=u[:, :, :], op0=ALU.mult,
                                         op1=ALU.max).then_inc(S.absu, 1)
                for g in range(GROUPS2):
                    r, first = rows(g), (b * GROUPS2 + g) * (TAPS - 1)
                    dve.wait_ge(S.evac, b * 6 + (g + 3))
                    dve.wait_ge(S.silu, b * 4 + (g + 1))
                    step(dve, dve.tensor_scalar(acc[r, g, :], craw[r, g, TAPS - 1:], cw[r, g, TAPS - 1:TAPS],
                                                cw[r, g, TAPS:TAPS + 1], ALU.mult, ALU.add), S.taps, first + 1)
                    for t in range(1, TAPS):
                        ins = dve.scalar_tensor_tensor(out=acc[r, g, :], in0=craw[r, g, TAPS - 1 - t:TAPS - 1 - t + SEQ],
                                                       scalar=cw[r, g, TAPS - 1 - t:TAPS - t], in1=acc[r, g, :],
                                                       op0=ALU.mult, op1=ALU.add)
                        if t < TAPS - 1:
                            step(dve, ins, S.taps, first + (t + 1))
                        else:
                            ins.then_inc(S.conv, 1)
                    if g == 0:
                        dve.wait_ge(S.ln, b + 1)
                        step(dve, dve.scalar_tensor_tensor(out=dt[:, q, :, :], in0=u[:, :, :], scalar=0.0, in1=au[:, :, :],
                                                           op0=ALU.max, op1=ALU.add), S.dt, b + 1)
                        dve.tensor_tensor(a[:, q, :, :], dt[:, q, :, :], spread(A[:, :], 1, TILES), ALU.mult).then_inc(S.a, 1)

            def back(b, q):
                for c in range(TILES):
                    k = b * TILES + c
                    dve.wait_ge(S.xtok, k + 1)
                    dve.wait_ge(S.Y, k + 1)
                    step(dve, dve.tensor_tensor(Xdt[:, :, :], psX[:, 0:SHEADS * HD].rearrange("p (h d) -> p h d", h=SHEADS),
                                                spread(dt[:, q, c, :], 2, HD), ALU.mult), S.Xdt, k + 2)
                    dve.tensor_copy(Btok[:, :], psX[:, 2 * P:2 * P + SSTATE]).then_inc(S.Btok, 1)
                    dve.wait_ge(S.G, k + 1)
                    step(dve, dve.tensor_tensor(Gm[:, :], psG[:, 0:P], tri[:, :], ALU.mult), S.Gm, k + 1)
                    dve.wait_ge(S.E, k + 2)
                    dve.tensor_tensor(M[:, :, :], E[:, :, :], spread(Gm[:, :], 1, SHEADS), ALU.mult).then_inc(S.M, 1)
                    dve.tensor_tensor(Xs[:, :, :], Xdt[:, :, :], E[:, :, P - 1:P].to_broadcast([P, SHEADS, HD]),
                                      ALU.mult).then_inc(S.Xs, 1)
                    dve.wait_ge(S.M, k + 1)
                    dve.wait_ge(S.St, k + 2)
                    add = psG[0:64, ST0:ST0 + SHEADS * HD].rearrange("p (h d) -> p h d", h=SHEADS)
                    if c == 0:
                        step(dve, dve.tensor_copy(state[:, 0, :, :], add), S.state, k + 2)
                    elif c < TILES - 1:
                        dve.wait_ge(S.dec, k + 2)
                        step(dve, dve.tensor_tensor(state[:, c % 2, :, :], state[:, (c - 1) % 2, :, :],
                                                    dec[:, :, P - 1:P].to_broadcast([64, SHEADS, HD]), ALU.mult),
                             S.decayed, 4 + b * 2 + c)
                        step(dve, dve.tensor_tensor(state[:, c % 2, :, :], state[:, c % 2, :, :], add, ALU.add), S.state, k + 2)
                    else:
                        dve.nop().then_inc(S.state, 1)
                dve.wait_ge(S.Y, b * TILES + (TILES + 1))
                for h in range(2):
                    dve.scalar_tensor_tensor(out=yg[:, h, :], in0=xc[:, q, 2 + h, :], scalar=Dcol[:, h:h + 1],
                                             in1=psY[:, h, :], op0=ALU.mult, op1=ALU.add).then_inc(S.skip, 1)
                dve.wait_ge(S.skip, b * 2 + 2)
                step(dve, dve.tensor_tensor(yg[:, :, :], yg[:, :, :], zs[:, q, :, :], ALU.mult), S.yg, b + 2)
                dve.wait_ge(S.ms, b + 1)
                dve.tensor_scalar(rs[:, :], psC[:, 0:TILES], 1.0 / INNER, EPS, ALU.mult, ALU.add).then_inc(S.rv, 1)
                dve.wait_ge(S.rs, b + 1)
                dve.wait_ge(S.out, b + 1)
                for j in range(TILES):
                    last = dve.scalar_tensor_tensor(out=y_tok[:, bass.ds(b * TILES + j, 1), :].squeeze(1),
                                                    in0=psO[:, j * P:(j + 1) * P], scalar=rs[:, j:j + 1],
                                                    in1=xin[:, q, j, :], op0=ALU.mult, op1=ALU.add)
                last.then_inc(S.y, 1)

            lead(dve, S.rv, 1)
            lead(dve, S.Xdt, 1)
            lead(dve, S.Btok, 1)
            lead(dve, S.Xs, 1)
            lead(dve, S.state, 1)
            lead(dve, S.yg, 1)
            lead(dve, S.y, 2)
            front(0, 0)
            sequence_turns(dve, lambda b, q: (None if is_at(b, BATCH - 1) else front(b + 1, 1 - q), back(b, q)))


def layout2(a, np):
    f = np.float32
    cw, cb = a["L1_attn_conv_w"], a["L1_attn_conv_b"]
    w = np.concatenate([cw, cb[:, None]], 1)
    zero = np.zeros((64, TAPS + 1), f)
    conv = np.concatenate([w[INNER:INNER + 64], zero, w[INNER + 64:], zero, w[:P], w[P:INNER]], 0)
    row = lambda v: np.tile(v[None], (P, 1))
    two = lambda v: v.reshape(2, P).T
    return {
        "m_in": a["L1_attn_W_in"].T,
        "m_small": np.concatenate([conv.reshape(GROUPS2, P, TAPS + 1).transpose(1, 0, 2).reshape(P, -1),
                                   row(a["L1_attn_dt_bias"]), row(a["L1_attn_A_log"]),
                                   two(np.repeat(a["L1_attn_D"], HD)), two(a["L1_attn_norm_w"])], 1),
        "m_out": a["L1_attn_W_out"].T.reshape(2, P, D).transpose(1, 0, 2),
        "m_tri": np.triu(np.ones((P, P), f)),
        "m_strict": np.tril(np.ones((P, P), f), -1),
    }


EXPERTS, FF = 8, 512
KF = FF // P
EC = 2 * FF + KF + 2


def stage3_route(nc, x_tok, xn_tok, con, centT, xT, gates):
    with ExitStack() as ctx:
        sb = lambda n, s: ctx.enter_context(nc.sbuf_tensor(f"g3_{n}", s, F32))
        S = semaphores(nc, ctx, "g3", "n0 n1 x0 x1 xt nt raw xT aff affs ex own")
        raw_in, norm_in = sb("raw_in", [P, 2, TILES, D]), sb("norm_in", [P, 2, TILES, D])
        rawT = sb("rawT", [P, 2, SEQ])
        aff, score = sb("aff", [P, NT, EXPERTS]), sb("score", [P, NT, EXPERTS])
        top, alpha = sb("top", [P, NT]), sb("alpha", [P, NT])
        pb = lambda n: ctx.enter_context(nc.psum_tensor(f"g3_{n}", [P, 2, 512], F32))
        ps_x, ps_n, ps_a = pb("ps_x"), pb("ps_n"), pb("ps_a")
        block = ctx.enter_context(nc.Block())

        @block.sync
        def _(sp):
            with sp.Fori(0, BATCH // 2) as i:
                for q in range(2):
                    b = 2 * i + q
                    sp.wait_ge(S.nt, b + 1)
                    sp.dma_start(raw_in[:, q, :, :], x_tok[:, bass.ds(b * TILES, TILES), :]).then_inc((S.x0, S.x1)[q], 16)
                    sp.dma_start(norm_in[:, q, :, :], xn_tok[:, bass.ds(b * TILES, TILES), :]).then_inc((S.n0, S.n1)[q], 16)

        @block.tensor
        def _(pe):
            lead(pe, S.nt, 2)
            with pe.Fori(0, BATCH // 2) as i:
                for q in range(2):
                    b = 2 * i + q
                    pe.wait_ge(S.xT, b + 1)
                    pe.wait_ge((S.x0, S.x1)[q], i * 16 + 16)
                    for j in range(TILES):
                        last = pe.transpose(ps_x[:, q, j * P:(j + 1) * P], raw_in[:, q, j, :], con["ident"])
                    last.then_inc(S.xt, 1)
                    pe.wait_ge((S.n0, S.n1)[q], i * 16 + 16)
                    for j in range(TILES):
                        last = pe.transpose(ps_n[:, q, j * P:(j + 1) * P], norm_in[:, q, j, :], con["ident"])
                    last.then_inc(S.nt, 1)
                    pe.wait_ge(S.raw, b + 1)
                    pe.wait_ge(S.affs, b + 1)
                    for j in range(TILES):
                        last = pe.matmul(ps_a[:, q, j * EXPERTS:(j + 1) * EXPERTS], rawT[:, q, j * P:(j + 1) * P], centT,
                                         start=True, stop=True, skip_group_check=True)
                    last.then_inc(S.aff, 1)

        @block.scalar
        def _(act):
            lead(act, S.xT, 2)
            with act.Fori(0, BATCH // 2) as i:
                for q in range(2):
                    b = 2 * i + q
                    act.wait_ge(S.xt, b + 1)
                    act.copy(rawT[:, q, :], ps_x[:, q, :]).then_inc(S.raw, 1)
                    act.wait_ge(S.nt, b + 3)
                    act.copy(xT[:, bass.ds(b * SEQ, SEQ)], ps_n[:, q, :]).then_inc(S.xT, 1)
            act.wait_ge(S.own, 1)
            act.activation(alpha[:, :], top[:, :], ACT.Exp, scale=-1.0).then_inc(S.ex, 1)

        @block.vector
        def _(dve):
            lead(dve, S.affs, 2)
            with dve.Fori(0, BATCH // 2) as i:
                for q in range(2):
                    b = 2 * i + q
                    dve.wait_ge(S.aff, b + 1)
                    dve.tensor_copy(aff[:, bass.ds(b * TILES, TILES), :],
                                    ps_a[:, q, 0:TILES * EXPERTS].rearrange("p (j e) -> p j e", j=TILES)).then_inc(S.affs, 1)
            dve.wait_ge(S.affs, 2 + BATCH)
            own = Order(dve, S.own)
            own(dve.tensor_reduce(top[:, :], aff[:, :, :], AX.X, ALU.max))
            own(dve.tensor_tensor(score[:, :, :], aff[:, :, :], spread(top[:, :], 2, EXPERTS), ALU.is_equal))
            own(dve.tensor_tensor(score[:, :, :], score[:, :, :], spread(con["countdown"], 1, NT), ALU.mult))
            dve.wait_ge(S.ex, 1)
            own(dve.tensor_reduce(top[:, :], score[:, :, :], AX.X, ALU.max))
            own(dve.tensor_tensor(score[:, :, :], score[:, :, :], spread(top[:, :], 2, EXPERTS), ALU.is_equal))
            own(dve.tensor_scalar(alpha[:, :], alpha[:, :], 1.0, None, ALU.add))
            own(dve.reciprocal(alpha[:, :], alpha[:, :]))
            own(dve.tensor_tensor(gates[:, :, :], score[:, :, :], spread(alpha[:, :], 2, EXPERTS), ALU.mult))


def edge_turns(eng, turn, n):
    turn(0)
    with eng.Fori(0, n - 2) as i:
        turn(i + 1)
    turn(n - 1)


def stage3_experts(nc, con, dram, xT, gates, acc):
    with ExitStack() as ctx:
        sb = lambda n, s: ctx.enter_context(nc.sbuf_tensor(f"e3_{n}", s, F32))
        S = semaphores(nc, ctx, "e3", " ".join(f"w{e}" for e in range(EXPERTS)) + " b2 x up hA hV down acc own")
        wts = sb("wts", [P, EXPERTS, EC])
        b2 = sb("b2", [1, EXPERTS, D])
        xe = sb("xe", [P, 2, SEQ])
        hid = sb("hid", [P, 2, KF, SEQ])
        ps_u = ctx.enter_context(nc.psum_tensor("e3_ps_u", [P, KF, 512], F32))
        ps_d = ctx.enter_context(nc.psum_tensor("e3_ps_d", [P, 2, 512], F32))
        loaded = S[:EXPERTS]
        w1 = lambda e, f: wts[:, e, f * P:(f + 1) * P]
        w2 = lambda e, f: wts[:, e, FF + f * P:FF + (f + 1) * P]
        b1 = lambda e, f: wts[:, e, 2 * FF + f:2 * FF + f + 1]
        ACT_F = KF - 1
        block = ctx.enter_context(nc.Block())

        def following(b, e):
            if e + 1 < EXPERTS:
                return b, e + 1
            return None if is_at(b, BATCH - 1) else (b + 1, 0)

        def preceding(b, e):
            if e:
                return b, e - 1
            return None if is_at(b, 0) else (b - 1, EXPERTS - 1)

        @block.sync
        def _(sp):
            sp.dma_start(b2[:, :, :], dram["eb2"]).then_inc(S.b2, 16)
            for e in range(EXPERTS):
                sp.dma_start(wts[:, e, :], dram["ew"][:, e, :]).then_inc(loaded[e], 16)

        @block.tensor
        def _(pe):
            def ups(b, e):
                m = b * EXPERTS + e
                pe.wait_ge(loaded[e], 16)
                pe.wait_ge(S.x, m + 1)
                pe.wait_ge(S.hA, m + 1)
                pe.wait_ge(S.hV, m + 1)
                for f in range(KF):
                    pe.matmul(ps_u[:, f, :], w1(e, f), xe[:, e % 2, :], start=True, stop=True).then_inc(S.up, 1)

            def turn(b):
                for e in range(EXPERTS):
                    m = b * EXPERTS + e
                    if following(b, e):
                        ups(*following(b, e))
                    else:
                        pe.wait_ge(S.hA, m + 2)
                        pe.wait_ge(S.hV, m + 2)
                    pe.wait_ge(S.acc, m + 1)
                    for j in range(TILES):
                        for f in range(KF):
                            pe.matmul(ps_d[:, e % 2, j * P:(j + 1) * P], hid[:, e % 2, f, j * P:(j + 1) * P], w2(e, f),
                                      start=f == 0, stop=False)
                        last = pe.matmul(ps_d[:, e % 2, j * P:(j + 1) * P], con["ones"][0:1, :], b2[:, e, :],
                                         start=False, stop=True)
                    last.then_inc(S.down, 1)

            lead(pe, S.down, 2)
            pe.wait_ge(S.b2, 16)
            ups(0, 0)
            edge_turns(pe, turn, BATCH)

        @block.scalar
        def _(act):
            def turn(b):
                for e in range(EXPERTS):
                    m = b * EXPERTS + e
                    act.wait_ge(S.down, m + 1)
                    for f in range(ACT_F):
                        act.wait_ge(S.up, m * KF + (f + 1))
                        last = act.activation(hid[:, e % 2, f, :], ps_u[:, f, :], ACT.Relu, bias=b1(e, f))
                    last.then_inc(S.hA, 1)

            lead(act, S.hA, 1)
            for e in range(EXPERTS):
                act.wait_ge(loaded[e], 16)
            edge_turns(act, turn, BATCH)

        @block.vector
        def _(dve):
            def affine(b, e):
                dve.tensor_scalar(xe[:, e % 2, :], xT[:, bass.ds(b * SEQ, SEQ)], wts[:, e, EC - 2:EC - 1],
                                  wts[:, e, EC - 1:EC], ALU.mult, ALU.add).then_inc(S.x, 1)

            def add(b, e):
                m = b * EXPERTS + e
                dve.wait_ge(S.down, m + 3)
                for j in range(TILES):
                    t = b * TILES + j
                    a = acc[:, bass.ds(t, 1), :].squeeze(1)
                    last = dve.scalar_tensor_tensor(out=a, in0=ps_d[:, e % 2, j * P:(j + 1) * P],
                                                    scalar=gates[:, bass.ds(t, 1), e], in1=a, op0=ALU.mult, op1=ALU.add)
                last.then_inc(S.acc, 1)
                dve.wait_ge(S.acc, m + 3)

            def turn(b):
                for e in range(EXPERTS):
                    m = b * EXPERTS + e
                    if following(b, e):
                        affine(*following(b, e))
                    dve.wait_ge(S.down, m + 1)
                    for f in range(ACT_F, KF):
                        dve.wait_ge(S.up, m * KF + (f + 1))
                        last = dve.tensor_scalar(hid[:, e % 2, f, :], ps_u[:, f, :], b1(e, f), 0.0, ALU.add, ALU.max)
                    last.then_inc(S.hV, 1)
                    if preceding(b, e):
                        add(*preceding(b, e))

            lead(dve, S.hV, 1)
            lead(dve, S.acc, 2)
            for e in range(EXPERTS):
                dve.wait_ge(loaded[e], 16)
            affine(0, 0)
            edge_turns(dve, turn, BATCH)
            add(BATCH - 1, EXPERTS - 1)


def stage3(nc, xn_tok, y_tok, con, dram):
    with ExitStack() as ctx:
        sb = lambda n, s: ctx.enter_context(nc.sbuf_tensor(f"s3_{n}", s, F32))
        S = semaphores(nc, ctx, "s3", "load copy")
        small = sb("small", [P, EXPERTS])
        xT, gates = sb("xT", [P, BATCH * SEQ]), sb("gates", [P, NT, EXPERTS])
        twice = sb("twice", [P, NT, D])
        with nc.Block() as block:
            @block.sync
            def _(sp):
                sp.dma_start(small[:, :], dram["e_small"]).then_inc(S.load, 16)
                sp.wait_ge(S.load, 16)
        normalize(nc, "n3b", con, xn_tok, twice)
        stage3_route(nc, xn_tok, twice, con, small[:, 0:EXPERTS], xT, gates)
        with nc.Block() as block:
            @block.vector
            def _(dve):
                dve.tensor_copy(y_tok[:, :, :], xn_tok[:, :, :]).then_inc(S.copy, 1)
        stage3_experts(nc, con, dram, xT, gates, y_tok)


def layout3(a, np):
    w1 = a["L1_ffn_w1"].transpose(1, 0, 2)
    w2 = a["L1_ffn_w2"].reshape(EXPERTS, KF, P, D).transpose(2, 0, 1, 3).reshape(P, EXPERTS, FF)
    return {
        "ew": np.concatenate([w1, w2, a["L1_ffn_b1"].reshape(EXPERTS, KF, P).transpose(2, 0, 1),
                              a["L1_ffn_ln_g"].T[:, :, None], a["L1_ffn_ln_b"].T[:, :, None]], 2),
        "eb2": a["L1_ffn_b2"][None],
        "e_small": a["L1_ffn_centroids"].T,
    }

def host_layout(a, np):
    return {**layout1(a, np), **layout2(a, np), **layout3(a, np)}


def build(nc, x, consts, w0, out, extra):
    with ExitStack() as ctx:
        sb = lambda n, s, t=F32: ctx.enter_context(nc.sbuf_tensor(n, s, t))
        x_tok, xn_tok, y_tok = (sb(n, [P, NT, D]) for n in ("x_tok", "xn_tok", "y_tok"))
        kc = sb("con_sb", [P, 2 * P + 2 * 64 + 1 + 8])
        con = dict(ident=kc[:, 0:P], ones=kc[:, P:2 * P], half=kc[:, 2 * P:2 * P + 64],
                   mhalf=kc[:, 2 * P + 64:2 * P + 128], clamp_dt=kc[:, 2 * P + 128:2 * P + 129],
                   countdown=kc[:, 2 * P + 129:2 * P + 137])
        S = semaphores(nc, ctx, "io", "load store")
        tiles = lambda t: t.rearrange("b (j p) d -> p (b j) d", p=P)
        with nc.Block() as block:
            @block.sync
            def _(sp):
                sp.dma_start(kc[:, :], consts).then_inc(S.load, 16)
                sp.dma_start(x_tok[:, :, :], tiles(x)).then_inc(S.load, 16)
                sp.wait_ge(S.load, 32)
        if FIRST < 1:
            normalize(nc, "n0", con, x_tok, xn_tok)
            stage0(nc, None, xn_tok, y_tok, con, w0)
            normalize(nc, "r0", con, y_tok, xn_tok, x_tok)
        if STAGES > 1 and FIRST < 2:
            normalize(nc, "n1", con, x_tok, xn_tok)
            stage1(nc, xn_tok, y_tok, con, extra)
            normalize(nc, "r1", con, y_tok, xn_tok, x_tok)
        if STAGES > 2 and FIRST < 3:
            normalize(nc, "n2", con, x_tok, xn_tok)
            stage2(nc, xn_tok, y_tok, con, extra)
            normalize(nc, "r2", con, y_tok, xn_tok, x_tok)
        if STAGES > 3:
            normalize(nc, "n3", con, x_tok, xn_tok)
            stage3(nc, xn_tok, y_tok, con, extra)
            normalize(nc, "r3", con, y_tok, xn_tok, x_tok)
        with nc.Block() as block:
            @block.sync
            def _(sp):
                sp.dma_start(tiles(out), x_tok[:, :, :]).then_inc(S.store, 16)
                sp.wait_ge(S.store, 16)


def kernel(**inputs):
    import numpy as np
    import concourse.bacc as bacc
    from concourse.bass_utils import run_bass_kernel_spmd

    a = {k: np.asarray(v) for k, v in inputs.items()}
    f = np.float32
    c, r = (0.1 + 0.001) / 2, (0.1 - 0.001) / 2
    arrays = {
        "x": a["L0_attn_x"],
        "consts": np.concatenate([np.eye(P, dtype=f), np.ones((P, P), f), np.full((P, 64), 0.5, f),
                                  np.full((P, 64), -0.5, f), np.full((P, 1), -c * 0.5 / (r + 1e-8), f),
                                  np.tile(np.arange(8, 0, -1, dtype=f), (P, 1))], 1),
        "w0": np.concatenate([a["L0_attn_W_dt"].T, a["L0_attn_W_B"].T, a["L0_attn_W_C"].T, a["L0_attn_A_log"],
                              a["L0_attn_b_dt"][:, None], a["L0_attn_D_param"][:, None]], 1),
    }
    arrays.update(host_layout(a, np))
    arrays = {k: np.ascontiguousarray(v) for k, v in arrays.items()}
    nc = bacc.Bacc("TRN2", target_bir_lowering=False, num_devices=1)
    dram = {k: nc.dram_tensor(k, v.shape, mybir.dt.from_np(v.dtype), kind="ExternalInput").ap() for k, v in arrays.items()}
    out = nc.dram_tensor("out", a["L0_attn_x"].shape, F32, kind="ExternalOutput").ap()
    build(nc, dram.pop("x"), dram.pop("consts"), dram.pop("w0"), out, dram)
    result = run_bass_kernel_spmd(nc, [arrays], core_ids=[0])
    return result.results[0]["out"]
```

```python
import concourse.bass as bass
from concourse import mybir
from collections import namedtuple
from contextlib import ExitStack

F32 = mybir.dt.float32
BF16 = mybir.dt.bfloat16
ALU = mybir.AluOpType
ACT = mybir.ActivationFunctionType
AX = mybir.AxisListType

P = 128
BATCH, SEQ, D = 8, 512, 128
TILES = SEQ // P
EPS = 1e-5
STAGES = 4
FIRST = 0


def semaphores(nc, ctx, prefix, names):
    sems = [nc.alloc_semaphore(name=f"{prefix}_{n}") for n in names.split()]

    def clear():
        nc.clear_and_free_semaphores(sems)
        nc.all_engine_barrier()

    ctx.callback(clear)
    return namedtuple("Semaphores", names)(*sems)


def lead(eng, sem, n):
    for _ in range(n):
        eng.nop().then_inc(sem, 1)


def step(eng, ins, sem, count):
    ins.then_inc(sem, 1)
    eng.wait_ge(sem, count)


class Order:

    def __init__(self, eng, sem, per=0, base=0):
        self.eng, self.sem, self.per, self.base, self.turn, self.n = eng, sem, per, base, 0, 0

    def start(self, turn):
        self.turn, self.n = turn, 0

    def __call__(self, ins):
        self.n += 1
        step(self.eng, ins, self.sem, self.turn * self.per + (self.base + self.n))

    def end(self):
        assert self.n == self.per, (self.n, self.per)


def spread(ap, axis, n):
    ap = ap.unsqueeze(axis)
    return ap.to_broadcast([n if k == axis else m for k, m in enumerate(ap.shape)])


NT = BATCH * TILES


def stage_sequences(sp, src, buf, used, staged):
    with sp.Fori(0, BATCH // 2) as i:
        for q in range(2):
            sp.wait_ge(used, 2 * i + (q + 1))
            sp.dma_start(buf[:, q, :, :], src[:, bass.ds((2 * i + q) * TILES, TILES), :]).then_inc(staged[q], 16)


def transpose_sequences(pe, buf, ps, con, staged, copied, done):
    lead(pe, done, 2)
    with pe.Fori(0, BATCH // 2) as i:
        for q in range(2):
            pe.wait_ge(copied, 2 * i + (q + 1))
            pe.wait_ge(staged[q], i * 16 + 16)
            for j in range(TILES):
                last = pe.transpose(ps[:, q, j * P:(j + 1) * P], buf[:, q, j, :], con["ident"])
            last.then_inc(done, 1)


MOMENTS = 6


def moments(dve, own, stats, mean, diff, var):
    own(dve.tensor_tensor(mean[:, :], stats[:, :, 1], stats[:, :, 4], ALU.add))
    own(dve.tensor_scalar(mean[:, :], mean[:, :], 0.5, None, ALU.mult))
    own(dve.tensor_tensor(diff[:, :], stats[:, :, 1], stats[:, :, 4], ALU.subtract))
    own(dve.scalar_tensor_tensor(out=diff[:, :], in0=diff[:, :], scalar=0.25, in1=diff[:, :], op0=ALU.mult, op1=ALU.mult))
    own(dve.tensor_tensor(var[:, :], stats[:, :, 2], stats[:, :, 5], ALU.add))
    own(dve.scalar_tensor_tensor(out=var[:, :], in0=var[:, :], scalar=1.0 / D, in1=diff[:, :], op0=ALU.mult, op1=ALU.add))


def normalize(nc, tag, con, src, dst, add_to=None):
    with ExitStack() as ctx:
        sb = lambda n, s: ctx.enter_context(nc.sbuf_tensor(f"{tag}_{n}", s, F32))
        S = semaphores(nc, ctx, tag, "stats own veps rstd")
        stats = sb("stats", [P, NT, 6])
        mean, diff, var, rstd = (sb(n, [P, NT]) for n in ("mean", "diff", "var", "rstd"))
        block = ctx.enter_context(nc.Block())

        @block.vector
        def _(dve):
            with dve.Fori(0, NT // 4) as i:
                for j in range(4):
                    t = 4 * i + j
                    dve.bn_stats(stats[:, bass.ds(t, 1), :].squeeze(1), src[:, bass.ds(t, 1), :].squeeze(1)).then_inc(S.stats, 1)
            dve.wait_ge(S.stats, NT)
            own = Order(dve, S.own)
            moments(dve, own, stats, mean, diff, var)
            dve.tensor_scalar(var[:, :], var[:, :], EPS, None, ALU.add).then_inc(S.veps, 1)
            dve.wait_ge(S.rstd, 1)
            n0 = own.n
            with dve.Fori(0, NT // 4) as i:
                for j in range(4):
                    t = 4 * i + j
                    dve.tensor_scalar(dst[:, bass.ds(t, 1), :].squeeze(1), src[:, bass.ds(t, 1), :].squeeze(1),
                                      mean[:, bass.ds(t, 1)], rstd[:, bass.ds(t, 1)], ALU.subtract, ALU.mult).then_inc(S.own, 1)
            if add_to is not None:
                dve.wait_ge(S.own, n0 + NT)
                dve.tensor_tensor(add_to[:, :, :], add_to[:, :, :], dst[:, :, :], ALU.add).then_inc(S.own, 1)

        @block.gpsimd
        def _(pool):
            pool.wait_ge(S.veps, 1)
            pool.tensor_tensor(rstd[:, :], var[:, :], con["mhalf"][:, 0:NT], ALU.pow).then_inc(S.rstd, 1)


N_STATE = 8
STEPS = 10
CHUNKS = -(-SEQ // STEPS)
CW = BATCH * STEPS
HALF = N_STATE // 2 * CW
COLS0 = CHUNKS * CW


def stage0_project(nc, xn_tok, w, con, xnT, dt, dtx):
    with ExitStack() as ctx:
        sb = lambda n, s: ctx.enter_context(nc.sbuf_tensor(n, s, F32))
        S = semaphores(nc, ctx, "p0", "staged0 staged1 xt xT xT_part proj u absu ex ln sp th pad dt dtx")
        xn = sb("p0_xn", [P, 2, TILES, D])
        u, a = sb("p0_u", [P, COLS0]), sb("p0_a", [P, COLS0])
        ps_t = ctx.enter_context(nc.psum_tensor("p0_ps_t", [P, 2, SEQ], F32))
        ps_p = ctx.enter_context(nc.psum_tensor("p0_ps_p", [P, 2, SEQ], F32))
        GROUPS, GW = 10, COLS0 // 10
        c, r = (0.1 + 0.001) / 2, (0.1 - 0.001) / 2
        block = ctx.enter_context(nc.Block())

        @block.sync
        def _(sp):
            stage_sequences(sp, xn_tok, xn, S.xt, (S.staged0, S.staged1))

        @block.vector
        def _(dve):
            dve.memset(xnT[:, (CHUNKS - 1) * CW:], 0.0).then_inc(S.pad, 1)
            dve.wait_ge(S.u, 2 + GROUPS)
            dve.scalar_tensor_tensor(out=a[:, :], in0=u[:, :], scalar=-1.0, in1=u[:, :], op0=ALU.mult,
                                     op1=ALU.max).then_inc(S.absu, 1)
            dve.wait_ge(S.ln, 1)
            dve.scalar_tensor_tensor(out=u[:, :], in0=u[:, :], scalar=0.0, in1=a[:, :], op0=ALU.max,
                                     op1=ALU.add).then_inc(S.sp, 1)
            dve.wait_ge(S.th, 1)
            step(dve, dve.tensor_scalar(dt[:, :], u[:, :], r / 0.5, c, ALU.mult, ALU.add), S.dt, 1)
            dve.wait_ge(S.xT, 2 + BATCH)
            step(dve, dve.tensor_tensor(dtx[:, :], dt[:, :], xnT[:, :], ALU.mult), S.dtx, 1)

        @block.tensor
        def _(pe):
            transpose_sequences(pe, xn, ps_t, con, (S.staged0, S.staged1), S.xT, S.xt)
            pe.wait_ge(S.xT, 2 + BATCH)
            pe.wait_ge(S.pad, 1)
            with pe.Fori(0, GROUPS // 2) as i:
                for q in range(2):
                    pe.wait_ge(S.u, 2 * i + (q + 1))
                    pe.matmul(ps_p[:, q, 0:GW], w["W_dtT"], xnT[:, bass.ds((2 * i + q) * GW, GW)],
                              start=True, stop=True).then_inc(S.proj, 1)

        @block.scalar
        def _(act):
            lead(act, S.xT, 2)
            lead(act, S.u, 2)
            full = (CHUNKS - 1) * STEPS
            cols = xnT[:, :].rearrange("p (k b t) -> p k b t", b=BATCH, t=STEPS)
            act.wait_ge(S.pad, 1)
            with act.Fori(0, BATCH // 2) as i:
                for q in range(2):
                    act.wait_ge(S.xt, 2 * i + (q + 3))
                    b = 2 * i + q
                    act.copy(cols[:, 0:CHUNKS - 1, bass.ds(b, 1), :],
                             ps_t[:, q, 0:full].rearrange("p (k t) -> p k t", t=STEPS).unsqueeze(2)).then_inc(S.xT_part, 1)
                    act.wait_ge(S.xT_part, 2 * i + (q + 1))
                    act.copy(cols[:, CHUNKS - 1, bass.ds(b, 1), 0:SEQ - full],
                             ps_t[:, q, full:SEQ].unsqueeze(1)).then_inc(S.xT, 1)
            with act.Fori(0, GROUPS // 2) as i:
                for q in range(2):
                    act.wait_ge(S.proj, 2 * i + (q + 1))
                    act.activation(u[:, bass.ds((2 * i + q) * GW, GW)], ps_p[:, q, 0:GW], ACT.Identity,
                                   bias=w["b_dt"]).then_inc(S.u, 1)
            act.wait_ge(S.absu, 1)
            step(act, act.activation(a[:, :], a[:, :], ACT.Exp, scale=-1.0), S.ex, 1)
            step(act, act.activation(a[:, :], a[:, :], ACT.Ln, bias=1.0), S.ln, 1)
            act.wait_ge(S.sp, 1)
            act.activation(u[:, :], u[:, :], ACT.Tanh, scale=0.5 / (r + 1e-8), bias=con["clamp_dt"]).then_inc(S.th, 1)


def chunk_turns(eng, turn):
    turn(0, 0)
    with eng.Fori(0, (CHUNKS - 2) // 2) as i:
        turn(2 * i + 1, 1)
        turn(2 * i + 2, 0)
    turn(CHUNKS - 1, 1)


def is_at(k, chunk):
    return isinstance(k, int) and k == chunk


def stage0_scan(nc, w, con, xnT, dt, dtx, y):
    with ExitStack() as ctx:
        sb = lambda n, s: ctx.enter_context(nc.sbuf_tensor(n, s, F32))
        pb = lambda n, s: ctx.enter_context(nc.psum_tensor(n, s, F32))
        S = semaphores(nc, ctx, "s0", "arg tanh dA B C dBx sq ones ss root h hC Y out own zero")
        W, ROWS = N_STATE * CW, N_STATE * BATCH
        arg = sb("s0_arg", [P, 2, W])
        dA = sb("s0_dA", [P, 2, W])
        dBx = sb("s0_dBx", [P, 2, W])
        h = sb("s0_h", [P, 2, W])
        hC = sb("s0_hC", [P, 2, W])
        first = sb("s0_first", [P, ROWS])
        sq = sb("s0_sq", [P, ROWS])
        ss, root, scale = sb("s0_ss", [P, BATCH]), sb("s0_root", [P, BATCH]), sb("s0_scale", [P, BATCH])
        psB, psC = pb("s0_psB", [P, 2, 512]), pb("s0_psC", [P, 2, 512])
        psS = pb("s0_psS", [P, 512])
        psY = pb("s0_psY", [P, 2, 512])
        block = ctx.enter_context(nc.Block())
        step_of = lambda t, s: t.rearrange("p (r t) -> p r t", t=STEPS)[:, :, s]
        halves = lambda t: t.rearrange("p (a n c) -> p a n c", a=2, n=N_STATE // 2)
        banks = lambda t: t[:, :, 0:HALF].rearrange("p a (n c) -> p a n c", n=N_STATE // 2)

        @block.gpsimd
        def _(pool):
            def decay_argument(k, q):
                pool.wait_ge(S.dA, k + 1)
                pool.tensor_tensor(arg[:, q, :].rearrange("p (n c) -> p n c", n=N_STATE),
                                   spread(dt[:, bass.ds(k * CW, CW)], 1, N_STATE),
                                   spread(w["A16"], 2, CW), ALU.mult).then_inc(S.arg, 1)

            def turn(k, q):
                pool.wait_ge(S.ss, k + 1)
                pool.tensor_tensor(root[:, :], ss[:, :], con["half"][:, 0:BATCH], ALU.pow).then_inc(S.root, 1)
                if not is_at(k, CHUNKS - 1):
                    decay_argument(k + 1, 1 - q)

            decay_argument(0, 0)
            chunk_turns(pool, turn)

        @block.scalar
        def _(act):
            lead(act, S.dA, 2)
            lead(act, S.out, 2)

            def decay(k, q):
                act.wait_ge(S.arg, k + 1)
                step(act, act.activation(arg[:, q, :], arg[:, q, :], ACT.Tanh), S.tanh, k + 1)
                act.wait_ge(S.h, k + 1)
                act.activation(dA[:, q, :], arg[:, q, :], ACT.Exp, scale=16.0).then_inc(S.dA, 1)

            def copy_out(k, q):
                act.wait_ge(S.Y, k + 3)
                act.copy(y[:, :, bass.ds(k * STEPS, STEPS)],
                         psY[:, q, 0:CW].rearrange("p (b t) -> p b t", b=BATCH)).then_inc(S.out, 1)

            def turn(k, q):
                if not is_at(k, CHUNKS - 1):
                    decay(k + 1, 1 - q)
                if not is_at(k, 0):
                    copy_out(k - 1, 1 - q)

            decay(0, 0)
            chunk_turns(act, turn)
            copy_out(CHUNKS - 1, 1)

        @block.tensor
        def _(pe):
            def rows_of(ps, weights, k, used, count, ready):
                pe.wait_ge(used, count)
                for n in range(N_STATE):
                    o = n % 4 * CW
                    last = pe.matmul(ps[:, n // 4, o:o + CW], weights[:, n, :], xnT[:, bass.ds(k * CW, CW)],
                                     start=True, stop=True)
                last.then_inc(ready, 1)

            def sum_states(k, q):
                pe.wait_ge(S.hC, k + 2)
                pe.wait_ge(S.out, k + 1)
                pe.matmul(psY[:, q, 0:CW], w["diagD"], xnT[:, bass.ds(k * CW, CW)], start=True, stop=False)
                for n in range(N_STATE):
                    last = pe.matmul(psY[:, q, 0:CW], con["ident"], hC[:, q, n * CW:(n + 1) * CW],
                                     start=False, stop=n == N_STATE - 1)
                last.then_inc(S.Y, 1)

            def turn(k, q):
                pe.wait_ge(S.sq, k + 1)
                pe.matmul(psS[:, 0:ROWS], con["ones"], sq[:, :], start=True, stop=True).then_inc(S.ones, 1)
                if not is_at(k, CHUNKS - 1):
                    rows_of(psB, w["WB_rep"], k + 1, S.dBx, k + 2, S.B)
                if not is_at(k, 0):
                    sum_states(k - 1, 1 - q)
                rows_of(psC, w["WC_rep"], k, S.hC, k + 1, S.C)

            lead(pe, S.Y, 2)
            rows_of(psB, w["WB_rep"], 0, S.dBx, 1, S.B)
            chunk_turns(pe, turn)
            sum_states(CHUNKS - 1, 1)

        @block.vector
        def _(dve):
            OWN = 7
            own = Order(dve, S.own, OWN)

            def inputs(k, q):
                dve.wait_ge(S.B, k + 1)
                dve.tensor_tensor(halves(dBx[:, q, :]), banks(psB),
                                  spread(dtx[:, bass.ds(k * CW, CW)], 1, N_STATE).rearrange("p (a n) c -> p a n c", a=2),
                                  ALU.mult).then_inc(S.dBx, 1)

            def outputs(k, q):
                dve.wait_ge(S.C, k + 1)
                dve.wait_ge(S.Y, k + 1)
                dve.tensor_tensor(halves(hC[:, q, :]), banks(psC), halves(h[:, q, :]), ALU.mult).then_inc(S.hC, 1)

            lead(dve, S.h, 2)
            lead(dve, S.dBx, 1)
            lead(dve, S.hC, 1)
            step(dve, dve.memset(h[:, :, :], 0.0), S.zero, 1)
            inputs(0, 0)

            def turn(k, q):
                own.start(k)
                dve.wait_ge(S.dBx, k + 2)
                dve.wait_ge(S.dA, k + 3)
                own(dve.tensor_tensor(first[:, :], step_of(dA[:, q, :], 0), step_of(h[:, 1 - q, :], STEPS - 1), ALU.mult))
                own(dve.tensor_tensor(first[:, :], first[:, :], step_of(dBx[:, q, :], 0), ALU.add))
                step(dve, dve.tensor_tensor(sq[:, :], first[:, :], first[:, :], ALU.mult), S.sq, k + 1)
                own(dve.memset(step_of(dA[:, q, :], 0), 0.0))
                dve.wait_ge(S.ones, k + 1)
                step(dve, dve.tensor_reduce(ss[:, :], psS[:, 0:ROWS].rearrange("p (n b) -> p b n", b=BATCH), AX.X,
                                            ALU.add), S.ss, k + 1)
                if not is_at(k, 0):
                    outputs(k - 1, 1 - q)
                if not is_at(k, CHUNKS - 1):
                    inputs(k + 1, 1 - q)
                dve.wait_ge(S.root, k + 1)
                own(dve.tensor_scalar(scale[:, :], root[:, :], 1e-8, None, ALU.add))
                own(dve.reciprocal(scale[:, :], scale[:, :]))
                own(dve.tensor_scalar(scale[:, :], scale[:, :], 20.0, 1.0, ALU.mult, ALU.min))
                own(dve.tensor_tensor(step_of(dBx[:, q, :], 0).rearrange("p (n b) -> p n b", b=BATCH),
                                      first[:, :].rearrange("p (n b) -> p n b", b=BATCH),
                                      spread(scale[:, :], 1, N_STATE), ALU.mult))
                step(dve, dve.tensor_tensor_scan(h[:, q, :], dA[:, q, :], dBx[:, q, :], 0.0, ALU.mult, ALU.add),
                     S.h, k + 3)
                own.end()

            chunk_turns(dve, turn)
            outputs(CHUNKS - 1, 1)


def stage0_output(nc, y, con, y_tok):
    with ExitStack() as ctx:
        S = semaphores(nc, ctx, "o0", "staged0 staged1 yt y_tok")
        buf = ctx.enter_context(nc.sbuf_tensor("o0_buf", [P, 2, TILES, P], F32))
        ps = ctx.enter_context(nc.psum_tensor("o0_ps", [P, 2, SEQ], F32))
        block = ctx.enter_context(nc.Block())

        @block.sync
        def _(sp):
            with sp.Fori(0, BATCH // 2) as i:
                for q in range(2):
                    sp.wait_ge(S.yt, 2 * i + (q + 1))
                    sp.dma_start(buf[:, q, :, :].rearrange("p j t -> p (j t)"),
                                 y[:, bass.ds(2 * i + q, 1), 0:SEQ].squeeze(1)).then_inc((S.staged0, S.staged1)[q], 16)

        @block.tensor
        def _(pe):
            transpose_sequences(pe, buf, ps, con, (S.staged0, S.staged1), S.y_tok, S.yt)

        @block.scalar
        def _(act):
            lead(act, S.y_tok, 2)
            with act.Fori(0, BATCH // 2) as i:
                for q in range(2):
                    act.wait_ge(S.yt, 2 * i + (q + 3))
                    act.copy(y_tok[:, bass.ds((2 * i + q) * TILES, TILES), :],
                             ps[:, q, :].rearrange("p (j d) -> p j d", j=TILES)).then_inc(S.y_tok, 1)


def stage0(nc, mem, xn_tok, y_tok, con, weights):
    with ExitStack() as ctx:
        sb = lambda n, s: ctx.enter_context(nc.sbuf_tensor(n, s, F32))
        W0 = 2 * D + 2 * N_STATE + N_STATE + 2
        raw = sb("w0_raw", [P, W0])
        wdt, wb, wc = raw[:, 0:D], raw[:, D:D + N_STATE], raw[:, D + N_STATE:D + 2 * N_STATE]
        alog, bdt, dpar = (raw[:, D + 2 * N_STATE:D + 3 * N_STATE], raw[:, D + 3 * N_STATE:D + 3 * N_STATE + 1],
                           raw[:, D + 3 * N_STATE + 1:D + 3 * N_STATE + 2])
        WBr, WCr = sb("w0_WB", [P, N_STATE, P]), sb("w0_WC", [P, N_STATE, P])
        A16, diagD = sb("w0_A16", [P, N_STATE]), sb("w0_diagD", [P, P])
        S = semaphores(nc, ctx, "w0", "load th ex own")
        with nc.Block() as block:
            @block.sync
            def _(sp):
                sp.dma_start(raw[:, 0:D + 3 * N_STATE + 2], weights).then_inc(S.load, 16)

            @block.scalar
            def _(act):
                act.wait_ge(S.load, 16)
                step(act, act.activation(A16[:, :], alog, ACT.Tanh, scale=0.5 / (5.0 + 1e-8)), S.th, 1)
                act.activation(A16[:, :], A16[:, :], ACT.Exp, scale=10.0).then_inc(S.ex, 1)

            @block.vector
            def _(dve):
                dve.wait_ge(S.load, 16)
                dve.tensor_copy(WBr[:, :, :], spread(wb, 2, P)).then_inc(S.own, 1)
                dve.tensor_copy(WCr[:, :, :], spread(wc, 2, P)).then_inc(S.own, 1)
                dve.tensor_scalar(diagD[:, :], con["ident"], dpar, None, ALU.mult).then_inc(S.own, 1)
                dve.wait_ge(S.ex, 1)
                dve.tensor_scalar(A16[:, :], A16[:, :], -0.5 / (8.0 + 1e-8), None, ALU.mult).then_inc(S.own, 1)

        w = dict(W_dtT=wdt, b_dt=bdt, WB_rep=WBr, WC_rep=WCr, A16=A16[:, :], diagD=diagD[:, :])
        xnT, dt, dtx = (sb(f"s0_{n}", [P, COLS0]) for n in ("xnT", "dt", "dtx"))
        y = sb("s0_y", [P, BATCH, CHUNKS * STEPS])
        stage0_project(nc, xn_tok, w, con, xnT, dt, dtx)
        stage0_scan(nc, w, con, xnT, dt, dtx, y)
        stage0_output(nc, y, con, y_tok)



LAYERS, HEADS, DH, WINDOW = 2, 8, 64, 64
PAIRS = HEADS // 2
HIDDEN = int(D * 4 * 2 / 3)
KH = -(-HIDDEN // P)
W1C = 2 * KH * P
UPC = W1C + 2 * KH + 2
MASKED = -1e30
TINY = 1e-30
LN_EXP_SET = 6
USES = 18
FIRST_USE = (0, 4, 8, 14)

DOWN_LAST, WO_TAIL, NORMED_TAIL, UP_TAIL, DOWN_TAIL = 15, 14, 17, (16, 19, 18), 21


def slot(n, u):
    return u % 2, n * (USES // 2) + (u // 2 + 1 + u % 2)


def layer_turns(eng, turn):
    turn(0)
    with eng.Fori(1, BATCH - 1) as n:
        turn(n)
    turn(BATCH - 1)


def stage1(nc, z, con, dram):
    with ExitStack() as ctx:
        sb = lambda n, s, t=F32: ctx.enter_context(nc.sbuf_tensor(f"s1_{n}", s, t))
        S = semaphores(nc, ctx, "w1", "load prep tab")
        wqk = sb("wqk", [P, LAYERS, PAIRS, 4, P])
        wv = sb("wv", [P, LAYERS, PAIRS, P])
        wo = sb("wo", [P, LAYERS, PAIRS, D])
        w2 = sb("w2", [P, LAYERS, KH, D])
        b2 = sb("b2", [1, LAYERS, D])
        up = sb("up", [P, LAYERS, UPC])
        base = sb("rot_base", [P, 4, SEQ])
        gain = sb("qk_gain", [P, LAYERS, 4])
        tab = sb("rot_tab", [P, LAYERS, 4, SEQ])
        mask_f = sb("mask_f", [P, TILES * P])
        mask = sb("mask", [P, TILES * P], BF16)
        ident16 = sb("ident16", [P, P], BF16)
        tiny = sb("tiny", [P, 1])
        pair = sb("pair", [P, 2])
        pair_ones = sb("pair_ones", [P, P])
        hT = sb("hT", [P, SEQ + 1])
        ft = sb("ft", [P, TILES, D])
        v_skew = sb("v_skew", [P, 2, TILES, P])
        with nc.Block() as block:
            @block.sync
            def _(sp):
                for dst, name in ((base, "rot_base"), (gain, "qk_gain"), (mask_f, "mask"), (wqk, "wqk"), (wv, "wv"),
                                  (wo, "wo"), (w2, "w2"), (b2, "b2"), (up, "up")):
                    sp.dma_start(dst[tuple([slice(None)] * len(dst.shape))], dram[name]).then_inc(S.load, 16)
                sp.wait_ge(S.load, 9 * 16)

            @block.vector
            def _(dve):
                dve.memset(hT[:, 0:1], 0.0).then_inc(S.prep, 1)
                dve.memset(ft[0:1, 0, D // 2:D], 0.0).then_inc(S.prep, 1)
                dve.memset(v_skew[64:128, :, 0, :], 0.0).then_inc(S.prep, 1)
                dve.memset(tiny[:, :], TINY).then_inc(S.prep, 1)
                for h in range(2):
                    dve.memset(pair[h * DH:(h + 1) * DH, h:h + 1], 1.0).then_inc(S.prep, 1)
                    dve.memset(pair[h * DH:(h + 1) * DH, 1 - h:2 - h], 0.0).then_inc(S.prep, 1)
                    for g in range(2):
                        dve.memset(pair_ones[h * DH:(h + 1) * DH, g * DH:(g + 1) * DH], float(h == g)).then_inc(S.prep, 1)
                dve.wait_ge(S.load, 9 * 16)
                dve.tensor_copy(mask[:, :], mask_f[:, :]).then_inc(S.prep, 1)
                dve.tensor_copy(ident16[:, :], con["ident"]).then_inc(S.prep, 1)
                for l in range(LAYERS):
                    for i in range(4):
                        dve.tensor_scalar(tab[:, l, i, :], base[:, i, :], gain[:, l, i:i + 1], None,
                                          ALU.mult).then_inc(S.tab, 1)
        for l in range(LAYERS):
            weights = dict(wqk=wqk[:, l, :, :, :], wv=wv[:, l, :, :], wo=wo[:, l, :, :], w2=w2[:, l, :, :], b2=b2[:, l, :],
                           up=up[:, l, :], tab=tab[:, l, :, :], mask=mask, ident16=ident16, tiny=tiny, pair_ones=pair_ones, pair=pair,
                           hT=hT, ft=ft, v_skew=v_skew)
            stage1_layer(nc, f"l{l}", z, con, weights)


def stage1_layer(nc, tag, z, con, w):
    with ExitStack() as ctx:
        sb = lambda n, s, t=F32: ctx.enter_context(nc.sbuf_tensor(f"{tag}_{n}", s, t))
        pb = lambda n, s: ctx.enter_context(nc.psum_tensor(f"{tag}_{n}", s, F32))
        S = semaphores(nc, ctx, tag, "own zb zT hT hT_half free0 free1 proj vps sq ss ln rn rotC rotS sum tn v "
                  "sim0 sim1 max0 max1 exp0 exp1 rin0 rin1 pn0 pn1 pt0 pt1 PT0 PT1 av oT wo z_att shift fst fvar frs fn "
                  "fnt fnT up gelu hid down z_ffn skew0 skew1 clip mraw gate value")
        hT, ft, up, tab, v_skew = w["hT"], w["ft"], w["up"], w["tab"], w["v_skew"]
        zb = sb("zb", [P, TILES, D])
        sq, rk = sb("sq", [P, 2, SEQ]), sb("rk", [P, SEQ])
        rq, rqc = sb("rq", [P, 2 * TILES]), sb("rqc", [P, TILES, 2])
        rc, rs = sb("rc", [P, 2, SEQ]), sb("rs", [P, 2, SEQ])
        qkT = sb("qkT", [P, 2, SEQ])
        v = sb("v", [P, 2, TILES, P])
        mraw, nmax, rsum, rinv = (sb(n, [P, 2, TILES]) for n in ("mraw", "nmax", "rsum", "rinv"))
        prob = sb("prob", [P, 2, TILES, P])
        probT = sb("probT", [P, 2, SEQ])
        oT = sb("oT", [P, PAIRS, SEQ])
        fstats = sb("fstats", [P, TILES, 6])
        fmean, fdiff, frstd = (sb(n, [P, TILES]) for n in ("fmean", "fdiff", "frstd"))
        fn, fnT = sb("fn", [P, TILES, D]), sb("fnT", [P, SEQ])
        gl, hid = sb("gl", [P, KH, SEQ]), sb("hid", [P, KH, SEQ])
        psX = pb("psX", [P, 2, 2, 512])
        psN = pb("psN", [P, 512])
        psS = pb("psS", [P, 2, 512])
        psT = pb("psT", [P, 512])
        block = ctx.enter_context(nc.Block())
        free, skew = (S.free0, S.free1), (S.skew0, S.skew1)
        sim, mx, ex, rin, pn, pt, PT = ((S.sim0, S.sim1), (S.max0, S.max1), (S.exp0, S.exp1), (S.rin0, S.rin1),
                                        (S.pn0, S.pn1), (S.pt0, S.pt1), (S.PT0, S.PT1))
        is_first, is_last = (lambda n: is_at(n, 0)), (lambda n: is_at(n, BATCH - 1))
        rows = lambda t, s: t[:, bass.ds(s * TILES, TILES), :]

        @block.sync
        def _(sp):
            sp.dma_start(zb[:, :, :], rows(z, 0)).then_inc(S.zb, 16)

            def turn(n):
                if not is_last(n):
                    ahead = (n + 1) * TILES if isinstance(n, int) else sp.snap((n + 1) * TILES, min_val=0, max_val=NT - TILES)
                    sp.wait_ge(S.zT, n + 1)
                    sp.dma_start(zb[:, :, :], z[:, bass.ds(ahead, TILES), :]).then_inc(S.zb, 16)
                if not is_first(n):
                    shift_tokens(n - 1)
                for hp in range(PAIRS):
                    if not (is_last(n) and hp == PAIRS - 1):
                        skew_v(n * PAIRS + (hp + 1), (hp + 1) % 2)

            def shift_tokens(s):
                tile = s * TILES if isinstance(s, int) else sp.snap(s * TILES, min_val=0, max_val=NT - TILES)
                h = D // 2
                sp.wait_ge(S.z_att, s + 1)
                sp.dma_start(ft[:, :, 0:h], z[:, bass.ds(tile, TILES), 0:h]).then_inc(S.shift, 16)
                sp.dma_start(ft[1:P, :, h:D], z[0:P - 1, bass.ds(tile, TILES), h:D]).then_inc(S.shift, 16)
                sp.dma_start(ft[0:1, 1:TILES, h:D], z[P - 1:P, bass.ds(tile, TILES - 1), h:D]).then_inc(S.shift, 16)

            def skew_v(k, q):
                sp.wait_ge(S.v, k + 1)
                sp.dma_start(v_skew[0:64, q, :, :], v[0:64, q, :, :]).then_inc(skew[q], 16)
                sp.dma_start(v_skew[64:128, q, 1:TILES, :], v[64:128, q, 0:TILES - 1, :]).then_inc(skew[q], 16)

            skew_v(0, 0)
            layer_turns(sp, turn)
            shift_tokens(BATCH - 1)

        @block.tensor
        def _(pe):
            def transposes(bank, src):
                for j in range(TILES):
                    last = pe.transpose(bank[:, j * P:(j + 1) * P], src(j), con["ident"])
                return last

            def take(n, u):
                s, before = slot(n, u)
                pe.wait_ge(free[s], before + 1)
                return psX[:, s, :, :]

            def absent(n, u):
                take(n, u)
                pe.nop().then_inc(free[slot(n, u)[0]], 1)

            def transpose_z(n):
                if is_at(n, 0):
                    pe.wait_ge(S.zb, 16)
                else:
                    pe.wait_ge(S.ln, 8 * n + 1)
                    pe.wait_ge(S.zb, n * 16 + 16)
                transposes(psN, lambda j: zb[:, j, :]).then_inc(S.zT, 1)

            def project(n, u, k, hp, c):
                ps = take(n, u)
                for i in range(2):
                    last = pe.matmul(ps[:, i, :], w["wqk"][:, hp, 2 * c + i, :], hT[:, 0:SEQ], start=True, stop=True)
                last.then_inc(S.proj, 1)

            def project_v(n, u, k, hp):
                ps = take(n, u)
                for j in range(TILES):
                    last = pe.matmul(ps[:, 0, j * P:(j + 1) * P], hT[:, j * P:(j + 1) * P], w["wv"][:, hp, :],
                                     start=True, stop=True)
                last.then_inc(S.vps, 1)

            def sum_squares(k, c):
                pe.wait_ge(S.sq, 2 * k + (c + 1))
                pe.wait_ge(S.ln, 2 * k + (c + 1))
                if c == 0:
                    for j in range(TILES):
                        last = pe.matmul(psN[:, 2 * j:2 * j + 2], sq[:, 0, j * P:(j + 1) * P], w["pair"][:, :],
                                         start=True, stop=True, skip_group_check=True)
                else:
                    last = pe.matmul(psN[:, :], w["pair_ones"][:, :], sq[:, 1, :], start=True, stop=True)
                last.then_inc(S.ss, 1)

            def scores(k, h):
                pe.wait_ge(ex[h], k + 1)
                pe.matmul(psS[:, h, :], w["ident16"][:, :], w["mask"][:, :], start=True, stop=False, skip_group_check=True)
                r = slice(h * DH, (h + 1) * DH)
                for j in range(TILES):
                    o, m = j * P, j * P + WINDOW
                    pe.matmul(psS[0:64, h, o:m], qkT[r, 0, o:m], qkT[r, 1, o:m], start=False, stop=True, skip_group_check=True)
                    if j > 0:
                        pe.matmul(psS[0:64, h, m:o + P], qkT[r, 0, o:m], qkT[r, 1, o - WINDOW:o],
                                  start=False, stop=True, skip_group_check=True)
                    last = pe.matmul(psS[64:128, h, o:o + P], qkT[r, 0, m:o + P], qkT[r, 1, o:o + P],
                                     start=False, stop=True, skip_group_check=True)
                last.then_inc(sim[h], 1)

            def transpose_probabilities(k, h):
                pe.wait_ge(pn[h], k + 1)
                if h == 0:
                    pe.wait_ge(S.oT, k + 1)
                else:
                    pe.wait_ge(PT[0], k + 1)
                transposes(psT, lambda j: prob[:, h, j, :]).then_inc(pt[h], 1)

            def outputs(n, k, hp):
                pe.wait_ge(PT[1], k + 1)
                pe.wait_ge(skew[hp % 2], n * 64 + (hp // 2 + 1) * 32)
                for h in range(2):
                    r = slice(h * DH, (h + 1) * DH)
                    for j in range(TILES):
                        for odd in range(2):
                            o = j * P + odd * WINDOW
                            last = pe.matmul(psT[r, o:o + WINDOW], (v, v_skew)[1 - odd][:, hp % 2, j, r], probT[:, h, o:o + WINDOW],
                                             start=True, stop=True, skip_group_check=True)
                last.then_inc(S.av, 1)

            def project_out(n, u, s):
                ps = take(n, u)
                pe.wait_ge(S.oT, s * PAIRS + (PAIRS + 1))
                for j in range(TILES):
                    for hp in range(PAIRS):
                        last = pe.matmul(ps[:, 0, j * P:(j + 1) * P], oT[:, hp, j * P:(j + 1) * P], w["wo"][:, hp, :],
                                         start=hp == 0, stop=hp == PAIRS - 1)
                last.then_inc(S.wo, 1)

            def transpose_normed(n, u, s):
                ps = take(n, u)
                pe.wait_ge(S.fn, s + 1)
                transposes(ps[:, 0, :], lambda j: fn[:, j, :]).then_inc(S.fnt, 1)

            def up_chunk(n, u, s, c):
                ps = take(n, u)
                pe.wait_ge(S.fnT, s + 1)
                for g in range(2):
                    o = (g * KH + c) * P
                    last = pe.matmul(ps[:, g, :], up[:, o:o + P], fnT[:, :], start=True, stop=True)
                last.then_inc(S.up, 1)

            def down(n, u, s):
                ps = take(n, u)
                pe.wait_ge(S.hid, s + 1)
                for j in range(TILES):
                    o = ps[:, 0, j * P:(j + 1) * P]
                    for c in range(KH):
                        pe.matmul(o, hid[:, c, j * P:(j + 1) * P], w["w2"][:, c, :], start=c == 0, stop=False)
                    last = pe.matmul(o, con["ones"][0:1, :], w["b2"], start=False, stop=True)
                last.then_inc(S.down, 1)

            def body(n, hp):
                k = n * PAIRS + hp
                u = FIRST_USE[hp]
                ffn = (lambda f, u, *a: absent(n, u)) if is_first(n) else (lambda f, u, *a: f(n, u, n - 1, *a))
                ahead = not (is_last(n) and hp == PAIRS - 1)
                nxt = (hp + 1) % PAIRS
                extra = (1, 0, 1, 0)[hp]
                if ahead:
                    if nxt == 0:
                        pe.wait_ge(S.hT, n + 2)
                    project(n, u, k + 1, nxt, 0)
                pe.wait_ge(S.tn, k + 1)
                scores(k, 0)
                scores(k, 1)
                if hp == 0:
                    ffn(project_out, u + 1)
                if hp == 2:
                    ffn(up_chunk, u + 1, 0)
                if ahead:
                    project(n, u + extra + 1, k + 1, nxt, 1)
                    sum_squares(k + 1, 0)
                    project_v(n, u + extra + 2, k + 1, nxt)
                    sum_squares(k + 1, 1)
                transpose_probabilities(k, 0)
                if hp == 2:
                    ffn(up_chunk, u + 4, 1)
                    if not is_last(n):
                        transpose_z(n + 1)
                transpose_probabilities(k, 1)
                if hp == 2:
                    ffn(up_chunk, u + 5, 2)
                outputs(n, k, hp)
                if hp == 1:
                    ffn(transpose_normed, u + 3)
                if hp == 3:
                    ffn(down, DOWN_LAST if is_last(n) else u + 3)

            def turn(n):
                for hp in range(PAIRS):
                    body(n, hp)

            transpose_z(0)
            pe.wait_ge(S.hT, 1)
            project(0, -3, 0, 0, 0)
            project(0, -2, 0, 0, 1)
            sum_squares(0, 0)
            project_v(0, -1, 0, 0)
            sum_squares(0, 1)
            layer_turns(pe, turn)
            n, s = BATCH - 1, BATCH - 1
            project_out(n, WO_TAIL, s)
            transpose_normed(n, NORMED_TAIL, s)
            for c in range(KH):
                up_chunk(n, UP_TAIL[c], s, c)
            down(n, DOWN_TAIL, s)

        @block.scalar
        def _(act):
            def load_functions():
                act.add_instruction(mybir.InstLoadActFuncSet(name=nc.get_next_instruction_name(), act_func_set_id=LN_EXP_SET,
                                                             engine=mybir.EngineType.Activation, ins=[], outs=[]))

            def square(n, u, k, c):
                act.wait_ge(S.proj, 2 * k + (c + 1))
                act.activation(sq[:, c, :], psX[:, slot(n, u)[0], 0, :], ACT.Square).then_inc(S.sq, 1)

            def inverse_norm(k, c):
                act.wait_ge(S.ss, 2 * k + (c + 1))
                r, n = (rq[:, :], 2 * TILES) if c == 0 else (rk[:, :], SEQ)
                act.activation(r, psN[:, 0:n], ACT.Ln, bias=w["tiny"][:, :]).then_inc(S.ln, 1)
                act.wait_ge(S.ln, 2 * k + (c + 2))
                act.activation(r, r, ACT.Exp, scale=-0.5).then_inc(S.rn, 1)

            def exponentials(k, h):
                act.wait_ge(mx[h], k + 1)
                for j in range(TILES):
                    last = act.activation(prob[:, h, j, :], psS[:, h, j * P:(j + 1) * P], ACT.Exp,
                                          bias=nmax[:, h, j:j + 1], scale=rqc[:, j, h:h + 1], accum_out=rsum[:, h, j:j + 1])
                last.then_inc(ex[h], 1)

            def copy_probabilities(k, h):
                act.wait_ge(pt[h], k + 1)
                act.copy(probT[:, h, :], psT[:, :]).then_inc(PT[h], 1)

            def copy_z(n):
                act.wait_ge(S.zT, n + 1)
                act.copy(hT[0:64, 0:SEQ], psN[0:64, :]).then_inc(S.hT_half, 1)
                act.copy(hT[64:128, 1:1 + SEQ], psN[64:128, :]).then_inc(S.hT, 1)

            def gate_chunk(n, u, s, c):
                act.wait_ge(S.up, s * KH + (c + 1))
                if c == 0 and not is_at(s, 0):
                    act.wait_ge(S.hid, s)
                act.activation(gl[:, c, :], psX[:, slot(n, u)[0], 1, :], ACT.Identity,
                               bias=up[:, W1C + KH + c:W1C + KH + c + 1]).then_inc(S.gate, 1)

            def gelu(s):
                act.wait_ge(S.gate, s * KH + KH)
                act.activation(gl[:, :, :], gl[:, :, :], ACT.Gelu).then_inc(S.gelu, 1)
                load_functions()

            def scale_normed(n, u, s):
                sl = slot(n, u)[0]
                act.wait_ge(S.fnt, s + 1)
                act.activation(fnT[:, :], psX[:, sl, 0, :], ACT.Identity, bias=up[:, UPC - 1:UPC],
                               scale=up[:, UPC - 2:UPC - 1]).then_inc(S.fnT, 1)
                act.wait_ge(S.fnT, s + 1)
                act.nop().then_inc(free[sl], 1)

            def body(n, hp):
                k = n * PAIRS + hp
                u, extra = FIRST_USE[hp], (1, 0, 1, 0)[hp]
                ahead = not (is_last(n) and hp == PAIRS - 1)
                ffn = not is_first(n)
                if ahead:
                    square(n, u, k + 1, 0)
                if hp == 3 and ffn:
                    gelu(n - 1)
                exponentials(k, 0)
                if hp == 2 and ffn:
                    gate_chunk(n, u + 1, n - 1, 0)
                if ahead:
                    square(n, u + extra + 1, k + 1, 1)
                exponentials(k, 1)
                if ahead:
                    inverse_norm(k + 1, 0)
                    inverse_norm(k + 1, 1)
                copy_probabilities(k, 0)
                if hp == 2 and ffn:
                    gate_chunk(n, u + 4, n - 1, 1)
                if hp == 2 and not is_last(n):
                    act.wait_ge(S.vps, k + 2)
                    copy_z(n + 1)
                copy_probabilities(k, 1)
                if hp == 2 and ffn:
                    gate_chunk(n, u + 5, n - 1, 2)
                act.wait_ge(S.av, k + 1)
                if hp == 0 and ffn:
                    act.wait_ge(S.wo, n)
                act.copy(oT[:, hp, :], psT[:, :]).then_inc(S.oT, 1)
                if hp == 1 and ffn:
                    scale_normed(n, u + 3, n - 1)

            def turn(n):
                for hp in range(PAIRS):
                    body(n, hp)

            lead(act, S.ln, 1)
            lead(act, S.exp0, 1)
            lead(act, S.exp1, 1)
            lead(act, S.oT, 1)
            load_functions()
            copy_z(0)
            square(0, -3, 0, 0)
            square(0, -2, 0, 1)
            inverse_norm(0, 0)
            inverse_norm(0, 1)
            layer_turns(act, turn)
            n, s = BATCH - 1, BATCH - 1
            scale_normed(n, NORMED_TAIL, s)
            for c in range(KH):
                gate_chunk(n, UP_TAIL[c], s, c)
            gelu(s)

        @block.gpsimd
        def _(pool):
            def add_rotated(k, c):
                pool.wait_ge(S.rotC, 2 * k + (c + 1))
                pool.wait_ge(S.rotS, 2 * k + (c + 1))
                if c == 0 and not is_at(k, 0):
                    pool.wait_ge(sim[1], k)
                pool.tensor_tensor((qkT if c == 0 else rc)[:, c, :], rc[:, c, :], rs[:, c, :], ALU.add).then_inc(S.sum, 1)

            def scale_probabilities(k, h):
                pool.wait_ge(rin[h], k + 1)
                pool.tensor_tensor(prob[:, h, :, :], prob[:, h, :, :], spread(rinv[:, h, :], 2, P),
                                   ALU.mult).then_inc(pn[h], 1)

            def turn(n):
                for hp in range(PAIRS):
                    k = n * PAIRS + hp
                    ahead = not (is_last(n) and hp == PAIRS - 1)
                    if ahead:
                        add_rotated(k + 1, 0)
                    scale_probabilities(k, 0)
                    if ahead:
                        add_rotated(k + 1, 1)
                    scale_probabilities(k, 1)
                    if hp == 0 and not is_first(n):
                        root(n - 1)

            def root(s):
                pool.wait_ge(S.fvar, s + 1)
                pool.tensor_tensor(frstd[:, :], frstd[:, :], con["mhalf"][:, 0:TILES], ALU.pow).then_inc(S.frs, 1)

            add_rotated(0, 0)
            add_rotated(0, 1)
            layer_turns(pool, turn)
            root(BATCH - 1)

        @block.vector
        def _(dve):
            own = Order(dve, S.own, MOMENTS)

            def rotate(n, u, k, c):
                s, before = slot(n, u)
                dve.wait_ge(S.sq, 2 * k + (c + 1))
                dve.tensor_tensor(rc[:, c, :], psX[:, s, 0, :], tab[:, 2 * c, :], ALU.mult).then_inc(S.rotC, 1)
                dve.tensor_tensor(rs[:, c, :], psX[:, s, 1, :], tab[:, 2 * c + 1, :], ALU.mult).then_inc(S.rotS, 1)
                dve.wait_ge(S.rotC, 2 * k + (c + 1))
                dve.wait_ge(S.rotS, 2 * k + (c + 1))
                dve.nop().then_inc(free[s], 1)

            def clip_q(k):
                dve.wait_ge(S.rn, 2 * k + 1)
                step(dve, dve.tensor_scalar(rqc[:, :, :], rq[:, :].rearrange("p (j h) -> p j h", h=2), 1e12, None, ALU.min),
                     S.clip, k + 1)

            def norm_k(k):
                dve.wait_ge(S.rn, 2 * k + 2)
                dve.wait_ge(S.sum, 2 * k + 2)
                step(dve, dve.scalar_tensor_tensor(out=qkT[:, 1, :], in0=rk[:, :], scalar=1e12, in1=rc[:, 1, :],
                                                   op0=ALU.min, op1=ALU.mult), S.tn, k + 1)

            def copy_v(n, u, k, hp):
                s, before = slot(n, u)
                dve.wait_ge(S.vps, k + 1)
                if not is_at(k, 1):
                    dve.wait_ge(S.av, k - 1)
                dve.tensor_copy(v[:, hp % 2, :, :].rearrange("p j f -> p (j f)"), psX[:, s, 0, :]).then_inc(S.v, 1)
                dve.wait_ge(S.v, k + 1)
                dve.nop().then_inc(free[s], 1)

            def row_max(k, h):
                dve.wait_ge(sim[h], k + 1)
                step(dve, dve.tensor_reduce(mraw[:, h, :], psS[:, h, :].rearrange("p (j c) -> p j c", j=TILES), AX.X,
                                            ALU.max, negate=True), S.mraw, 2 * k + (h + 1))
                dve.tensor_tensor(nmax[:, h, :], mraw[:, h, :], rqc[:, :, h], ALU.mult).then_inc(mx[h], 1)

            def invert(k, h):
                dve.wait_ge(ex[h], k + 2)
                dve.reciprocal(rinv[:, h, :], rsum[:, h, :]).then_inc(rin[h], 1)

            def add_to_z(n, u, s, made, sem):
                sl = slot(n, u)[0]
                dve.wait_ge(made, s + 1)
                step(dve, dve.tensor_tensor(rows(z, s), rows(z, s), psX[:, sl, 0, :].rearrange("p (j d) -> p j d", j=TILES),
                                            ALU.add), sem, s + 1)
                dve.nop().then_inc(free[sl], 1)

            def statistics(s):
                own.start(s)
                dve.wait_ge(S.shift, s * 48 + 48)
                for j in range(TILES):
                    dve.bn_stats(fstats[:, j, :], ft[:, j, :]).then_inc(S.fst, 1)
                dve.wait_ge(S.fst, s * TILES + TILES)
                moments(dve, own, fstats, fmean, fdiff, frstd)
                dve.tensor_scalar(frstd[:, :], frstd[:, :], EPS, None, ALU.add).then_inc(S.fvar, 1)
                own.end()

            def norm(s):
                dve.wait_ge(S.frs, s + 1)
                for j in range(TILES):
                    last = dve.tensor_scalar(fn[:, j, :], ft[:, j, :], fmean[:, j:j + 1], frstd[:, j:j + 1],
                                             ALU.subtract, ALU.mult)
                last.then_inc(S.fn, 1)

            def value_chunk(n, u, s, c):
                sl = slot(n, u)[0]
                dve.wait_ge(S.gate, s * KH + (c + 1))
                if c == 0 and not is_at(s, 0):
                    dve.wait_ge(S.down, s)
                step(dve, dve.tensor_scalar(hid[:, c, :], psX[:, sl, 0, :], up[:, W1C + c:W1C + c + 1], None, ALU.add),
                     S.value, s * KH + (c + 1))
                dve.nop().then_inc(free[sl], 1)

            def apply_gates(s):
                dve.wait_ge(S.gelu, s + 1)
                dve.tensor_tensor(hid[:, :, :], hid[:, :, :], gl[:, :, :], ALU.mult).then_inc(S.hid, 1)

            def body(n, hp):
                k = n * PAIRS + hp
                u, extra = FIRST_USE[hp], (1, 0, 1, 0)[hp]
                ahead = not (is_last(n) and hp == PAIRS - 1)
                ffn = not is_first(n)
                if ahead:
                    rotate(n, u, k + 1, 0)
                row_max(k, 0)
                row_max(k, 1)
                if hp == 0 and ffn:
                    add_to_z(n, u + 1, n - 1, S.wo, S.z_att)
                invert(k, 0)
                if hp == 2 and ffn:
                    value_chunk(n, u + 1, n - 1, 0)
                if ahead:
                    rotate(n, u + extra + 1, k + 1, 1)
                invert(k, 1)
                if hp == 3 and ffn:
                    apply_gates(n - 1)
                if ahead:
                    copy_v(n, u + extra + 2, k + 1, (hp + 1) % PAIRS)
                if hp == 0 and ffn:
                    statistics(n - 1)
                if hp == 1 and ffn:
                    norm(n - 1)
                if ahead:
                    clip_q(k + 1)
                    norm_k(k + 1)
                if hp == 2 and ffn:
                    value_chunk(n, u + 4, n - 1, 1)
                    value_chunk(n, u + 5, n - 1, 2)
                if hp == 3 and ffn:
                    add_to_z(n, DOWN_LAST if is_last(n) else u + 3, n - 1, S.down, S.z_ffn)

            def turn(n):
                for hp in range(PAIRS):
                    body(n, hp)

            lead(dve, S.free0, 1)
            lead(dve, S.free1, 1)
            rotate(0, -3, 0, 0)
            rotate(0, -2, 0, 1)
            clip_q(0)
            dve.wait_ge(S.vps, 1)
            dve.tensor_copy(v[:, 0, :, :].rearrange("p j f -> p (j f)"), psX[:, 1, 0, :]).then_inc(S.v, 1)
            dve.wait_ge(S.v, 1)
            dve.nop().then_inc(free[1], 1)
            norm_k(0)
            layer_turns(dve, turn)
            n, s = BATCH - 1, BATCH - 1
            add_to_z(n, WO_TAIL, s, S.wo, S.z_att)
            statistics(s)
            norm(s)
            for c in range(KH):
                value_chunk(n, UP_TAIL[c], s, c)
            apply_gates(s)
            add_to_z(n, DOWN_TAIL, s, S.down, S.z_ffn)


def layout1(a, np):
    f = np.float32
    pad = lambda w, n: np.concatenate([w, np.zeros(w.shape[:-1] + (n - w.shape[-1],), f)], -1)
    two = lambda w: np.concatenate([pad(w[..., :HIDDEN], KH * P), pad(w[..., HIDDEN:], KH * P)], -1)
    w1, b1 = two(a["L0_ffn_w1"]), two(a["L0_ffn_b1"])
    w2 = np.concatenate([a["L0_ffn_w2"], np.zeros((LAYERS, KH * P - HIDDEN, D), f)], 1)
    half = np.arange(0, DH, 2, dtype=f)
    inv = (1.0 / 10000.0 ** (half / f(DH))).astype(f)
    t = np.arange(SEQ, dtype=f)
    freqs = t[:, None] * inv[None, :]
    base = ((half + f(0.4 * DH)) / f(1.4 * DH)).astype(f)
    decay = base[None, :] ** ((t - SEQ // 2) / f(WINDOW // 2))[:, None]
    freqs, decay = np.concatenate([freqs, freqs], 1), np.concatenate([decay, decay], 1)
    sign = np.concatenate([-np.ones(DH // 2, f), np.ones(DH // 2, f)])
    cos, sin = np.cos(freqs), np.sin(freqs) * sign
    tab = np.stack([cos * decay * 8, sin * decay * 8, cos / decay, sin / decay]).astype(f)
    tab = np.concatenate([tab, tab], -1).transpose(2, 0, 1)
    gain = np.stack([a["L0_ffn_q_scale"], a["L0_ffn_k_scale"]], 1)
    gain = np.stack([gain, np.roll(gain, DH // 2, -1)], 2).reshape(LAYERS, 4, DH)
    gain = np.concatenate([gain, gain], -1).transpose(2, 0, 1)
    i, c = np.arange(P)[:, None] % WINDOW, np.arange(P)[None, :] % WINDOW
    own = (np.arange(P)[:, None] < WINDOW) == (np.arange(P)[None, :] < WINDOW)
    mask = np.tile(np.where(np.where(own, c <= i, c >= i), 0, MASKED).astype(f), (1, TILES))
    mask[:WINDOW, WINDOW:P] = MASKED
    wqkv = a["L0_ffn_wqkv"].reshape(LAYERS, D, 3, HEADS, DH)
    qk = np.stack([wqkv[:, :, 0:2], np.roll(wqkv[:, :, 0:2], DH // 2, -1)], 3)
    qk = qk.reshape(LAYERS, D, 4, PAIRS, P).transpose(1, 0, 3, 2, 4)
    return {
        "wqk": qk,
        "wv": wqkv[:, :, 2].reshape(LAYERS, D, PAIRS, P).transpose(1, 0, 2, 3),
        "wo": a["L0_ffn_wo"].reshape(LAYERS, PAIRS, P, D).transpose(2, 0, 1, 3),
        "w2": w2.reshape(LAYERS, KH, P, D).transpose(2, 0, 1, 3),
        "b2": a["L0_ffn_b2"][None],
        "up": np.concatenate([w1.transpose(1, 0, 2), b1.reshape(LAYERS, 2 * KH, P).transpose(2, 0, 1),
                              a["L0_ffn_ln_g"].T[:, :, None], a["L0_ffn_ln_b"].T[:, :, None]], 2),
        "rot_base": tab,
        "qk_gain": gain,
        "mask": mask,
    }


INNER, SSTATE, SHEADS, HD, TAPS = 2 * D, 64, 4, 64, 4
GROUPS2 = 4


def sequence_turns(eng, turn):
    turn(0, 0)
    with eng.Fori(0, (BATCH - 2) // 2) as i:
        turn(2 * i + 1, 1)
        turn(2 * i + 2, 0)
    turn(BATCH - 1, 1)


def stage2(nc, xn_tok, y_tok, con, dram):
    with ExitStack() as ctx:
        sb = lambda n, s: ctx.enter_context(nc.sbuf_tensor(f"s2_{n}", s, F32))
        S = semaphores(nc, ctx, "s2", "load prep xin0 xin1 xt xT dtp u absu ex ln dt a prod evac taps conv silu "
                  "xtok Xdt Btok R seg cum G E dec Gm M Cdec Xs Y St decayed state skip yg sqr ms rv rs out y")
        WC = 2 * INNER + 2 * SSTATE + SHEADS
        win = sb("win", [P, WC])
        small = sb("small", [P, GROUPS2 * (TAPS + 1) + 2 * SHEADS + 2 + 2])
        cw = small[:, 0:GROUPS2 * (TAPS + 1)].rearrange("p (g t) -> p g t", g=GROUPS2)
        o = GROUPS2 * (TAPS + 1)
        dt_bias, Alog, Dcol, norm_w = (small[:, o:o + 4], small[:, o + 4:o + 8], small[:, o + 8:o + 10], small[:, o + 10:o + 12])
        wout = sb("wout", [P, 2, D])
        tri, strict = sb("tri", [P, P]), sb("strict", [P, P])
        A = sb("A", [P, SHEADS])
        xin = sb("xin", [P, 2, TILES, D])
        xT = sb("xT", [P, SEQ])
        craw = sb("craw", [P, GROUPS2, TAPS - 1 + SEQ])
        acc = sb("acc", [P, GROUPS2, SEQ])
        xc = sb("xc", [P, 2, GROUPS2, SEQ])
        zs = sb("zs", [P, 2, 2, SEQ])
        u, au = sb("u", [P, TILES, SHEADS]), sb("au", [P, TILES, SHEADS])
        dt, a = sb("dt", [P, 2, TILES, SHEADS]), sb("a", [P, 2, TILES, SHEADS])
        Xdt, Xs = sb("Xdt", [P, SHEADS, HD]), sb("Xs", [P, SHEADS, HD])
        Btok = sb("Btok", [P, SSTATE])
        R, E, M = (sb(n, [P, SHEADS, P]) for n in ("R", "E", "M"))
        Gm = sb("Gm", [P, P])
        dec, Cdec = sb("dec", [64, SHEADS, P]), sb("Cdec", [64, SHEADS, P])
        state = sb("state", [64, 2, SHEADS, HD])
        yg, ysq = sb("yg", [P, 2, SEQ]), sb("ysq", [P, 2, SEQ])
        rs = sb("rs", [P, TILES])

        with nc.Block() as block:
            @block.sync
            def _(sp):
                for dst, name in ((win[:, :], "m_in"), (small[:, :], "m_small"), (wout[:, :, :], "m_out"),
                                  (tri[:, :], "m_tri"), (strict[:, :], "m_strict")):
                    sp.dma_start(dst, dram[name]).then_inc(S.load, 16)

            @block.scalar
            def _(act):
                act.wait_ge(S.load, 5 * 16)
                act.activation(A[:, :], Alog, ACT.Exp).then_inc(S.prep, 1)

            @block.vector
            def _(dve):
                dve.memset(craw[:, :, 0:TAPS - 1], 0.0).then_inc(S.decayed, 1)
                dve.wait_ge(S.load, 5 * 16)
                for h in range(2):
                    dve.tensor_scalar(wout[:, h, :], wout[:, h, :], norm_w[:, h:h + 1], None, ALU.mult).then_inc(S.decayed, 1)
                dve.wait_ge(S.prep, 1)
                dve.tensor_scalar(A[:, :], A[:, :], -1.0, None, ALU.mult).then_inc(S.decayed, 1)

        pb = lambda n, s: ctx.enter_context(nc.psum_tensor(f"s2_{n}", s, F32))
        psA = pb("psA", [P, 2, 512])
        psX = pb("psX", [P, 512])
        psG = pb("psG", [P, 512])
        psE, psC = pb("psE", [P, 512]), pb("psC", [P, 512])
        psY = pb("psY", [P, 2, 512])
        ST0 = P
        psO = psE
        block = ctx.enter_context(nc.Block())
        PROD = [(2 * INNER, 64), (2 * INNER + SSTATE, 64), (INNER, P), (INNER + P, P), (0, P), (P, P)]
        rows = lambda g: slice(0, PROD[g][1])
        xins = S.xin0, S.xin1

        @block.sync
        def _(sp):
            with sp.Fori(0, BATCH // 2) as i:
                for q in range(2):
                    b = 2 * i + q
                    sp.wait_ge(S.y, b + 1)
                    sp.dma_start(xin[:, q, :, :], xn_tok[:, bass.ds(b * TILES, TILES), :]).then_inc(xins[q], 16)

        @block.tensor
        def _(pe):
            def front(b, q, half_b):
                pe.wait_ge(xins[q], half_b * 16 + 16)
                pe.wait_ge(S.evac, b * 6 + 1)
                for j in range(TILES):
                    last = pe.transpose(psA[:, 0, j * P:(j + 1) * P], xin[:, q, j, :], con["ident"])
                last.then_inc(S.xt, 1)
                pe.wait_ge(S.xT, b + 1)
                pe.wait_ge(S.evac, b * 6 + 2)
                for j in range(TILES):
                    last = pe.matmul(psA[:, 1, j * SHEADS:(j + 1) * SHEADS], xT[:, j * P:(j + 1) * P],
                                     win[:, WC - SHEADS:WC], start=True, stop=True, skip_group_check=True)
                last.then_inc(S.dtp, 1)
                for g, (col, m) in enumerate(PROD):
                    pe.wait_ge(S.evac, b * 6 + (g + 1))
                    if g == 1:
                        pe.wait_ge(S.u, b + 1)
                    pe.matmul(psA[0:m, g % 2, :], win[:, col:col + m], xT[:, :], start=True, stop=True).then_inc(S.prod, 1)

            def back(b, q):
                for c in range(TILES):
                    k = b * TILES + c
                    t = slice(c * P, (c + 1) * P)
                    if c == 0:
                        pe.wait_ge(S.silu, b * 4 + 8)
                    pe.wait_ge(S.Xdt, k + 1)
                    pe.wait_ge(S.Btok, k + 1)
                    for h in range(2):
                        pe.transpose(psX[:, h * P:(h + 1) * P], xc[:, q, 2 + h, t], con["ident"])
                    pe.transpose(psX[:, 2 * P:2 * P + SSTATE], xc[0:64, q, 0, t], con["ident"][0:64, 0:64]).then_inc(S.xtok, 1)
                    pe.wait_ge(S.state, k + 1)
                    pe.matmul(psG[:, 0:P], xc[0:64, q, 0, t], xc[0:64, q, 1, t], start=True, stop=True,
                              skip_group_check=True).then_inc(S.G, 1)
                    pe.wait_ge(S.R, k + 1)
                    pe.wait_ge(S.E, k + 1)
                    if c == 0:
                        pe.wait_ge(S.y, b + 2)
                    pe.matmul(psE[:, :], strict[:, :], R[:, :, :], start=True, stop=True).then_inc(S.seg, 1)
                    pe.wait_ge(S.dec, k + 1)
                    if c == 0:
                        pe.wait_ge(S.rv, b + 1)
                    pe.matmul(psC[0:64, :], con["ones"][:, 0:64], R[:, :, :], start=True, stop=True).then_inc(S.cum, 1)
                    if c < TILES - 1:
                        pe.wait_ge(S.Xs, k + 2)
                        pe.wait_ge(S.Btok, k + 2)
                        pe.matmul(psG[0:64, ST0:ST0 + SHEADS * HD], Btok[:, :], Xs[:, :, :], start=True, stop=True,
                                  skip_group_check=True).then_inc(S.St, 1)
                    else:
                        pe.nop().then_inc(S.St, 1)
                    pe.wait_ge(S.M, k + 1)
                    pe.wait_ge(S.Cdec, k + 2)
                    if c == 0:
                        pe.wait_ge(S.yg, b + 1)
                    for h in range(SHEADS):
                        out = psY[h % 2 * 64:h % 2 * 64 + 64, h // 2, t]
                        last = pe.matmul(out, Xdt[:, h, :], M[:, h, :], start=True, stop=c == 0, skip_group_check=True)
                        if c:
                            last = pe.matmul(out, state[:, (c - 1) % 2, h, :], Cdec[:, h, :], start=False, stop=True, skip_group_check=True)
                    last.then_inc(S.Y, 1)
                pe.wait_ge(S.sqr, b + 1)
                for j in range(TILES):
                    for h in range(2):
                        last = pe.matmul(psC[:, j:j + 1], ysq[:, h, j * P:(j + 1) * P], con["ones"][:, 0:1],
                                         start=h == 0, stop=h == 1, skip_group_check=True)
                last.then_inc(S.ms, 1)
                pe.wait_ge(S.E, b * TILES + TILES + 1)
                for j in range(TILES):
                    for h in range(2):
                        last = pe.matmul(psO[:, j * P:(j + 1) * P], yg[:, h, j * P:(j + 1) * P], wout[:, h, :],
                                         start=h == 0, stop=h == 1)
                last.then_inc(S.out, 1)

            def turn(b, q):
                if not is_at(b, BATCH - 1):
                    front(b + 1, 1 - q, (b + 1 - (1 - q)) // 2 if isinstance(b, int) else (b + q) >> 1)
                back(b, q)

            lead(pe, S.cum, 1)
            lead(pe, S.St, 1)
            lead(pe, S.Y, 1)
            front(0, 0, 0)
            sequence_turns(pe, turn)

        @block.scalar
        def _(act):
            def front(b, q):
                act.wait_ge(S.xt, b + 1)
                act.copy(xT[:, :], psA[:, 0, :]).then_inc(S.xT, 1)
                act.wait_ge(S.absu, b + 1)
                step(act, act.activation(au[:, :, :], au[:, :, :], ACT.Exp, scale=-1.0), S.ex, b + 1)
                act.activation(au[:, :, :], au[:, :, :], ACT.Ln, bias=1.0).then_inc(S.ln, 1)
                for g in range(6):
                    act.wait_ge(S.prod, b * 6 + (g + 1))
                    if g < GROUPS2:
                        act.copy(craw[rows(g), g, TAPS - 1:], psA[rows(g), g % 2, :]).then_inc(S.evac, 1)
                    else:
                        act.activation(zs[:, q, g - 4, :], psA[:, g % 2, :], ACT.Silu).then_inc(S.evac, 1)
                for g in range(GROUPS2):
                    act.wait_ge(S.conv, b * 4 + (g + 1))
                    act.activation(xc[rows(g), q, g, :], acc[rows(g), g, :], ACT.Silu).then_inc(S.silu, 1)

            def back(b, q):
                for c in range(TILES):
                    k = b * TILES + c
                    act.wait_ge(S.seg, k + 1)
                    act.wait_ge(S.Xs, k + 1)
                    act.activation(E[:, :, :], psE[:, :].rearrange("p (h i) -> p h i", h=SHEADS), ACT.Exp).then_inc(S.E, 1)
                    act.wait_ge(S.cum, k + 2)
                    act.wait_ge(S.Cdec, k + 1)
                    act.wait_ge(S.state, k + 1)
                    act.activation(dec[:, :, :], psC[0:64, :].rearrange("p (h i) -> p h i", h=SHEADS), ACT.Exp).then_inc(S.dec, 1)
                act.wait_ge(S.yg, b + 2)
                act.activation(ysq[:, :, :], yg[:, :, :], ACT.Square).then_inc(S.sqr, 1)

            lead(act, S.evac, 2)
            lead(act, S.E, 1)
            lead(act, S.dec, 1)
            lead(act, S.silu, 4)
            front(0, 0)
            sequence_turns(act, lambda b, q: (None if is_at(b, BATCH - 1) else front(b + 1, 1 - q), back(b, q)))

        @block.gpsimd
        def _(pool):
            def back(b, q):
                for c in range(TILES):
                    k = b * TILES + c
                    if c == 0:
                        pool.wait_ge(S.a, b + 1)
                        pool.wait_ge(S.silu, b * 4 + 8)
                    pool.wait_ge(S.cum, k + 1)
                    pool.tensor_tensor(R[:, :, :], spread(tri[:, :], 1, SHEADS), spread(a[:, q, c, :], 2, P),
                                       ALU.mult).then_inc(S.R, 1)
                    pool.wait_ge(S.dec, k + 2)
                    pool.wait_ge(S.Y, k + 1)
                    pool.tensor_tensor(Cdec[:, :, :], dec[:, :, :], spread(xc[0:64, q, 1, c * P:(c + 1) * P], 1, SHEADS),
                                       ALU.mult).then_inc(S.Cdec, 1)
                pool.wait_ge(S.rv, b + 2)
                pool.tensor_tensor(rs[:, :], rs[:, :], con["mhalf"][:, 0:TILES], ALU.pow).then_inc(S.rs, 1)

            lead(pool, S.Cdec, 1)
            sequence_turns(pool, back)

        @block.vector
        def _(dve):
            def front(b, q):
                dve.wait_ge(S.dtp, b + 1)
                step(dve, dve.tensor_tensor(u[:, :, :], psA[:, 1, 0:TILES * SHEADS].rearrange("p (j h) -> p j h", h=SHEADS),
                                            spread(dt_bias, 1, TILES), ALU.add), S.u, b + 1)
                dve.scalar_tensor_tensor(out=au[:, :, :], in0=u[:, :, :], scalar=-1.0, in1=u[:, :, :], op0=ALU.mult,
                                         op1=ALU.max).then_inc(S.absu, 1)
                for g in range(GROUPS2):
                    r, first = rows(g), (b * GROUPS2 + g) * (TAPS - 1)
                    dve.wait_ge(S.evac, b * 6 + (g + 3))
                    dve.wait_ge(S.silu, b * 4 + (g + 1))
                    step(dve, dve.tensor_scalar(acc[r, g, :], craw[r, g, TAPS - 1:], cw[r, g, TAPS - 1:TAPS],
                                                cw[r, g, TAPS:TAPS + 1], ALU.mult, ALU.add), S.taps, first + 1)
                    for t in range(1, TAPS):
                        ins = dve.scalar_tensor_tensor(out=acc[r, g, :], in0=craw[r, g, TAPS - 1 - t:TAPS - 1 - t + SEQ],
                                                       scalar=cw[r, g, TAPS - 1 - t:TAPS - t], in1=acc[r, g, :],
                                                       op0=ALU.mult, op1=ALU.add)
                        if t < TAPS - 1:
                            step(dve, ins, S.taps, first + (t + 1))
                        else:
                            ins.then_inc(S.conv, 1)
                    if g == 0:
                        dve.wait_ge(S.ln, b + 1)
                        step(dve, dve.scalar_tensor_tensor(out=dt[:, q, :, :], in0=u[:, :, :], scalar=0.0, in1=au[:, :, :],
                                                           op0=ALU.max, op1=ALU.add), S.dt, b + 1)
                        dve.tensor_tensor(a[:, q, :, :], dt[:, q, :, :], spread(A[:, :], 1, TILES), ALU.mult).then_inc(S.a, 1)

            def back(b, q):
                for c in range(TILES):
                    k = b * TILES + c
                    dve.wait_ge(S.xtok, k + 1)
                    dve.wait_ge(S.Y, k + 1)
                    step(dve, dve.tensor_tensor(Xdt[:, :, :], psX[:, 0:SHEADS * HD].rearrange("p (h d) -> p h d", h=SHEADS),
                                                spread(dt[:, q, c, :], 2, HD), ALU.mult), S.Xdt, k + 2)
                    dve.tensor_copy(Btok[:, :], psX[:, 2 * P:2 * P + SSTATE]).then_inc(S.Btok, 1)
                    dve.wait_ge(S.G, k + 1)
                    step(dve, dve.tensor_tensor(Gm[:, :], psG[:, 0:P], tri[:, :], ALU.mult), S.Gm, k + 1)
                    dve.wait_ge(S.E, k + 2)
                    dve.tensor_tensor(M[:, :, :], E[:, :, :], spread(Gm[:, :], 1, SHEADS), ALU.mult).then_inc(S.M, 1)
                    dve.tensor_tensor(Xs[:, :, :], Xdt[:, :, :], E[:, :, P - 1:P].to_broadcast([P, SHEADS, HD]),
                                      ALU.mult).then_inc(S.Xs, 1)
                    dve.wait_ge(S.M, k + 1)
                    dve.wait_ge(S.St, k + 2)
                    add = psG[0:64, ST0:ST0 + SHEADS * HD].rearrange("p (h d) -> p h d", h=SHEADS)
                    if c == 0:
                        step(dve, dve.tensor_copy(state[:, 0, :, :], add), S.state, k + 2)
                    elif c < TILES - 1:
                        dve.wait_ge(S.dec, k + 2)
                        step(dve, dve.tensor_tensor(state[:, c % 2, :, :], state[:, (c - 1) % 2, :, :],
                                                    dec[:, :, P - 1:P].to_broadcast([64, SHEADS, HD]), ALU.mult),
                             S.decayed, 4 + b * 2 + c)
                        step(dve, dve.tensor_tensor(state[:, c % 2, :, :], state[:, c % 2, :, :], add, ALU.add), S.state, k + 2)
                    else:
                        dve.nop().then_inc(S.state, 1)
                dve.wait_ge(S.Y, b * TILES + (TILES + 1))
                for h in range(2):
                    dve.scalar_tensor_tensor(out=yg[:, h, :], in0=xc[:, q, 2 + h, :], scalar=Dcol[:, h:h + 1],
                                             in1=psY[:, h, :], op0=ALU.mult, op1=ALU.add).then_inc(S.skip, 1)
                dve.wait_ge(S.skip, b * 2 + 2)
                step(dve, dve.tensor_tensor(yg[:, :, :], yg[:, :, :], zs[:, q, :, :], ALU.mult), S.yg, b + 2)
                dve.wait_ge(S.ms, b + 1)
                dve.tensor_scalar(rs[:, :], psC[:, 0:TILES], 1.0 / INNER, EPS, ALU.mult, ALU.add).then_inc(S.rv, 1)
                dve.wait_ge(S.rs, b + 1)
                dve.wait_ge(S.out, b + 1)
                for j in range(TILES):
                    last = dve.scalar_tensor_tensor(out=y_tok[:, bass.ds(b * TILES + j, 1), :].squeeze(1),
                                                    in0=psO[:, j * P:(j + 1) * P], scalar=rs[:, j:j + 1],
                                                    in1=xin[:, q, j, :], op0=ALU.mult, op1=ALU.add)
                last.then_inc(S.y, 1)

            lead(dve, S.rv, 1)
            lead(dve, S.Xdt, 1)
            lead(dve, S.Btok, 1)
            lead(dve, S.Xs, 1)
            lead(dve, S.state, 1)
            lead(dve, S.yg, 1)
            lead(dve, S.y, 2)
            front(0, 0)
            sequence_turns(dve, lambda b, q: (None if is_at(b, BATCH - 1) else front(b + 1, 1 - q), back(b, q)))


def layout2(a, np):
    f = np.float32
    cw, cb = a["L1_attn_conv_w"], a["L1_attn_conv_b"]
    w = np.concatenate([cw, cb[:, None]], 1)
    zero = np.zeros((64, TAPS + 1), f)
    conv = np.concatenate([w[INNER:INNER + 64], zero, w[INNER + 64:], zero, w[:P], w[P:INNER]], 0)
    row = lambda v: np.tile(v[None], (P, 1))
    two = lambda v: v.reshape(2, P).T
    return {
        "m_in": a["L1_attn_W_in"].T,
        "m_small": np.concatenate([conv.reshape(GROUPS2, P, TAPS + 1).transpose(1, 0, 2).reshape(P, -1),
                                   row(a["L1_attn_dt_bias"]), row(a["L1_attn_A_log"]),
                                   two(np.repeat(a["L1_attn_D"], HD)), two(a["L1_attn_norm_w"])], 1),
        "m_out": a["L1_attn_W_out"].T.reshape(2, P, D).transpose(1, 0, 2),
        "m_tri": np.triu(np.ones((P, P), f)),
        "m_strict": np.tril(np.ones((P, P), f), -1),
    }


EXPERTS, FF = 8, 512
KF = FF // P
EC = 2 * FF + KF + 2


def stage3_route(nc, x_tok, xn_tok, con, centT, xT, gates):
    with ExitStack() as ctx:
        sb = lambda n, s: ctx.enter_context(nc.sbuf_tensor(f"g3_{n}", s, F32))
        S = semaphores(nc, ctx, "g3", "n0 n1 x0 x1 xt nt raw xT aff affs ex own")
        raw_in, norm_in = sb("raw_in", [P, 2, TILES, D]), sb("norm_in", [P, 2, TILES, D])
        rawT = sb("rawT", [P, 2, SEQ])
        aff, score = sb("aff", [P, NT, EXPERTS]), sb("score", [P, NT, EXPERTS])
        top, alpha = sb("top", [P, NT]), sb("alpha", [P, NT])
        pb = lambda n: ctx.enter_context(nc.psum_tensor(f"g3_{n}", [P, 2, 512], F32))
        ps_x, ps_n, ps_a = pb("ps_x"), pb("ps_n"), pb("ps_a")
        block = ctx.enter_context(nc.Block())

        @block.sync
        def _(sp):
            with sp.Fori(0, BATCH // 2) as i:
                for q in range(2):
                    b = 2 * i + q
                    sp.wait_ge(S.nt, b + 1)
                    sp.dma_start(raw_in[:, q, :, :], x_tok[:, bass.ds(b * TILES, TILES), :]).then_inc((S.x0, S.x1)[q], 16)
                    sp.dma_start(norm_in[:, q, :, :], xn_tok[:, bass.ds(b * TILES, TILES), :]).then_inc((S.n0, S.n1)[q], 16)

        @block.tensor
        def _(pe):
            lead(pe, S.nt, 2)
            with pe.Fori(0, BATCH // 2) as i:
                for q in range(2):
                    b = 2 * i + q
                    pe.wait_ge(S.xT, b + 1)
                    pe.wait_ge((S.x0, S.x1)[q], i * 16 + 16)
                    for j in range(TILES):
                        last = pe.transpose(ps_x[:, q, j * P:(j + 1) * P], raw_in[:, q, j, :], con["ident"])
                    last.then_inc(S.xt, 1)
                    pe.wait_ge((S.n0, S.n1)[q], i * 16 + 16)
                    for j in range(TILES):
                        last = pe.transpose(ps_n[:, q, j * P:(j + 1) * P], norm_in[:, q, j, :], con["ident"])
                    last.then_inc(S.nt, 1)
                    pe.wait_ge(S.raw, b + 1)
                    pe.wait_ge(S.affs, b + 1)
                    for j in range(TILES):
                        last = pe.matmul(ps_a[:, q, j * EXPERTS:(j + 1) * EXPERTS], rawT[:, q, j * P:(j + 1) * P], centT,
                                         start=True, stop=True, skip_group_check=True)
                    last.then_inc(S.aff, 1)

        @block.scalar
        def _(act):
            lead(act, S.xT, 2)
            with act.Fori(0, BATCH // 2) as i:
                for q in range(2):
                    b = 2 * i + q
                    act.wait_ge(S.xt, b + 1)
                    act.copy(rawT[:, q, :], ps_x[:, q, :]).then_inc(S.raw, 1)
                    act.wait_ge(S.nt, b + 3)
                    act.copy(xT[:, bass.ds(b * SEQ, SEQ)], ps_n[:, q, :]).then_inc(S.xT, 1)
            act.wait_ge(S.own, 1)
            act.activation(alpha[:, :], top[:, :], ACT.Exp, scale=-1.0).then_inc(S.ex, 1)

        @block.vector
        def _(dve):
            lead(dve, S.affs, 2)
            with dve.Fori(0, BATCH // 2) as i:
                for q in range(2):
                    b = 2 * i + q
                    dve.wait_ge(S.aff, b + 1)
                    dve.tensor_copy(aff[:, bass.ds(b * TILES, TILES), :],
                                    ps_a[:, q, 0:TILES * EXPERTS].rearrange("p (j e) -> p j e", j=TILES)).then_inc(S.affs, 1)
            dve.wait_ge(S.affs, 2 + BATCH)
            own = Order(dve, S.own)
            own(dve.tensor_reduce(top[:, :], aff[:, :, :], AX.X, ALU.max))
            own(dve.tensor_tensor(score[:, :, :], aff[:, :, :], spread(top[:, :], 2, EXPERTS), ALU.is_equal))
            own(dve.tensor_tensor(score[:, :, :], score[:, :, :], spread(con["countdown"], 1, NT), ALU.mult))
            dve.wait_ge(S.ex, 1)
            own(dve.tensor_reduce(top[:, :], score[:, :, :], AX.X, ALU.max))
            own(dve.tensor_tensor(score[:, :, :], score[:, :, :], spread(top[:, :], 2, EXPERTS), ALU.is_equal))
            own(dve.tensor_scalar(alpha[:, :], alpha[:, :], 1.0, None, ALU.add))
            own(dve.reciprocal(alpha[:, :], alpha[:, :]))
            own(dve.tensor_tensor(gates[:, :, :], score[:, :, :], spread(alpha[:, :], 2, EXPERTS), ALU.mult))


def edge_turns(eng, turn, n):
    turn(0)
    with eng.Fori(0, n - 2) as i:
        turn(i + 1)
    turn(n - 1)


def stage3_experts(nc, con, dram, xT, gates, acc):
    with ExitStack() as ctx:
        sb = lambda n, s: ctx.enter_context(nc.sbuf_tensor(f"e3_{n}", s, F32))
        S = semaphores(nc, ctx, "e3", " ".join(f"w{e}" for e in range(EXPERTS)) + " b2 x up hA hV down acc own")
        wts = sb("wts", [P, EXPERTS, EC])
        b2 = sb("b2", [1, EXPERTS, D])
        xe = sb("xe", [P, 2, SEQ])
        hid = sb("hid", [P, 2, KF, SEQ])
        ps_u = ctx.enter_context(nc.psum_tensor("e3_ps_u", [P, KF, 512], F32))
        ps_d = ctx.enter_context(nc.psum_tensor("e3_ps_d", [P, 2, 512], F32))
        loaded = S[:EXPERTS]
        w1 = lambda e, f: wts[:, e, f * P:(f + 1) * P]
        w2 = lambda e, f: wts[:, e, FF + f * P:FF + (f + 1) * P]
        b1 = lambda e, f: wts[:, e, 2 * FF + f:2 * FF + f + 1]
        ACT_F = KF - 1
        block = ctx.enter_context(nc.Block())

        def following(b, e):
            if e + 1 < EXPERTS:
                return b, e + 1
            return None if is_at(b, BATCH - 1) else (b + 1, 0)

        def preceding(b, e):
            if e:
                return b, e - 1
            return None if is_at(b, 0) else (b - 1, EXPERTS - 1)

        @block.sync
        def _(sp):
            sp.dma_start(b2[:, :, :], dram["eb2"]).then_inc(S.b2, 16)
            for e in range(EXPERTS):
                sp.dma_start(wts[:, e, :], dram["ew"][:, e, :]).then_inc(loaded[e], 16)

        @block.tensor
        def _(pe):
            def ups(b, e):
                m = b * EXPERTS + e
                pe.wait_ge(loaded[e], 16)
                pe.wait_ge(S.x, m + 1)
                pe.wait_ge(S.hA, m + 1)
                pe.wait_ge(S.hV, m + 1)
                for f in range(KF):
                    pe.matmul(ps_u[:, f, :], w1(e, f), xe[:, e % 2, :], start=True, stop=True).then_inc(S.up, 1)

            def turn(b):
                for e in range(EXPERTS):
                    m = b * EXPERTS + e
                    if following(b, e):
                        ups(*following(b, e))
                    else:
                        pe.wait_ge(S.hA, m + 2)
                        pe.wait_ge(S.hV, m + 2)
                    pe.wait_ge(S.acc, m + 1)
                    for j in range(TILES):
                        for f in range(KF):
                            pe.matmul(ps_d[:, e % 2, j * P:(j + 1) * P], hid[:, e % 2, f, j * P:(j + 1) * P], w2(e, f),
                                      start=f == 0, stop=False)
                        last = pe.matmul(ps_d[:, e % 2, j * P:(j + 1) * P], con["ones"][0:1, :], b2[:, e, :],
                                         start=False, stop=True)
                    last.then_inc(S.down, 1)

            lead(pe, S.down, 2)
            pe.wait_ge(S.b2, 16)
            ups(0, 0)
            edge_turns(pe, turn, BATCH)

        @block.scalar
        def _(act):
            def turn(b):
                for e in range(EXPERTS):
                    m = b * EXPERTS + e
                    act.wait_ge(S.down, m + 1)
                    for f in range(ACT_F):
                        act.wait_ge(S.up, m * KF + (f + 1))
                        last = act.activation(hid[:, e % 2, f, :], ps_u[:, f, :], ACT.Relu, bias=b1(e, f))
                    last.then_inc(S.hA, 1)

            lead(act, S.hA, 1)
            for e in range(EXPERTS):
                act.wait_ge(loaded[e], 16)
            edge_turns(act, turn, BATCH)

        @block.vector
        def _(dve):
            def affine(b, e):
                dve.tensor_scalar(xe[:, e % 2, :], xT[:, bass.ds(b * SEQ, SEQ)], wts[:, e, EC - 2:EC - 1],
                                  wts[:, e, EC - 1:EC], ALU.mult, ALU.add).then_inc(S.x, 1)

            def add(b, e):
                m = b * EXPERTS + e
                dve.wait_ge(S.down, m + 3)
                for j in range(TILES):
                    t = b * TILES + j
                    a = acc[:, bass.ds(t, 1), :].squeeze(1)
                    last = dve.scalar_tensor_tensor(out=a, in0=ps_d[:, e % 2, j * P:(j + 1) * P],
                                                    scalar=gates[:, bass.ds(t, 1), e], in1=a, op0=ALU.mult, op1=ALU.add)
                last.then_inc(S.acc, 1)
                dve.wait_ge(S.acc, m + 3)

            def turn(b):
                for e in range(EXPERTS):
                    m = b * EXPERTS + e
                    if following(b, e):
                        affine(*following(b, e))
                    dve.wait_ge(S.down, m + 1)
                    for f in range(ACT_F, KF):
                        dve.wait_ge(S.up, m * KF + (f + 1))
                        last = dve.tensor_scalar(hid[:, e % 2, f, :], ps_u[:, f, :], b1(e, f), 0.0, ALU.add, ALU.max)
                    last.then_inc(S.hV, 1)
                    if preceding(b, e):
                        add(*preceding(b, e))

            lead(dve, S.hV, 1)
            lead(dve, S.acc, 2)
            for e in range(EXPERTS):
                dve.wait_ge(loaded[e], 16)
            affine(0, 0)
            edge_turns(dve, turn, BATCH)
            add(BATCH - 1, EXPERTS - 1)


def stage3(nc, xn_tok, y_tok, con, dram):
    with ExitStack() as ctx:
        sb = lambda n, s: ctx.enter_context(nc.sbuf_tensor(f"s3_{n}", s, F32))
        S = semaphores(nc, ctx, "s3", "load copy")
        small = sb("small", [P, EXPERTS])
        xT, gates = sb("xT", [P, BATCH * SEQ]), sb("gates", [P, NT, EXPERTS])
        twice = sb("twice", [P, NT, D])
        with nc.Block() as block:
            @block.sync
            def _(sp):
                sp.dma_start(small[:, :], dram["e_small"]).then_inc(S.load, 16)
                sp.wait_ge(S.load, 16)
        normalize(nc, "n3b", con, xn_tok, twice)
        stage3_route(nc, xn_tok, twice, con, small[:, 0:EXPERTS], xT, gates)
        with nc.Block() as block:
            @block.vector
            def _(dve):
                dve.tensor_copy(y_tok[:, :, :], xn_tok[:, :, :]).then_inc(S.copy, 1)
        stage3_experts(nc, con, dram, xT, gates, y_tok)


def layout3(a, np):
    w1 = a["L1_ffn_w1"].transpose(1, 0, 2)
    w2 = a["L1_ffn_w2"].reshape(EXPERTS, KF, P, D).transpose(2, 0, 1, 3).reshape(P, EXPERTS, FF)
    return {
        "ew": np.concatenate([w1, w2, a["L1_ffn_b1"].reshape(EXPERTS, KF, P).transpose(2, 0, 1),
                              a["L1_ffn_ln_g"].T[:, :, None], a["L1_ffn_ln_b"].T[:, :, None]], 2),
        "eb2": a["L1_ffn_b2"][None],
        "e_small": a["L1_ffn_centroids"].T,
    }

def host_layout(a, np):
    return {**layout1(a, np), **layout2(a, np), **layout3(a, np)}


def build(nc, x, consts, w0, out, extra):
    with ExitStack() as ctx:
        sb = lambda n, s, t=F32: ctx.enter_context(nc.sbuf_tensor(n, s, t))
        x_tok, xn_tok, y_tok = (sb(n, [P, NT, D]) for n in ("x_tok", "xn_tok", "y_tok"))
        kc = sb("con_sb", [P, 2 * P + 2 * 64 + 1 + 8])
        con = dict(ident=kc[:, 0:P], ones=kc[:, P:2 * P], half=kc[:, 2 * P:2 * P + 64],
                   mhalf=kc[:, 2 * P + 64:2 * P + 128], clamp_dt=kc[:, 2 * P + 128:2 * P + 129],
                   countdown=kc[:, 2 * P + 129:2 * P + 137])
        S = semaphores(nc, ctx, "io", "load store")
        tiles = lambda t: t.rearrange("b (j p) d -> p (b j) d", p=P)
        with nc.Block() as block:
            @block.sync
            def _(sp):
                sp.dma_start(kc[:, :], consts).then_inc(S.load, 16)
                sp.dma_start(x_tok[:, :, :], tiles(x)).then_inc(S.load, 16)
                sp.wait_ge(S.load, 32)
        if FIRST < 1:
            normalize(nc, "n0", con, x_tok, xn_tok)
            stage0(nc, None, xn_tok, y_tok, con, w0)
            normalize(nc, "r0", con, y_tok, xn_tok, x_tok)
        if STAGES > 1 and FIRST < 2:
            normalize(nc, "n1", con, x_tok, y_tok)
            stage1(nc, y_tok, con, extra)
            normalize(nc, "r1", con, y_tok, xn_tok, x_tok)
        if STAGES > 2 and FIRST < 3:
            normalize(nc, "n2", con, x_tok, xn_tok)
            stage2(nc, xn_tok, y_tok, con, extra)
            normalize(nc, "r2", con, y_tok, xn_tok, x_tok)
        if STAGES > 3:
            normalize(nc, "n3", con, x_tok, xn_tok)
            stage3(nc, xn_tok, y_tok, con, extra)
            normalize(nc, "r3", con, y_tok, xn_tok, x_tok)
        with nc.Block() as block:
            @block.sync
            def _(sp):
                sp.dma_start(tiles(out), x_tok[:, :, :]).then_inc(S.store, 16)
                sp.wait_ge(S.store, 16)


def kernel(**inputs):
    import numpy as np
    import concourse.bacc as bacc
    from concourse.bass_utils import run_bass_kernel_spmd

    a = {k: np.asarray(v) for k, v in inputs.items()}
    f = np.float32
    c, r = (0.1 + 0.001) / 2, (0.1 - 0.001) / 2
    arrays = {
        "x": a["L0_attn_x"],
        "consts": np.concatenate([np.eye(P, dtype=f), np.ones((P, P), f), np.full((P, 64), 0.5, f),
                                  np.full((P, 64), -0.5, f), np.full((P, 1), -c * 0.5 / (r + 1e-8), f),
                                  np.tile(np.arange(8, 0, -1, dtype=f), (P, 1))], 1),
        "w0": np.concatenate([a["L0_attn_W_dt"].T, a["L0_attn_W_B"].T, a["L0_attn_W_C"].T, a["L0_attn_A_log"],
                              a["L0_attn_b_dt"][:, None], a["L0_attn_D_param"][:, None]], 1),
    }
    arrays.update(host_layout(a, np))
    arrays = {k: np.ascontiguousarray(v) for k, v in arrays.items()}
    nc = bacc.Bacc("TRN2", target_bir_lowering=False, num_devices=1)
    dram = {k: nc.dram_tensor(k, v.shape, mybir.dt.from_np(v.dtype), kind="ExternalInput").ap() for k, v in arrays.items()}
    out = nc.dram_tensor("out", a["L0_attn_x"].shape, F32, kind="ExternalOutput").ap()
    build(nc, dram.pop("x"), dram.pop("consts"), dram.pop("w0"), out, dram)
    result = run_bass_kernel_spmd(nc, [arrays], core_ids=[0])
    return result.results[0]["out"]
```

```python
import concourse.bass as bass
from concourse import mybir
from collections import namedtuple
from contextlib import ExitStack

F32 = mybir.dt.float32
BF16 = mybir.dt.bfloat16
ALU = mybir.AluOpType
ACT = mybir.ActivationFunctionType
AX = mybir.AxisListType

P = 128
BATCH, SEQ, D = 8, 512, 128
TILES = SEQ // P
EPS = 1e-5
STAGES = 4
FIRST = 0


def semaphores(nc, ctx, prefix, names):
    sems = [nc.alloc_semaphore(name=f"{prefix}_{n}") for n in names.split()]

    def clear():
        nc.clear_and_free_semaphores(sems)
        nc.all_engine_barrier()

    ctx.callback(clear)
    return namedtuple("Semaphores", names)(*sems)


def lead(eng, sem, n):
    for _ in range(n):
        eng.nop().then_inc(sem, 1)


def step(eng, ins, sem, count):
    ins.then_inc(sem, 1)
    eng.wait_ge(sem, count)


class Order:

    def __init__(self, eng, sem, per=0, base=0):
        self.eng, self.sem, self.per, self.base, self.turn, self.n = eng, sem, per, base, 0, 0

    def start(self, turn):
        self.turn, self.n = turn, 0

    def __call__(self, ins):
        self.n += 1
        step(self.eng, ins, self.sem, self.turn * self.per + (self.base + self.n))

    def end(self):
        assert self.n == self.per, (self.n, self.per)


def spread(ap, axis, n):
    ap = ap.unsqueeze(axis)
    return ap.to_broadcast([n if k == axis else m for k, m in enumerate(ap.shape)])


NT = BATCH * TILES


def stage_sequences(sp, src, buf, used, staged):
    with sp.Fori(0, BATCH // 2) as i:
        for q in range(2):
            sp.wait_ge(used, 2 * i + (q + 1))
            sp.dma_start(buf[:, q, :, :], src[:, bass.ds((2 * i + q) * TILES, TILES), :]).then_inc(staged[q], 16)


def transpose_sequences(pe, buf, ps, con, staged, copied, done):
    lead(pe, done, 2)
    with pe.Fori(0, BATCH // 2) as i:
        for q in range(2):
            pe.wait_ge(copied, 2 * i + (q + 1))
            pe.wait_ge(staged[q], i * 16 + 16)
            for j in range(TILES):
                last = pe.transpose(ps[:, q, j * P:(j + 1) * P], buf[:, q, j, :], con["ident"])
            last.then_inc(done, 1)


MOMENTS = 6


def moment_step(dve, i, stats, mean, diff, var, sign=1):
    if i == 0:
        return dve.tensor_tensor(mean, stats[:, :, 1], stats[:, :, 4], ALU.add)
    if i == 1:
        return dve.tensor_tensor(diff, stats[:, :, 1], stats[:, :, 4], ALU.subtract)
    if i == 2:
        return dve.tensor_tensor(var, stats[:, :, 2], stats[:, :, 5], ALU.add)
    if i == 3:
        return dve.tensor_scalar(mean, mean, 0.5 * sign, None, ALU.mult)
    if i == 4:
        return dve.scalar_tensor_tensor(out=diff, in0=diff, scalar=0.25, in1=diff, op0=ALU.mult, op1=ALU.mult)
    return dve.scalar_tensor_tensor(out=var, in0=var, scalar=1.0 / D, in1=diff, op0=ALU.mult, op1=ALU.add)


def moments(dve, own, stats, mean, diff, var):
    for i in range(MOMENTS):
        own(moment_step(dve, i, stats, mean[:, :], diff[:, :], var[:, :]))


def normalize(nc, tag, con, y, x, xn):
    GROUPS = 4
    G = NT // GROUPS
    with ExitStack() as ctx:
        sb = lambda n, s: ctx.enter_context(nc.sbuf_tensor(f"{tag}_{n}", s, F32))
        S = semaphores(nc, ctx, tag, "stats0 stats1 own0 own1 veps0 veps1 rstd0 rstd1 offset out added")
        parts = ([(0, y)] if y is not None else []) + ([(1, x)] if xn is not None else [])
        stats_of, own_of, veps, rstds = (S[2 * i:2 * i + 2] for i in range(4))
        stats = sb("stats", [P, 2, NT, 6])
        mean, diff, var, rstd = (sb(n, [P, 2, NT]) for n in ("mean", "diff", "var", "rstd"))
        offset = sb("offset", [P, NT])
        block = ctx.enter_context(nc.Block())
        group = lambda g: slice(g * G, (g + 1) * G)

        @block.vector
        def _(dve):
            def add(g):
                dve.wait_ge(S.rstd0, g + 1)
                for t in range(g * G, (g + 1) * G):
                    last = dve.tensor_scalar(y[:, t, :], y[:, t, :], mean[:, 0, t:t + 1], rstd[:, 0, t:t + 1], ALU.add, ALU.mult)
                step(dve, last, S.out, g + 1)
                step(dve, dve.tensor_tensor(x[:, group(g), :], x[:, group(g), :], y[:, group(g), :], ALU.add), S.added, g + 1)

            def moment(i, g, n):
                a, s = own_of[i], g * MOMENTS
                if n == 0:
                    dve.wait_ge(stats_of[i], (g + 1) * G)
                if n > 2:
                    dve.wait_ge(a, s + (n - 2 if n < 5 else n))
                m = (mean[:, i, group(g)], diff[:, i, group(g)], var[:, i, group(g)])
                if n < MOMENTS:
                    moment_step(dve, n, stats[:, i, group(g), :], *m, -1).then_inc(a, 1)
                else:
                    dve.tensor_scalar(m[2], m[2], EPS, None, ALU.add).then_inc(veps[i], 1)

            for i, src in parts:
                for g in range(GROUPS + 1):
                    if g < GROUPS:
                        if i == 1 and y is not None:
                            add(g)
                        for j in range(G):
                            dve.bn_stats(stats[:, i, g * G + j, :], src[:, g * G + j, :]).then_inc(stats_of[i], 1)
                            if g > 0 and j <= MOMENTS:
                                moment(i, g - 1, j)
                    else:
                        for n in range(MOMENTS + 1):
                            moment(i, g - 1, n)
            if xn is None:
                for g in range(GROUPS):
                    add(g)

        @block.gpsimd
        def _(pool):
            for i, src in parts:
                for g in range(GROUPS):
                    pool.wait_ge(veps[i], g + 1)
                    step(pool, pool.tensor_tensor(rstd[:, i, group(g)], var[:, i, group(g)], con["mhalf"][:, 0:G], ALU.pow),
                         rstds[i], g + 1)
                    if i == 1:
                        pool.tensor_tensor(offset[:, group(g)], mean[:, 1, group(g)], rstd[:, 1, group(g)], ALU.mult).then_inc(S.offset, 1)

        @block.scalar
        def _(act):
            if xn is not None:
                for t in range(NT):
                    if t % G == 0:
                        act.wait_ge(S.offset, t // G + 1)
                    act.activation(xn[:, t, :], x[:, t, :], ACT.Identity, bias=offset[:, t:t + 1], scale=rstd[:, 1, t:t + 1])


N_STATE = 8
STEPS = 10
CHUNKS = -(-SEQ // STEPS)
CW = BATCH * STEPS
COLS0 = CHUNKS * CW


def stage0_project(nc, xn_tok, w, con, xnT, dt, dtx):
    with ExitStack() as ctx:
        sb = lambda n, s: ctx.enter_context(nc.sbuf_tensor(n, s, F32))
        S = semaphores(nc, ctx, "p0", "staged0 staged1 xt xT xT_part proj u absu ex ln sp th pad dt dtx")
        xn = sb("p0_xn", [P, 2, TILES, D])
        u, a = sb("p0_u", [P, COLS0]), sb("p0_a", [P, COLS0])
        ps_t = ctx.enter_context(nc.psum_tensor("p0_ps_t", [P, 2, SEQ], F32))
        ps_p = ctx.enter_context(nc.psum_tensor("p0_ps_p", [P, 2, SEQ], F32))
        GROUPS, GW = 10, COLS0 // 10
        c, r = (0.1 + 0.001) / 2, (0.1 - 0.001) / 2
        block = ctx.enter_context(nc.Block())

        @block.sync
        def _(sp):
            stage_sequences(sp, xn_tok, xn, S.xt, (S.staged0, S.staged1))

        @block.vector
        def _(dve):
            dve.memset(xnT[:, (CHUNKS - 1) * CW:], 0.0).then_inc(S.pad, 1)
            dve.wait_ge(S.u, 2 + GROUPS)
            dve.scalar_tensor_tensor(out=a[:, :], in0=u[:, :], scalar=-1.0, in1=u[:, :], op0=ALU.mult,
                                     op1=ALU.max).then_inc(S.absu, 1)
            dve.wait_ge(S.ln, 1)
            dve.scalar_tensor_tensor(out=u[:, :], in0=u[:, :], scalar=0.0, in1=a[:, :], op0=ALU.max,
                                     op1=ALU.add).then_inc(S.sp, 1)
            dve.wait_ge(S.th, 1)
            step(dve, dve.tensor_scalar(dt[:, :], u[:, :], r / 0.5, c, ALU.mult, ALU.add), S.dt, 1)
            dve.wait_ge(S.xT, 2 + BATCH)
            step(dve, dve.tensor_tensor(dtx[:, :], dt[:, :], xnT[:, :], ALU.mult), S.dtx, 1)

        @block.tensor
        def _(pe):
            transpose_sequences(pe, xn, ps_t, con, (S.staged0, S.staged1), S.xT, S.xt)
            pe.wait_ge(S.xT, 2 + BATCH)
            pe.wait_ge(S.pad, 1)
            with pe.Fori(0, GROUPS // 2) as i:
                for q in range(2):
                    pe.wait_ge(S.u, 2 * i + (q + 1))
                    pe.matmul(ps_p[:, q, 0:GW], w["W_dtT"], xnT[:, bass.ds((2 * i + q) * GW, GW)],
                              start=True, stop=True).then_inc(S.proj, 1)

        @block.scalar
        def _(act):
            lead(act, S.xT, 2)
            lead(act, S.u, 2)
            full = (CHUNKS - 1) * STEPS
            cols = xnT[:, :].rearrange("p (k b t) -> p k b t", b=BATCH, t=STEPS)
            act.wait_ge(S.pad, 1)
            with act.Fori(0, BATCH // 2) as i:
                for q in range(2):
                    act.wait_ge(S.xt, 2 * i + (q + 3))
                    b = 2 * i + q
                    act.copy(cols[:, 0:CHUNKS - 1, bass.ds(b, 1), :],
                             ps_t[:, q, 0:full].rearrange("p (k t) -> p k t", t=STEPS).unsqueeze(2)).then_inc(S.xT_part, 1)
                    act.wait_ge(S.xT_part, 2 * i + (q + 1))
                    act.copy(cols[:, CHUNKS - 1, bass.ds(b, 1), 0:SEQ - full],
                             ps_t[:, q, full:SEQ].unsqueeze(1)).then_inc(S.xT, 1)
            with act.Fori(0, GROUPS // 2) as i:
                for q in range(2):
                    act.wait_ge(S.proj, 2 * i + (q + 1))
                    act.activation(u[:, bass.ds((2 * i + q) * GW, GW)], ps_p[:, q, 0:GW], ACT.Identity,
                                   bias=w["b_dt"]).then_inc(S.u, 1)
            act.wait_ge(S.absu, 1)
            step(act, act.activation(a[:, :], a[:, :], ACT.Exp, scale=-1.0), S.ex, 1)
            step(act, act.activation(a[:, :], a[:, :], ACT.Ln, bias=1.0), S.ln, 1)
            act.wait_ge(S.sp, 1)
            act.activation(u[:, :], u[:, :], ACT.Tanh, scale=0.5 / (r + 1e-8), bias=con["clamp_dt"]).then_inc(S.th, 1)


GC = 4
GROUPS0 = CHUNKS // GC
GW = GC * CW


def group_turns(eng, turn):
    turn(0, 0)
    with eng.Fori(0, (GROUPS0 - 3) // 2) as i:
        turn(2 * i + 1, 1)
        turn(2 * i + 2, 0)
    turn(GROUPS0 - 2, 1)
    turn(GROUPS0 - 1, 0)


def is_at(k, chunk):
    return isinstance(k, int) and k == chunk


def stage0_scan(nc, w, con, xnT, dt, dtx, y):
    with ExitStack() as ctx:
        sb = lambda n, s: ctx.enter_context(nc.sbuf_tensor(n, s, F32))
        pb = lambda n, s: ctx.enter_context(nc.psum_tensor(n, s, F32))
        S = semaphores(nc, ctx, "s0", "arg tanh dA B C dBx sq ones ss root h hC Y out own zero")
        W, ROWS, N = N_STATE * CW, N_STATE * BATCH, N_STATE
        PER = N // GC
        arg = sb("s0_arg", [P, 2, W])
        dA = sb("s0_dA", [P, 2, GC, W])
        dBx = sb("s0_dBx", [P, 2, GC, W])
        h = sb("s0_h", [P, 2, GC, W])
        hC = sb("s0_hC", [P, N, GW])
        first = sb("s0_first", [P, ROWS])
        sq = sb("s0_sq", [P, ROWS])
        ss, root, scale = sb("s0_ss", [P, BATCH]), sb("s0_root", [P, BATCH]), sb("s0_scale", [P, BATCH])
        psB, psC = pb("s0_psB", [P, 2, 512]), pb("s0_psC", [P, 2, 512])
        psS = pb("s0_psS", [P, 512])
        psY = pb("s0_psY", [P, 2, 512])
        block = ctx.enter_context(nc.Block())
        step_of = lambda t, s: t.rearrange("p (r t) -> p r t", t=STEPS)[:, :, s]
        of_state = lambda t, n: t.rearrange("p c (n i) -> p c n i", n=N)[:, :, n, :]
        chunks = lambda t: t.rearrange("p (c i) -> p c i", c=GC)
        is_last = lambda g: is_at(g, GROUPS0 - 1)

        @block.gpsimd
        def _(pool):
            def decay_argument(k, c):
                pool.wait_ge(S.dA, k + 1)
                pool.tensor_tensor(arg[:, c % 2, :].rearrange("p (n c) -> p n c", n=N),
                                   spread(dt[:, bass.ds(k * CW, CW)], 1, N),
                                   spread(w["A16"], 2, CW), ALU.mult).then_inc(S.arg, 1)

            def turn(g, q):
                for c in range(GC):
                    k = g * GC + c
                    pool.wait_ge(S.ss, k + 1)
                    pool.tensor_tensor(root[:, :], ss[:, :], con["half"][:, 0:BATCH], ALU.pow).then_inc(S.root, 1)
                    if not is_last(g):
                        decay_argument(k + GC, c)

            for c in range(GC):
                decay_argument(c, c)
            group_turns(pool, turn)

        @block.scalar
        def _(act):
            lead(act, S.dA, 2)
            lead(act, S.out, 2)

            def decay(k, q, c):
                act.wait_ge(S.arg, k + 1)
                step(act, act.activation(arg[:, c % 2, :], arg[:, c % 2, :], ACT.Tanh), S.tanh, k + 1)
                act.wait_ge(S.h, k + 1)
                act.activation(dA[:, q, c, :], arg[:, c % 2, :], ACT.Exp, scale=16.0).then_inc(S.dA, 1)

            def copy_out(g, q):
                act.wait_ge(S.Y, g * N + 2 * N)
                act.copy(y[:, :, bass.ds(g * (GC * STEPS), GC * STEPS)].rearrange("p b (c t) -> p c b t", c=GC),
                         psY[:, q, 0:GW].rearrange("p (c b t) -> p c b t", c=GC, b=BATCH)).then_inc(S.out, 1)

            def turn(g, q):
                if not is_last(g):
                    for c in range(GC):
                        decay(g * GC + (GC + c), 1 - q, c)
                if not is_at(g, 0):
                    copy_out(g - 1, 1 - q)

            for c in range(GC):
                decay(c, 0, c)
            group_turns(act, turn)
            copy_out(GROUPS0 - 1, 0)

        @block.tensor
        def _(pe):
            def rows_of(ps, weights, g, n, used, ready):
                pe.wait_ge(used, g * N + (n + 1))
                pe.matmul(ps[:, n % 2, 0:GW], weights[:, n, :], xnT[:, bass.ds(g * GW, GW)],
                          start=True, stop=True).then_inc(ready, 1)

            def sum_state(g, q, n):
                if n == 0:
                    pe.wait_ge(S.out, g + 1)
                    pe.matmul(psY[:, q, 0:GW], w["diagD"], xnT[:, bass.ds(g * GW, GW)], start=True, stop=False)
                pe.wait_ge(S.hC, g * N + (n + 3))
                pe.matmul(psY[:, q, 0:GW], con["ident"], hC[:, n, :], start=False, stop=n == N - 1).then_inc(S.Y, 1)

            def turn(g, q):
                for c in range(GC):
                    pe.wait_ge(S.sq, g * GC + (c + 1))
                    pe.matmul(psS[:, 0:ROWS], con["ones"], sq[:, :], start=True, stop=True).then_inc(S.ones, 1)
                    for n in range(c * PER, (c + 1) * PER):
                        if not is_at(g, 0):
                            rows_of(psC, w["WC_rep"], g - 1, n, S.hC, S.C)
                        if not is_last(g):
                            rows_of(psB, w["WB_rep"], g + 1, n, S.dBx, S.B)
                    if not is_at(g, 0):
                        for n in range((c - 1) * PER, c * PER):
                            if n >= 0:
                                sum_state(g - 1, 1 - q, n)
                if not is_at(g, 0):
                    for n in range(N - PER, N):
                        sum_state(g - 1, 1 - q, n)

            lead(pe, S.Y, N)
            for n in range(N):
                rows_of(psB, w["WB_rep"], 0, n, S.dBx, S.B)
            group_turns(pe, turn)
            for n in range(N):
                rows_of(psC, w["WC_rep"], GROUPS0 - 1, n, S.hC, S.C)
                if n:
                    sum_state(GROUPS0 - 1, 0, n - 1)
            sum_state(GROUPS0 - 1, 0, N - 1)

        @block.vector
        def _(dve):
            OWN = 7
            own = Order(dve, S.own, OWN)

            def inputs(g, q, n):
                dve.wait_ge(S.B, g * N + (n + 1))
                dve.tensor_tensor(of_state(dBx[:, q, :, :], n), chunks(psB[:, n % 2, 0:GW]),
                                  chunks(dtx[:, bass.ds(g * GW, GW)]), ALU.mult).then_inc(S.dBx, 1)

            def outputs(g, q, n):
                dve.wait_ge(S.C, g * N + (n + 1))
                dve.wait_ge(S.Y, g * N + (n + 1))
                dve.tensor_tensor(chunks(hC[:, n, :]), chunks(psC[:, n % 2, 0:GW]), of_state(h[:, q, :, :], n),
                                  ALU.mult).then_inc(S.hC, 1)

            def turn(g, q):
                dve.wait_ge(S.dBx, g * N + (N + 2))
                if not is_at(g, 0):
                    dve.wait_ge(S.hC, g * N - (N - 2))
                for c in range(GC):
                    k = g * GC + c
                    dA_k, dBx_k = dA[:, q, c, :], dBx[:, q, c, :]
                    before = h[:, q, c - 1, :] if c else h[:, 1 - q, GC - 1, :]
                    own.start(k)
                    dve.wait_ge(S.dA, k + 3)
                    own(dve.tensor_tensor(first[:, :], step_of(dA_k, 0), step_of(before, STEPS - 1), ALU.mult))
                    own(dve.tensor_tensor(first[:, :], first[:, :], step_of(dBx_k, 0), ALU.add))
                    step(dve, dve.tensor_tensor(sq[:, :], first[:, :], first[:, :], ALU.mult), S.sq, k + 1)
                    own(dve.memset(step_of(dA_k, 0), 0.0))
                    dve.wait_ge(S.ones, k + 1)
                    step(dve, dve.tensor_reduce(ss[:, :], psS[:, 0:ROWS].rearrange("p (n b) -> p b n", b=BATCH), AX.X,
                                                ALU.add), S.ss, k + 1)
                    for n in range(c * PER, (c + 1) * PER):
                        if not is_at(g, 0):
                            outputs(g - 1, 1 - q, n)
                        if not is_last(g):
                            inputs(g + 1, 1 - q, n)
                    dve.wait_ge(S.root, k + 1)
                    own(dve.tensor_scalar(scale[:, :], root[:, :], 1e-8, None, ALU.add))
                    own(dve.reciprocal(scale[:, :], scale[:, :]))
                    own(dve.tensor_scalar(scale[:, :], scale[:, :], 20.0, 1.0, ALU.mult, ALU.min))
                    own(dve.tensor_tensor(step_of(dBx_k, 0).rearrange("p (n b) -> p n b", b=BATCH),
                                          first[:, :].rearrange("p (n b) -> p n b", b=BATCH),
                                          spread(scale[:, :], 1, N), ALU.mult))
                    step(dve, dve.tensor_tensor_scan(h[:, q, c, :], dA_k, dBx_k, 0.0, ALU.mult, ALU.add),
                         S.h, k + (2 * GC + 1))
                    own.end()

            lead(dve, S.h, 2 * GC)
            lead(dve, S.dBx, 2)
            lead(dve, S.hC, 2)
            step(dve, dve.memset(h[:, 1, GC - 1, :], 0.0), S.zero, 1)
            for n in range(N):
                inputs(0, 0, n)
            group_turns(dve, turn)
            for n in range(N):
                outputs(GROUPS0 - 1, 0, n)


def stage0_output(nc, y, con, y_tok):
    with ExitStack() as ctx:
        S = semaphores(nc, ctx, "o0", "staged0 staged1 yt y_tok")
        buf = ctx.enter_context(nc.sbuf_tensor("o0_buf", [P, 2, TILES, P], F32))
        ps = ctx.enter_context(nc.psum_tensor("o0_ps", [P, 2, SEQ], F32))
        block = ctx.enter_context(nc.Block())

        @block.sync
        def _(sp):
            with sp.Fori(0, BATCH // 2) as i:
                for q in range(2):
                    sp.wait_ge(S.yt, 2 * i + (q + 1))
                    sp.dma_start(buf[:, q, :, :].rearrange("p j t -> p (j t)"),
                                 y[:, bass.ds(2 * i + q, 1), 0:SEQ].squeeze(1)).then_inc((S.staged0, S.staged1)[q], 16)

        @block.tensor
        def _(pe):
            transpose_sequences(pe, buf, ps, con, (S.staged0, S.staged1), S.y_tok, S.yt)

        @block.scalar
        def _(act):
            lead(act, S.y_tok, 2)
            with act.Fori(0, BATCH // 2) as i:
                for q in range(2):
                    act.wait_ge(S.yt, 2 * i + (q + 3))
                    act.copy(y_tok[:, bass.ds((2 * i + q) * TILES, TILES), :],
                             ps[:, q, :].rearrange("p (j d) -> p j d", j=TILES)).then_inc(S.y_tok, 1)


def stage0(nc, xn_tok, y_tok, con, weights):
    with ExitStack() as ctx:
        sb = lambda n, s: ctx.enter_context(nc.sbuf_tensor(n, s, F32))
        W0 = 2 * D + 2 * N_STATE + N_STATE + 2
        raw = sb("w0_raw", [P, W0])
        wdt, wb, wc = raw[:, 0:D], raw[:, D:D + N_STATE], raw[:, D + N_STATE:D + 2 * N_STATE]
        alog, bdt, dpar = (raw[:, D + 2 * N_STATE:D + 3 * N_STATE], raw[:, D + 3 * N_STATE:D + 3 * N_STATE + 1],
                           raw[:, D + 3 * N_STATE + 1:D + 3 * N_STATE + 2])
        WBr, WCr = sb("w0_WB", [P, N_STATE, P]), sb("w0_WC", [P, N_STATE, P])
        A16, diagD = sb("w0_A16", [P, N_STATE]), sb("w0_diagD", [P, P])
        S = semaphores(nc, ctx, "w0", "load th ex own")
        with nc.Block() as block:
            @block.sync
            def _(sp):
                sp.dma_start(raw[:, 0:D + 3 * N_STATE + 2], weights).then_inc(S.load, 16)

            @block.scalar
            def _(act):
                act.wait_ge(S.load, 16)
                step(act, act.activation(A16[:, :], alog, ACT.Tanh, scale=0.5 / (5.0 + 1e-8)), S.th, 1)
                act.activation(A16[:, :], A16[:, :], ACT.Exp, scale=10.0).then_inc(S.ex, 1)

            @block.vector
            def _(dve):
                dve.wait_ge(S.load, 16)
                dve.tensor_copy(WBr[:, :, :], spread(wb, 2, P)).then_inc(S.own, 1)
                dve.tensor_copy(WCr[:, :, :], spread(wc, 2, P)).then_inc(S.own, 1)
                dve.tensor_scalar(diagD[:, :], con["ident"], dpar, None, ALU.mult).then_inc(S.own, 1)
                dve.wait_ge(S.ex, 1)
                dve.tensor_scalar(A16[:, :], A16[:, :], -0.5 / (8.0 + 1e-8), None, ALU.mult).then_inc(S.own, 1)

        w = dict(W_dtT=wdt, b_dt=bdt, WB_rep=WBr, WC_rep=WCr, A16=A16[:, :], diagD=diagD[:, :])
        xnT, dt, dtx = (sb(f"s0_{n}", [P, COLS0]) for n in ("xnT", "dt", "dtx"))
        y = sb("s0_y", [P, BATCH, CHUNKS * STEPS])
        stage0_project(nc, xn_tok, w, con, xnT, dt, dtx)
        stage0_scan(nc, w, con, xnT, dt, dtx, y)
        stage0_output(nc, y, con, y_tok)



LAYERS, HEADS, DH, WINDOW = 2, 8, 64, 64
PAIRS = HEADS // 2
HIDDEN = int(D * 4 * 2 / 3)
KH = -(-HIDDEN // P)
W1C = 2 * KH * P
UPC = W1C + 2 * KH + 2
MASKED = -1e30
TINY = 1e-30
LN_EXP_SET = 6
USES = 18
FIRST_USE = (0, 4, 8, 14)

DOWN_LAST, WO_TAIL, NORMED_TAIL, UP_TAIL, DOWN_TAIL = 15, 14, 17, (16, 19, 18), 21


def slot(n, u):
    return u % 2, n * (USES // 2) + (u // 2 + 1 + u % 2)


def layer_turns(eng, turn):
    turn(0)
    with eng.Fori(1, BATCH - 1) as n:
        turn(n)
    turn(BATCH - 1)


def stage1_load(nc, ctx, dram):
    sb = lambda n, s, t=F32: ctx.enter_context(nc.sbuf_tensor(f"s1_{n}", s, t))
    S = semaphores(nc, ctx, "w1", "load prep tab")
    wqk = sb("wqk", [P, LAYERS, PAIRS, 4, P])
    wv = sb("wv", [P, LAYERS, PAIRS, P])
    wo = sb("wo", [P, LAYERS, PAIRS, D])
    w2 = sb("w2", [P, LAYERS, KH, D])
    b2 = sb("b2", [1, LAYERS, D])
    up = sb("up", [P, LAYERS, UPC])
    base = sb("rot_base", [P, 4, SEQ])
    gain = sb("qk_gain", [P, LAYERS, 4])
    tab = sb("rot_tab", [P, LAYERS, 4, SEQ])
    mask_f = sb("mask_f", [P, TILES * P])
    mask = sb("mask", [P, TILES * P], BF16)
    ident16 = sb("ident16", [P, P], BF16)
    tiny = sb("tiny", [P, 1])
    pair = sb("pair", [P, 2])
    pair_ones = sb("pair_ones", [P, P])
    hT = sb("hT", [P, SEQ + 1])
    ft = sb("ft", [P, TILES, D])
    v_skew = sb("v_skew", [P, 2, TILES, P])
    loads = ((base, "rot_base"), (gain, "qk_gain"), (mask_f, "mask"), (wqk, "wqk"), (wv, "wv"), (wo, "wo"), (w2, "w2"),
             (b2, "b2"), (up, "up"))
    with nc.Block() as block:
        @block.sync
        def _(sp):
            for dst, name in loads:
                sp.dma_start(dst[tuple([slice(None)] * len(dst.shape))], dram[name]).then_inc(S.load, 16)
    return dict(S=S, wqk=wqk, wv=wv, wo=wo, w2=w2, b2=b2, up=up, base=base, gain=gain, tab=tab, mask_f=mask_f, mask=mask,
                ident16=ident16, tiny=tiny, pair=pair, pair_ones=pair_ones, hT=hT, ft=ft, v_skew=v_skew, loads=len(loads))


def stage1(nc, z, con, w):
    S, hT, ft, v_skew, tiny, pair, pair_ones = (w[k] for k in ("S", "hT", "ft", "v_skew", "tiny", "pair", "pair_ones"))
    with nc.Block() as block:
        @block.vector
        def _(dve):
            dve.memset(hT[:, 0:1], 0.0).then_inc(S.prep, 1)
            dve.memset(ft[0:1, 0, D // 2:D], 0.0).then_inc(S.prep, 1)
            dve.memset(v_skew[64:128, :, 0, :], 0.0).then_inc(S.prep, 1)
            dve.memset(tiny[:, :], TINY).then_inc(S.prep, 1)
            for h in range(2):
                dve.memset(pair[h * DH:(h + 1) * DH, h:h + 1], 1.0).then_inc(S.prep, 1)
                dve.memset(pair[h * DH:(h + 1) * DH, 1 - h:2 - h], 0.0).then_inc(S.prep, 1)
                for g in range(2):
                    dve.memset(pair_ones[h * DH:(h + 1) * DH, g * DH:(g + 1) * DH], float(h == g)).then_inc(S.prep, 1)
            dve.wait_ge(S.load, w["loads"] * 16)
            dve.tensor_copy(w["mask"][:, :], w["mask_f"][:, :]).then_inc(S.prep, 1)
            dve.tensor_copy(w["ident16"][:, :], con["ident"]).then_inc(S.prep, 1)
            for l in range(LAYERS):
                for i in range(4):
                    dve.tensor_scalar(w["tab"][:, l, i, :], w["base"][:, i, :], w["gain"][:, l, i:i + 1], None,
                                      ALU.mult).then_inc(S.tab, 1)
    for l in range(LAYERS):
        weights = {k: w[k] for k in ("mask", "ident16", "tiny", "pair", "pair_ones", "hT", "ft", "v_skew")}
        weights.update({k: w[k][:, l] for k in ("wqk", "wv", "wo", "w2", "b2", "up", "tab")})
        stage1_layer(nc, f"l{l}", z, con, weights)


def stage1_layer(nc, tag, z, con, w):
    with ExitStack() as ctx:
        sb = lambda n, s, t=F32: ctx.enter_context(nc.sbuf_tensor(f"{tag}_{n}", s, t))
        pb = lambda n, s: ctx.enter_context(nc.psum_tensor(f"{tag}_{n}", s, F32))
        S = semaphores(nc, ctx, tag, "own zb zT hT hT_half free0 free1 proj vps sq ss ln rn rotC rotS sum tn v "
                  "sim0 sim1 max0 max1 exp0 exp1 rin0 rin1 pn0 pn1 pt0 pt1 PT0 PT1 av oT wo z_att shift fst fvar frs fn "
                  "fnt fnT up gelu hid down z_ffn skew0 skew1 clip mraw gate value")
        hT, ft, up, tab, v_skew = w["hT"], w["ft"], w["up"], w["tab"], w["v_skew"]
        zb = sb("zb", [P, TILES, D])
        sq, rk = sb("sq", [P, 2, SEQ]), sb("rk", [P, SEQ])
        rq, rqc = sb("rq", [P, 2 * TILES]), sb("rqc", [P, TILES, 2])
        rc, rs = sb("rc", [P, 2, SEQ]), sb("rs", [P, 2, SEQ])
        qkT = sb("qkT", [P, 2, SEQ])
        v = sb("v", [P, 2, TILES, P])
        mraw, nmax, rsum, rinv = (sb(n, [P, 2, TILES]) for n in ("mraw", "nmax", "rsum", "rinv"))
        prob = sb("prob", [P, 2, TILES, P])
        probT = sb("probT", [P, 2, SEQ])
        oT = sb("oT", [P, PAIRS, SEQ])
        fstats = sb("fstats", [P, TILES, 6])
        fmean, fdiff, frstd = (sb(n, [P, TILES]) for n in ("fmean", "fdiff", "frstd"))
        fn, fnT = sb("fn", [P, TILES, D]), sb("fnT", [P, SEQ])
        gl, hid = sb("gl", [P, KH, SEQ]), sb("hid", [P, KH, SEQ])
        psX = pb("psX", [P, 2, 2, 512])
        psN = pb("psN", [P, 512])
        psS = pb("psS", [P, 2, 512])
        psT = pb("psT", [P, 512])
        block = ctx.enter_context(nc.Block())
        free, skew = (S.free0, S.free1), (S.skew0, S.skew1)
        sim, mx, ex, rin, pn, pt, PT = ((S.sim0, S.sim1), (S.max0, S.max1), (S.exp0, S.exp1), (S.rin0, S.rin1),
                                        (S.pn0, S.pn1), (S.pt0, S.pt1), (S.PT0, S.PT1))
        is_first, is_last = (lambda n: is_at(n, 0)), (lambda n: is_at(n, BATCH - 1))
        rows = lambda t, s: t[:, bass.ds(s * TILES, TILES), :]

        @block.sync
        def _(sp):
            sp.dma_start(zb[:, :, :], rows(z, 0)).then_inc(S.zb, 16)

            def turn(n):
                if not is_last(n):
                    ahead = (n + 1) * TILES if isinstance(n, int) else sp.snap((n + 1) * TILES, min_val=0, max_val=NT - TILES)
                    sp.wait_ge(S.zT, n + 1)
                    sp.dma_start(zb[:, :, :], z[:, bass.ds(ahead, TILES), :]).then_inc(S.zb, 16)
                if not is_first(n):
                    shift_tokens(n - 1)
                for hp in range(PAIRS):
                    if not (is_last(n) and hp == PAIRS - 1):
                        skew_v(n * PAIRS + (hp + 1), (hp + 1) % 2)

            def shift_tokens(s):
                tile = s * TILES if isinstance(s, int) else sp.snap(s * TILES, min_val=0, max_val=NT - TILES)
                h = D // 2
                sp.wait_ge(S.z_att, s + 1)
                sp.dma_start(ft[:, :, 0:h], z[:, bass.ds(tile, TILES), 0:h]).then_inc(S.shift, 16)
                sp.dma_start(ft[1:P, :, h:D], z[0:P - 1, bass.ds(tile, TILES), h:D]).then_inc(S.shift, 16)
                sp.dma_start(ft[0:1, 1:TILES, h:D], z[P - 1:P, bass.ds(tile, TILES - 1), h:D]).then_inc(S.shift, 16)

            def skew_v(k, q):
                sp.wait_ge(S.v, k + 1)
                sp.dma_start(v_skew[0:64, q, :, :], v[0:64, q, :, :]).then_inc(skew[q], 16)
                sp.dma_start(v_skew[64:128, q, 1:TILES, :], v[64:128, q, 0:TILES - 1, :]).then_inc(skew[q], 16)

            skew_v(0, 0)
            layer_turns(sp, turn)
            shift_tokens(BATCH - 1)

        @block.tensor
        def _(pe):
            def transposes(bank, src):
                for j in range(TILES):
                    last = pe.transpose(bank[:, j * P:(j + 1) * P], src(j), con["ident"])
                return last

            def take(n, u):
                s, before = slot(n, u)
                pe.wait_ge(free[s], before + 1)
                return psX[:, s, :, :]

            def absent(n, u):
                take(n, u)
                pe.nop().then_inc(free[slot(n, u)[0]], 1)

            def transpose_z(n):
                if is_at(n, 0):
                    pe.wait_ge(S.zb, 16)
                else:
                    pe.wait_ge(S.ln, 8 * n + 1)
                    pe.wait_ge(S.zb, n * 16 + 16)
                transposes(psN, lambda j: zb[:, j, :]).then_inc(S.zT, 1)

            def project(n, u, k, hp, c):
                ps = take(n, u)
                for i in range(2):
                    last = pe.matmul(ps[:, i, :], w["wqk"][:, hp, 2 * c + i, :], hT[:, 0:SEQ], start=True, stop=True)
                last.then_inc(S.proj, 1)

            def project_v(n, u, k, hp):
                ps = take(n, u)
                for j in range(TILES):
                    last = pe.matmul(ps[:, 0, j * P:(j + 1) * P], hT[:, j * P:(j + 1) * P], w["wv"][:, hp, :],
                                     start=True, stop=True)
                last.then_inc(S.vps, 1)

            def sum_squares(k, c):
                pe.wait_ge(S.sq, 2 * k + (c + 1))
                pe.wait_ge(S.ln, 2 * k + (c + 1))
                if c == 0:
                    for j in range(TILES):
                        last = pe.matmul(psN[:, 2 * j:2 * j + 2], sq[:, 0, j * P:(j + 1) * P], w["pair"][:, :],
                                         start=True, stop=True, skip_group_check=True)
                else:
                    last = pe.matmul(psN[:, :], w["pair_ones"][:, :], sq[:, 1, :], start=True, stop=True)
                last.then_inc(S.ss, 1)

            def scores(k, h):
                if h == 0:
                    pe.wait_ge(S.oT, k + 1)
                pe.matmul(psS[:, h, :], w["ident16"][:, :], w["mask"][:, :], start=True, stop=False, skip_group_check=True)
                r = slice(h * DH, (h + 1) * DH)
                for j in range(TILES):
                    o, m = j * P, j * P + WINDOW
                    pe.matmul(psS[0:64, h, o:m], qkT[r, 0, o:m], qkT[r, 1, o:m], start=False, stop=True, skip_group_check=True)
                    if j > 0:
                        pe.matmul(psS[0:64, h, m:o + P], qkT[r, 0, o:m], qkT[r, 1, o - WINDOW:o],
                                  start=False, stop=True, skip_group_check=True)
                    last = pe.matmul(psS[64:128, h, o:o + P], qkT[r, 0, m:o + P], qkT[r, 1, o:o + P],
                                     start=False, stop=True, skip_group_check=True)
                last.then_inc(sim[h], 1)

            def transpose_probabilities(k, h):
                pe.wait_ge(pn[h], k + 1)
                transposes((psT, psS[:, 1, :])[h], lambda j: prob[:, h, j, :]).then_inc(pt[h], 1)

            def outputs(n, k, hp):
                pe.wait_ge(skew[hp % 2], n * 64 + (hp // 2 + 1) * 32)
                for h in range(2):
                    pe.wait_ge(PT[h], k + 1)
                    r = slice(h * DH, (h + 1) * DH)
                    for j in range(TILES):
                        for odd in range(2):
                            o = j * P + odd * WINDOW
                            last = pe.matmul(psS[r, 0, o:o + WINDOW], (v, v_skew)[1 - odd][:, hp % 2, j, r], probT[:, h, o:o + WINDOW],
                                             start=True, stop=True, skip_group_check=True)
                last.then_inc(S.av, 1)

            def project_out(n, u, s):
                ps = take(n, u)
                pe.wait_ge(S.oT, s * PAIRS + (PAIRS + 1))
                for j in range(TILES):
                    for hp in range(PAIRS):
                        last = pe.matmul(ps[:, 0, j * P:(j + 1) * P], oT[:, hp, j * P:(j + 1) * P], w["wo"][:, hp, :],
                                         start=hp == 0, stop=hp == PAIRS - 1)
                last.then_inc(S.wo, 1)

            def transpose_normed(n, u, s):
                ps = take(n, u)
                pe.wait_ge(S.fn, s + 1)
                transposes(ps[:, 0, :], lambda j: fn[:, j, :]).then_inc(S.fnt, 1)

            def up_chunk(n, u, s, c):
                ps = take(n, u)
                pe.wait_ge(S.fnT, s + 1)
                for g in range(2):
                    o = (g * KH + c) * P
                    last = pe.matmul(ps[:, g, :], up[:, o:o + P], fnT[:, :], start=True, stop=True)
                last.then_inc(S.up, 1)

            def down(n, u, s):
                ps = take(n, u)
                pe.wait_ge(S.hid, s + 1)
                for j in range(TILES):
                    o = ps[:, 0, j * P:(j + 1) * P]
                    for c in range(KH):
                        pe.matmul(o, hid[:, c, j * P:(j + 1) * P], w["w2"][:, c, :], start=c == 0, stop=False)
                    last = pe.matmul(o, con["ones"][0:1, :], w["b2"], start=False, stop=True)
                last.then_inc(S.down, 1)

            def body(n, hp):
                k = n * PAIRS + hp
                u = FIRST_USE[hp]
                ffn = (lambda f, u, *a: absent(n, u)) if is_first(n) else (lambda f, u, *a: f(n, u, n - 1, *a))
                ahead = not (is_last(n) and hp == PAIRS - 1)
                nxt = (hp + 1) % PAIRS
                extra = (1, 0, 1, 0)[hp]
                if ahead:
                    if nxt == 0:
                        pe.wait_ge(S.hT, n + 2)
                    project(n, u, k + 1, nxt, 0)
                pe.wait_ge(S.tn, k + 1)
                scores(k, 0)
                scores(k, 1)
                if hp == 0:
                    ffn(project_out, u + 1)
                if hp == 2:
                    ffn(up_chunk, u + 1, 0)
                if ahead:
                    project(n, u + extra + 1, k + 1, nxt, 1)
                    sum_squares(k + 1, 0)
                    project_v(n, u + extra + 2, k + 1, nxt)
                transpose_probabilities(k, 0)
                if ahead:
                    sum_squares(k + 1, 1)
                if hp == 2:
                    ffn(up_chunk, u + 4, 1)
                    if not is_last(n):
                        transpose_z(n + 1)
                transpose_probabilities(k, 1)
                if hp == 2:
                    ffn(up_chunk, u + 5, 2)
                outputs(n, k, hp)
                if hp == 1:
                    ffn(transpose_normed, u + 3)
                if hp == 3:
                    ffn(down, DOWN_LAST if is_last(n) else u + 3)

            def turn(n):
                for hp in range(PAIRS):
                    body(n, hp)

            transpose_z(0)
            pe.wait_ge(S.hT, 1)
            project(0, -3, 0, 0, 0)
            project(0, -2, 0, 0, 1)
            sum_squares(0, 0)
            project_v(0, -1, 0, 0)
            sum_squares(0, 1)
            layer_turns(pe, turn)
            n, s = BATCH - 1, BATCH - 1
            project_out(n, WO_TAIL, s)
            transpose_normed(n, NORMED_TAIL, s)
            for c in range(KH):
                up_chunk(n, UP_TAIL[c], s, c)
            down(n, DOWN_TAIL, s)

        @block.scalar
        def _(act):
            def load_functions():
                act.add_instruction(mybir.InstLoadActFuncSet(name=nc.get_next_instruction_name(), act_func_set_id=LN_EXP_SET,
                                                             engine=mybir.EngineType.Activation, ins=[], outs=[]))

            def square(n, u, k, c):
                act.wait_ge(S.proj, 2 * k + (c + 1))
                act.activation(sq[:, c, :], psX[:, slot(n, u)[0], 0, :], ACT.Square).then_inc(S.sq, 1)

            def inverse_norm(k, c):
                act.wait_ge(S.ss, 2 * k + (c + 1))
                r, n = (rq[:, :], 2 * TILES) if c == 0 else (rk[:, :], SEQ)
                act.activation(r, psN[:, 0:n], ACT.Ln, bias=w["tiny"][:, :]).then_inc(S.ln, 1)
                act.wait_ge(S.ln, 2 * k + (c + 2))
                act.activation(r, r, ACT.Exp, scale=-0.5).then_inc(S.rn, 1)

            def exponentials(k, h):
                act.wait_ge(mx[h], k + 1)
                for j in range(TILES):
                    last = act.activation(prob[:, h, j, :], psS[:, h, j * P:(j + 1) * P], ACT.Exp,
                                          bias=nmax[:, h, j:j + 1], scale=rqc[:, j, h:h + 1], accum_out=rsum[:, h, j:j + 1])
                last.then_inc(ex[h], 1)

            def copy_probabilities(k, h):
                act.wait_ge(pt[h], k + 1)
                act.copy(probT[:, h, :], psT[:, :] if h == 0 else psS[:, 1, :]).then_inc(PT[h], 1)

            def copy_z(n):
                act.wait_ge(S.zT, n + 1)
                act.copy(hT[0:64, 0:SEQ], psN[0:64, :]).then_inc(S.hT_half, 1)
                act.copy(hT[64:128, 1:1 + SEQ], psN[64:128, :]).then_inc(S.hT, 1)

            def gate_chunk(n, u, s, c):
                act.wait_ge(S.up, s * KH + (c + 1))
                if c == 0 and not is_at(s, 0):
                    act.wait_ge(S.hid, s)
                act.activation(gl[:, c, :], psX[:, slot(n, u)[0], 1, :], ACT.Identity,
                               bias=up[:, W1C + KH + c:W1C + KH + c + 1]).then_inc(S.gate, 1)

            def gelu(s):
                act.wait_ge(S.gate, s * KH + KH)
                act.activation(gl[:, :, :], gl[:, :, :], ACT.Gelu).then_inc(S.gelu, 1)
                load_functions()

            def scale_normed(n, u, s):
                sl = slot(n, u)[0]
                act.wait_ge(S.fnt, s + 1)
                act.activation(fnT[:, :], psX[:, sl, 0, :], ACT.Identity, bias=up[:, UPC - 1:UPC],
                               scale=up[:, UPC - 2:UPC - 1]).then_inc(S.fnT, 1)
                act.wait_ge(S.fnT, s + 1)
                act.nop().then_inc(free[sl], 1)

            def body(n, hp):
                k = n * PAIRS + hp
                u, extra = FIRST_USE[hp], (1, 0, 1, 0)[hp]
                ahead = not (is_last(n) and hp == PAIRS - 1)
                ffn = not is_first(n)
                if ahead:
                    square(n, u, k + 1, 0)
                if hp == 3 and ffn:
                    gelu(n - 1)
                exponentials(k, 0)
                if hp == 2 and ffn:
                    gate_chunk(n, u + 1, n - 1, 0)
                if ahead:
                    square(n, u + extra + 1, k + 1, 1)
                exponentials(k, 1)
                if ahead:
                    inverse_norm(k + 1, 0)
                copy_probabilities(k, 0)
                if ahead:
                    inverse_norm(k + 1, 1)
                if hp == 2 and ffn:
                    gate_chunk(n, u + 4, n - 1, 1)
                if hp == 2 and not is_last(n):
                    act.wait_ge(S.vps, k + 2)
                    copy_z(n + 1)
                copy_probabilities(k, 1)
                if hp == 2 and ffn:
                    gate_chunk(n, u + 5, n - 1, 2)
                act.wait_ge(S.av, k + 1)
                if hp == 0 and ffn:
                    act.wait_ge(S.wo, n)
                act.copy(oT[:, hp, :], psS[:, 0, :]).then_inc(S.oT, 1)
                if hp == 1 and ffn:
                    scale_normed(n, u + 3, n - 1)

            def turn(n):
                for hp in range(PAIRS):
                    body(n, hp)

            lead(act, S.ln, 1)
            lead(act, S.exp0, 1)
            lead(act, S.exp1, 1)
            lead(act, S.oT, 1)
            load_functions()
            copy_z(0)
            square(0, -3, 0, 0)
            square(0, -2, 0, 1)
            inverse_norm(0, 0)
            inverse_norm(0, 1)
            layer_turns(act, turn)
            n, s = BATCH - 1, BATCH - 1
            scale_normed(n, NORMED_TAIL, s)
            for c in range(KH):
                gate_chunk(n, UP_TAIL[c], s, c)
            gelu(s)

        @block.gpsimd
        def _(pool):
            def add_rotated(k, c):
                pool.wait_ge(S.rotC, 2 * k + (c + 1))
                pool.wait_ge(S.rotS, 2 * k + (c + 1))
                if c == 0 and not is_at(k, 0):
                    pool.wait_ge(sim[1], k)
                pool.tensor_tensor((qkT if c == 0 else rc)[:, c, :], rc[:, c, :], rs[:, c, :], ALU.add).then_inc(S.sum, 1)

            def scale_probabilities(k, h):
                pool.wait_ge(rin[h], k + 1)
                pool.tensor_tensor(prob[:, h, :, :], prob[:, h, :, :], spread(rinv[:, h, :], 2, P),
                                   ALU.mult).then_inc(pn[h], 1)

            def turn(n):
                for hp in range(PAIRS):
                    k = n * PAIRS + hp
                    ahead = not (is_last(n) and hp == PAIRS - 1)
                    if ahead:
                        add_rotated(k + 1, 0)
                    scale_probabilities(k, 0)
                    scale_probabilities(k, 1)
                    if ahead:
                        add_rotated(k + 1, 1)
                    if hp == 0 and not is_first(n):
                        root(n - 1)

            def root(s):
                pool.wait_ge(S.fvar, s + 1)
                pool.tensor_tensor(frstd[:, :], frstd[:, :], con["mhalf"][:, 0:TILES], ALU.pow).then_inc(S.frs, 1)

            add_rotated(0, 0)
            add_rotated(0, 1)
            layer_turns(pool, turn)
            root(BATCH - 1)

        @block.vector
        def _(dve):
            own = Order(dve, S.own, MOMENTS)

            def rotate(n, u, k, c):
                s, before = slot(n, u)
                dve.wait_ge(S.sq, 2 * k + (c + 1))
                dve.tensor_tensor(rc[:, c, :], psX[:, s, 0, :], tab[:, 2 * c, :], ALU.mult).then_inc(S.rotC, 1)
                dve.tensor_tensor(rs[:, c, :], psX[:, s, 1, :], tab[:, 2 * c + 1, :], ALU.mult).then_inc(S.rotS, 1)
                dve.wait_ge(S.rotC, 2 * k + (c + 1))
                dve.wait_ge(S.rotS, 2 * k + (c + 1))
                dve.nop().then_inc(free[s], 1)

            def clip_q(k):
                dve.wait_ge(S.rn, 2 * k + 1)
                step(dve, dve.tensor_scalar(rqc[:, :, :], rq[:, :].rearrange("p (j h) -> p j h", h=2), 1e12, None, ALU.min),
                     S.clip, k + 1)

            def norm_k(k):
                dve.wait_ge(S.rn, 2 * k + 2)
                dve.wait_ge(S.sum, 2 * k + 2)
                step(dve, dve.scalar_tensor_tensor(out=qkT[:, 1, :], in0=rk[:, :], scalar=1e12, in1=rc[:, 1, :],
                                                   op0=ALU.min, op1=ALU.mult), S.tn, k + 1)

            def copy_v(n, u, k, hp):
                s, before = slot(n, u)
                dve.wait_ge(S.vps, k + 1)
                if not is_at(k, 1):
                    dve.wait_ge(S.av, k - 1)
                dve.tensor_copy(v[:, hp % 2, :, :].rearrange("p j f -> p (j f)"), psX[:, s, 0, :]).then_inc(S.v, 1)
                dve.wait_ge(S.v, k + 1)
                dve.nop().then_inc(free[s], 1)

            def row_max(k, h):
                dve.wait_ge(sim[h], k + 1)
                step(dve, dve.tensor_reduce(mraw[:, h, :], psS[:, h, :].rearrange("p (j c) -> p j c", j=TILES), AX.X,
                                            ALU.max, negate=True), S.mraw, 2 * k + (h + 1))
                dve.tensor_tensor(nmax[:, h, :], mraw[:, h, :], rqc[:, :, h], ALU.mult).then_inc(mx[h], 1)

            def invert(k, h):
                dve.wait_ge(ex[h], k + 2)
                dve.reciprocal(rinv[:, h, :], rsum[:, h, :]).then_inc(rin[h], 1)

            def add_to_z(n, u, s, made, sem):
                sl = slot(n, u)[0]
                dve.wait_ge(made, s + 1)
                step(dve, dve.tensor_tensor(rows(z, s), rows(z, s), psX[:, sl, 0, :].rearrange("p (j d) -> p j d", j=TILES),
                                            ALU.add), sem, s + 1)
                dve.nop().then_inc(free[sl], 1)

            def statistics(s):
                own.start(s)
                dve.wait_ge(S.shift, s * 48 + 48)
                for j in range(TILES):
                    dve.bn_stats(fstats[:, j, :], ft[:, j, :]).then_inc(S.fst, 1)
                dve.wait_ge(S.fst, s * TILES + TILES)
                moments(dve, own, fstats, fmean, fdiff, frstd)
                dve.tensor_scalar(frstd[:, :], frstd[:, :], EPS, None, ALU.add).then_inc(S.fvar, 1)
                own.end()

            def norm(s):
                dve.wait_ge(S.frs, s + 1)
                for j in range(TILES):
                    last = dve.tensor_scalar(fn[:, j, :], ft[:, j, :], fmean[:, j:j + 1], frstd[:, j:j + 1],
                                             ALU.subtract, ALU.mult)
                last.then_inc(S.fn, 1)

            def value_chunk(n, u, s, c):
                sl = slot(n, u)[0]
                dve.wait_ge(S.gate, s * KH + (c + 1))
                if c == 0 and not is_at(s, 0):
                    dve.wait_ge(S.down, s)
                step(dve, dve.tensor_scalar(hid[:, c, :], psX[:, sl, 0, :], up[:, W1C + c:W1C + c + 1], None, ALU.add),
                     S.value, s * KH + (c + 1))
                dve.nop().then_inc(free[sl], 1)

            def apply_gates(s):
                dve.wait_ge(S.gelu, s + 1)
                dve.tensor_tensor(hid[:, :, :], hid[:, :, :], gl[:, :, :], ALU.mult).then_inc(S.hid, 1)

            def body(n, hp):
                k = n * PAIRS + hp
                u, extra = FIRST_USE[hp], (1, 0, 1, 0)[hp]
                ahead = not (is_last(n) and hp == PAIRS - 1)
                ffn = not is_first(n)
                if ahead:
                    rotate(n, u, k + 1, 0)
                row_max(k, 0)
                row_max(k, 1)
                if hp == 0 and ffn:
                    add_to_z(n, u + 1, n - 1, S.wo, S.z_att)
                invert(k, 0)
                if hp == 2 and ffn:
                    value_chunk(n, u + 1, n - 1, 0)
                if ahead:
                    rotate(n, u + extra + 1, k + 1, 1)
                invert(k, 1)
                if hp == 3 and ffn:
                    apply_gates(n - 1)
                if ahead:
                    copy_v(n, u + extra + 2, k + 1, (hp + 1) % PAIRS)
                if hp == 0 and ffn:
                    statistics(n - 1)
                if hp == 1 and ffn:
                    norm(n - 1)
                if ahead:
                    clip_q(k + 1)
                    norm_k(k + 1)
                if hp == 2 and ffn:
                    value_chunk(n, u + 4, n - 1, 1)
                    value_chunk(n, u + 5, n - 1, 2)
                if hp == 3 and ffn:
                    add_to_z(n, DOWN_LAST if is_last(n) else u + 3, n - 1, S.down, S.z_ffn)

            def turn(n):
                for hp in range(PAIRS):
                    body(n, hp)

            lead(dve, S.free0, 1)
            lead(dve, S.free1, 1)
            rotate(0, -3, 0, 0)
            rotate(0, -2, 0, 1)
            clip_q(0)
            dve.wait_ge(S.vps, 1)
            dve.tensor_copy(v[:, 0, :, :].rearrange("p j f -> p (j f)"), psX[:, 1, 0, :]).then_inc(S.v, 1)
            dve.wait_ge(S.v, 1)
            dve.nop().then_inc(free[1], 1)
            norm_k(0)
            layer_turns(dve, turn)
            n, s = BATCH - 1, BATCH - 1
            add_to_z(n, WO_TAIL, s, S.wo, S.z_att)
            statistics(s)
            norm(s)
            for c in range(KH):
                value_chunk(n, UP_TAIL[c], s, c)
            apply_gates(s)
            add_to_z(n, DOWN_TAIL, s, S.down, S.z_ffn)


def layout1(a, np):
    f = np.float32
    pad = lambda w, n: np.concatenate([w, np.zeros(w.shape[:-1] + (n - w.shape[-1],), f)], -1)
    two = lambda w: np.concatenate([pad(w[..., :HIDDEN], KH * P), pad(w[..., HIDDEN:], KH * P)], -1)
    w1, b1 = two(a["L0_ffn_w1"]), two(a["L0_ffn_b1"])
    w2 = np.concatenate([a["L0_ffn_w2"], np.zeros((LAYERS, KH * P - HIDDEN, D), f)], 1)
    half = np.arange(0, DH, 2, dtype=f)
    inv = (1.0 / 10000.0 ** (half / f(DH))).astype(f)
    t = np.arange(SEQ, dtype=f)
    freqs = t[:, None] * inv[None, :]
    base = ((half + f(0.4 * DH)) / f(1.4 * DH)).astype(f)
    decay = base[None, :] ** ((t - SEQ // 2) / f(WINDOW // 2))[:, None]
    freqs, decay = np.concatenate([freqs, freqs], 1), np.concatenate([decay, decay], 1)
    sign = np.concatenate([-np.ones(DH // 2, f), np.ones(DH // 2, f)])
    cos, sin = np.cos(freqs), np.sin(freqs) * sign
    tab = np.stack([cos * decay * 8, sin * decay * 8, cos / decay, sin / decay]).astype(f)
    tab = np.concatenate([tab, tab], -1).transpose(2, 0, 1)
    gain = np.stack([a["L0_ffn_q_scale"], a["L0_ffn_k_scale"]], 1)
    gain = np.stack([gain, np.roll(gain, DH // 2, -1)], 2).reshape(LAYERS, 4, DH)
    gain = np.concatenate([gain, gain], -1).transpose(2, 0, 1)
    i, c = np.arange(P)[:, None] % WINDOW, np.arange(P)[None, :] % WINDOW
    own = (np.arange(P)[:, None] < WINDOW) == (np.arange(P)[None, :] < WINDOW)
    mask = np.tile(np.where(np.where(own, c <= i, c >= i), 0, MASKED).astype(f), (1, TILES))
    mask[:WINDOW, WINDOW:P] = MASKED
    wqkv = a["L0_ffn_wqkv"].reshape(LAYERS, D, 3, HEADS, DH)
    qk = np.stack([wqkv[:, :, 0:2], np.roll(wqkv[:, :, 0:2], DH // 2, -1)], 3)
    qk = qk.reshape(LAYERS, D, 4, PAIRS, P).transpose(1, 0, 3, 2, 4)
    return {
        "wqk": qk,
        "wv": wqkv[:, :, 2].reshape(LAYERS, D, PAIRS, P).transpose(1, 0, 2, 3),
        "wo": a["L0_ffn_wo"].reshape(LAYERS, PAIRS, P, D).transpose(2, 0, 1, 3),
        "w2": w2.reshape(LAYERS, KH, P, D).transpose(2, 0, 1, 3),
        "b2": a["L0_ffn_b2"][None],
        "up": np.concatenate([w1.transpose(1, 0, 2), b1.reshape(LAYERS, 2 * KH, P).transpose(2, 0, 1),
                              a["L0_ffn_ln_g"].T[:, :, None], a["L0_ffn_ln_b"].T[:, :, None]], 2),
        "rot_base": tab,
        "qk_gain": gain,
        "mask": mask,
    }


INNER, SSTATE, SHEADS, HD, TAPS = 2 * D, 64, 4, 64, 4
GROUPS2 = 4


def sequence_turns(eng, turn):
    turn(0, 0)
    with eng.Fori(0, (BATCH - 2) // 2) as i:
        turn(2 * i + 1, 1)
        turn(2 * i + 2, 0)
    turn(BATCH - 1, 1)


def stage2(nc, xn_tok, y_tok, con, dram):
    with ExitStack() as ctx:
        sb = lambda n, s: ctx.enter_context(nc.sbuf_tensor(f"s2_{n}", s, F32))
        S = semaphores(nc, ctx, "s2", "load prep xin0 xin1 xt xT dtp u absu ex ln dt a prod evac taps conv silu "
                  "xtok Xdt Btok R seg cum G E dec Gm M Cdec Xs Y St decayed state skip yg sqr ms rv rs out y")
        WC = 2 * INNER + 2 * SSTATE + SHEADS
        win = sb("win", [P, WC])
        small = sb("small", [P, GROUPS2 * (TAPS + 1) + 2 * SHEADS + 2 + 2])
        cw = small[:, 0:GROUPS2 * (TAPS + 1)].rearrange("p (g t) -> p g t", g=GROUPS2)
        o = GROUPS2 * (TAPS + 1)
        dt_bias, Alog, Dcol, norm_w = (small[:, o:o + 4], small[:, o + 4:o + 8], small[:, o + 8:o + 10], small[:, o + 10:o + 12])
        wout = sb("wout", [P, 2, D])
        tri, strict = sb("tri", [P, P]), sb("strict", [P, P])
        A = sb("A", [P, SHEADS])
        xin = sb("xin", [P, 2, TILES, D])
        xT = sb("xT", [P, SEQ])
        craw = sb("craw", [P, GROUPS2, TAPS - 1 + SEQ])
        acc = sb("acc", [P, GROUPS2, SEQ])
        xc = sb("xc", [P, 2, GROUPS2, SEQ])
        zs = sb("zs", [P, 2, 2, SEQ])
        u, au = sb("u", [P, TILES, SHEADS]), sb("au", [P, TILES, SHEADS])
        dt, a = sb("dt", [P, 2, TILES, SHEADS]), sb("a", [P, 2, TILES, SHEADS])
        Xdt, Xs = sb("Xdt", [P, SHEADS, HD]), sb("Xs", [P, SHEADS, HD])
        Btok = sb("Btok", [P, SSTATE])
        R, E, M = (sb(n, [P, SHEADS, P]) for n in ("R", "E", "M"))
        Gm = sb("Gm", [P, P])
        dec, Cdec = sb("dec", [64, SHEADS, P]), sb("Cdec", [64, SHEADS, P])
        state = sb("state", [64, 2, SHEADS, HD])
        yg, ysq = sb("yg", [P, 2, SEQ]), sb("ysq", [P, 2, SEQ])
        rs = sb("rs", [P, TILES])

        with nc.Block() as block:
            @block.sync
            def _(sp):
                for dst, name in ((win[:, :], "m_in"), (small[:, :], "m_small"), (wout[:, :, :], "m_out"),
                                  (tri[:, :], "m_tri"), (strict[:, :], "m_strict")):
                    sp.dma_start(dst, dram[name]).then_inc(S.load, 16)

            @block.scalar
            def _(act):
                act.wait_ge(S.load, 5 * 16)
                act.activation(A[:, :], Alog, ACT.Exp).then_inc(S.prep, 1)

            @block.vector
            def _(dve):
                dve.memset(craw[:, :, 0:TAPS - 1], 0.0).then_inc(S.decayed, 1)
                dve.wait_ge(S.load, 5 * 16)
                for h in range(2):
                    dve.tensor_scalar(wout[:, h, :], wout[:, h, :], norm_w[:, h:h + 1], None, ALU.mult).then_inc(S.decayed, 1)
                dve.wait_ge(S.prep, 1)
                dve.tensor_scalar(A[:, :], A[:, :], -1.0, None, ALU.mult).then_inc(S.decayed, 1)

        pb = lambda n, s: ctx.enter_context(nc.psum_tensor(f"s2_{n}", s, F32))
        psA = pb("psA", [P, 2, 512])
        psX = pb("psX", [P, 512])
        psG = pb("psG", [P, 512])
        psE, psC = pb("psE", [P, 512]), pb("psC", [P, 512])
        psY = pb("psY", [P, 2, 512])
        ST0 = P
        psO, psM = psA[:, 0, :], psA[:, 1, :]
        block = ctx.enter_context(nc.Block())
        PROD = [(2 * INNER, 64), (2 * INNER + SSTATE, 64), (INNER, P), (INNER + P, P), (0, P), (P, P)]
        rows = lambda g: slice(0, PROD[g][1])
        xins = S.xin0, S.xin1

        @block.sync
        def _(sp):
            with sp.Fori(0, BATCH // 2) as i:
                for q in range(2):
                    b = 2 * i + q
                    sp.wait_ge(S.xt, b + 1)
                    sp.dma_start(xin[:, q, :, :], xn_tok[:, bass.ds(b * TILES, TILES), :]).then_inc(xins[q], 16)

        @block.tensor
        def _(pe):
            def front(b, q, half_b, part):
                if part == 0:
                    pe.wait_ge(xins[q], half_b * 16 + 16)
                    pe.wait_ge(S.evac, b * 6 + 1)
                    if not is_at(b, 0) and not is_at(b, 1):
                        pe.wait_ge(S.y, b - 1)
                        pe.wait_ge(S.rv, b - 1)
                    for j in range(TILES):
                        last = pe.transpose(psA[:, 0, j * P:(j + 1) * P], xin[:, q, j, :], con["ident"])
                    last.then_inc(S.xt, 1)
                    pe.wait_ge(S.xT, b + 1)
                    pe.wait_ge(S.evac, b * 6 + 2)
                    for j in range(TILES):
                        last = pe.matmul(psA[:, 1, j * SHEADS:(j + 1) * SHEADS], xT[:, j * P:(j + 1) * P],
                                         win[:, WC - SHEADS:WC], start=True, stop=True, skip_group_check=True)
                    last.then_inc(S.dtp, 1)
                    return
                for g in (2 * part - 2, 2 * part - 1):
                    col, m = PROD[g]
                    pe.wait_ge(S.evac, b * 6 + (g + 1))
                    if g == 1:
                        pe.wait_ge(S.u, b + 1)
                    pe.matmul(psA[0:m, g % 2, :], win[:, col:col + m], xT[:, :], start=True, stop=True).then_inc(S.prod, 1)

            def close(s):
                ahead = s if is_at(s, BATCH - 1) else s + 1
                pe.wait_ge(S.evac, ahead * 6 + 8)
                pe.wait_ge(S.sqr, s + 1)
                for j in range(TILES):
                    for h in range(2):
                        last = pe.matmul(psM[:, j:j + 1], ysq[:, h, j * P:(j + 1) * P], con["ones"][:, 0:1],
                                         start=h == 0, stop=h == 1, skip_group_check=True)
                last.then_inc(S.ms, 1)
                for j in range(TILES):
                    for h in range(2):
                        last = pe.matmul(psO[:, j * P:(j + 1) * P], yg[:, h, j * P:(j + 1) * P], wout[:, h, :],
                                         start=h == 0, stop=h == 1)
                last.then_inc(S.out, 1)

            def ahead(b, q, part):
                if not is_at(b, BATCH - 1):
                    front(b + 1, 1 - q, (b + 1 - (1 - q)) // 2 if isinstance(b, int) else (b + q) >> 1, part)

            def back(b, q):
                for c in range(TILES):
                    k = b * TILES + c
                    t = slice(c * P, (c + 1) * P)
                    if c == 0:
                        pe.wait_ge(S.silu, b * 4 + 8)
                    pe.wait_ge(S.Xdt, k + 1)
                    pe.wait_ge(S.Btok, k + 1)
                    for h in range(2):
                        pe.transpose(psX[:, h * P:(h + 1) * P], xc[:, q, 2 + h, t], con["ident"])
                    pe.transpose(psX[:, 2 * P:2 * P + SSTATE], xc[0:64, q, 0, t], con["ident"][0:64, 0:64]).then_inc(S.xtok, 1)
                    pe.wait_ge(S.state, k + 1)
                    pe.matmul(psG[:, 0:P], xc[0:64, q, 0, t], xc[0:64, q, 1, t], start=True, stop=True,
                              skip_group_check=True).then_inc(S.G, 1)
                    pe.wait_ge(S.R, k + 1)
                    pe.wait_ge(S.E, k + 1)
                    pe.matmul(psE[:, :], strict[:, :], R[:, :, :], start=True, stop=True).then_inc(S.seg, 1)
                    pe.wait_ge(S.dec, k + 1)
                    pe.matmul(psC[0:64, :], con["ones"][:, 0:64], R[:, :, :], start=True, stop=True).then_inc(S.cum, 1)
                    if c == 0 and not is_at(b, 0):
                        close(b - 1)
                    if c:
                        ahead(b, q, c)
                    if c < TILES - 1:
                        pe.wait_ge(S.Xs, k + 2)
                        pe.wait_ge(S.Btok, k + 2)
                        pe.matmul(psG[0:64, ST0:ST0 + SHEADS * HD], Btok[:, :], Xs[:, :, :], start=True, stop=True,
                                  skip_group_check=True).then_inc(S.St, 1)
                    else:
                        pe.nop().then_inc(S.St, 1)
                    if c == 0:
                        ahead(b, q, 0)
                    pe.wait_ge(S.M, k + 1)
                    pe.wait_ge(S.Cdec, k + 2)
                    if c == 0:
                        pe.wait_ge(S.yg, b + 1)
                    for h in range(SHEADS):
                        out = psY[h % 2 * 64:h % 2 * 64 + 64, h // 2, t]
                        last = pe.matmul(out, Xdt[:, h, :], M[:, h, :], start=True, stop=c == 0, skip_group_check=True)
                        if c:
                            last = pe.matmul(out, state[:, (c - 1) % 2, h, :], Cdec[:, h, :], start=False, stop=True, skip_group_check=True)
                    last.then_inc(S.Y, 1)
            lead(pe, S.xt, 2)
            lead(pe, S.cum, 1)
            lead(pe, S.St, 1)
            lead(pe, S.Y, 1)
            for part in range(4):
                front(0, 0, 0, part)
            sequence_turns(pe, back)
            close(BATCH - 1)

        @block.scalar
        def _(act):
            def load_functions():
                act.add_instruction(mybir.InstLoadActFuncSet(name=nc.get_next_instruction_name(), act_func_set_id=LN_EXP_SET,
                                                             engine=mybir.EngineType.Activation, ins=[], outs=[]))

            def front(b, q, part):
                if part == 0:
                    act.wait_ge(S.xt, b + 3)
                    act.copy(xT[:, :], psA[:, 0, :]).then_inc(S.xT, 1)
                    act.wait_ge(S.absu, b + 1)
                    step(act, act.activation(au[:, :, :], au[:, :, :], ACT.Exp, scale=-1.0), S.ex, b + 1)
                    act.activation(au[:, :, :], au[:, :, :], ACT.Ln, bias=1.0).then_inc(S.ln, 1)
                    return
                for g in (2 * part - 2, 2 * part - 1):
                    act.wait_ge(S.prod, b * 6 + (g + 1))
                    if g < GROUPS2:
                        act.copy(craw[rows(g), g, TAPS - 1:], psA[rows(g), g % 2, :]).then_inc(S.evac, 1)
                    else:
                        act.activation(zs[:, q, g - 4, :], psA[:, g % 2, :], ACT.Silu).then_inc(S.evac, 1)
                if part == 3:
                    for g in range(GROUPS2):
                        act.wait_ge(S.conv, b * 4 + (g + 1))
                        act.activation(xc[rows(g), q, g, :], acc[rows(g), g, :], ACT.Silu).then_inc(S.silu, 1)
                    load_functions()

            def back(b, q):
                for c in range(TILES):
                    k = b * TILES + c
                    act.wait_ge(S.seg, k + 1)
                    act.wait_ge(S.Xs, k + 1)
                    act.activation(E[:, :, :], psE[:, :].rearrange("p (h i) -> p h i", h=SHEADS), ACT.Exp).then_inc(S.E, 1)
                    act.wait_ge(S.cum, k + 2)
                    act.wait_ge(S.Cdec, k + 1)
                    act.wait_ge(S.state, k + 1)
                    act.activation(dec[:, :, :], psC[0:64, :].rearrange("p (h i) -> p h i", h=SHEADS), ACT.Exp).then_inc(S.dec, 1)
                    if not is_at(b, BATCH - 1):
                        front(b + 1, 1 - q, c)
                act.wait_ge(S.yg, b + 2)
                if not is_at(b, 0):
                    act.wait_ge(S.ms, b)
                act.activation(ysq[:, :, :], yg[:, :, :], ACT.Square).then_inc(S.sqr, 1)

            lead(act, S.evac, 2)
            lead(act, S.E, 1)
            lead(act, S.dec, 1)
            lead(act, S.silu, 4)
            load_functions()
            for part in range(4):
                front(0, 0, part)
            sequence_turns(act, back)

        @block.gpsimd
        def _(pool):
            def back(b, q):
                for c in range(TILES):
                    k = b * TILES + c
                    if c == 0:
                        pool.wait_ge(S.a, b + 1)
                        pool.wait_ge(S.silu, b * 4 + 8)
                    pool.wait_ge(S.cum, k + 1)
                    pool.tensor_tensor(R[:, :, :], spread(tri[:, :], 1, SHEADS), spread(a[:, q, c, :], 2, P),
                                       ALU.mult).then_inc(S.R, 1)
                    if c == 0 and not is_at(b, 0):
                        root(b - 1)
                    pool.wait_ge(S.dec, k + 2)
                    pool.wait_ge(S.Y, k + 1)
                    pool.tensor_tensor(Cdec[:, :, :], dec[:, :, :], spread(xc[0:64, q, 1, c * P:(c + 1) * P], 1, SHEADS),
                                       ALU.mult).then_inc(S.Cdec, 1)

            def root(s):
                pool.wait_ge(S.rv, s + 1)
                pool.tensor_tensor(rs[:, :], rs[:, :], con["mhalf"][:, 0:TILES], ALU.pow).then_inc(S.rs, 1)

            lead(pool, S.Cdec, 1)
            sequence_turns(pool, back)
            root(BATCH - 1)

        @block.vector
        def _(dve):
            def step_input(b):
                dve.wait_ge(S.dtp, b + 1)
                step(dve, dve.tensor_tensor(u[:, :, :], psA[:, 1, 0:TILES * SHEADS].rearrange("p (j h) -> p j h", h=SHEADS),
                                            spread(dt_bias, 1, TILES), ALU.add), S.u, b + 1)
                dve.scalar_tensor_tensor(out=au[:, :, :], in0=u[:, :, :], scalar=-1.0, in1=u[:, :, :], op0=ALU.mult,
                                         op1=ALU.max).then_inc(S.absu, 1)

            def step_sizes(b, q):
                dve.wait_ge(S.ln, b + 1)
                step(dve, dve.scalar_tensor_tensor(out=dt[:, q, :, :], in0=u[:, :, :], scalar=0.0, in1=au[:, :, :],
                                                   op0=ALU.max, op1=ALU.add), S.dt, b + 1)
                dve.tensor_tensor(a[:, q, :, :], dt[:, q, :, :], spread(A[:, :], 1, TILES), ALU.mult).then_inc(S.a, 1)

            def convolve(b, g):
                r, first = rows(g), (b * GROUPS2 + g) * (TAPS - 1)
                dve.wait_ge(S.evac, b * 6 + (g + 3))
                dve.wait_ge(S.silu, b * 4 + (g + 1))
                step(dve, dve.tensor_scalar(acc[r, g, :], craw[r, g, TAPS - 1:], cw[r, g, TAPS - 1:TAPS],
                                            cw[r, g, TAPS:TAPS + 1], ALU.mult, ALU.add), S.taps, first + 1)
                for t in range(1, TAPS):
                    ins = dve.scalar_tensor_tensor(out=acc[r, g, :], in0=craw[r, g, TAPS - 1 - t:TAPS - 1 - t + SEQ],
                                                   scalar=cw[r, g, TAPS - 1 - t:TAPS - t], in1=acc[r, g, :],
                                                   op0=ALU.mult, op1=ALU.add)
                    if t < TAPS - 1:
                        step(dve, ins, S.taps, first + (t + 1))
                    else:
                        ins.then_inc(S.conv, 1)

            def close(s):
                dve.wait_ge(S.rs, s + 1)
                dve.wait_ge(S.out, s + 1)
                for j in range(TILES):
                    t = bass.ds(s * TILES + j, 1)
                    last = dve.scalar_tensor_tensor(out=y_tok[:, t, :].squeeze(1), in0=psO[:, j * P:(j + 1) * P],
                                                    scalar=rs[:, j:j + 1], in1=xn_tok[:, t, :].squeeze(1), op0=ALU.mult, op1=ALU.add)
                last.then_inc(S.y, 1)

            def mean_squares(s):
                dve.wait_ge(S.ms, s + 1)
                dve.tensor_scalar(rs[:, :], psM[:, 0:TILES], 1.0 / INNER, EPS, ALU.mult, ALU.add).then_inc(S.rv, 1)

            def back(b, q):
                for c in range(TILES):
                    k = b * TILES + c
                    dve.wait_ge(S.xtok, k + 1)
                    dve.wait_ge(S.Y, k + 1)
                    step(dve, dve.tensor_tensor(Xdt[:, :, :], psX[:, 0:SHEADS * HD].rearrange("p (h d) -> p h d", h=SHEADS),
                                                spread(dt[:, q, c, :], 2, HD), ALU.mult), S.Xdt, k + 2)
                    dve.tensor_copy(Btok[:, :], psX[:, 2 * P:2 * P + SSTATE]).then_inc(S.Btok, 1)
                    dve.wait_ge(S.G, k + 1)
                    step(dve, dve.tensor_tensor(Gm[:, :], psG[:, 0:P], tri[:, :], ALU.mult), S.Gm, k + 1)
                    ahead = not is_at(b, BATCH - 1)
                    if c == 1 and ahead:
                        step_sizes(b + 1, 1 - q)
                    if c >= 2 and ahead:
                        convolve(b + 1, 2 * c - 3)
                    dve.wait_ge(S.E, k + 2)
                    dve.tensor_tensor(M[:, :, :], E[:, :, :], spread(Gm[:, :], 1, SHEADS), ALU.mult).then_inc(S.M, 1)
                    dve.tensor_tensor(Xs[:, :, :], Xdt[:, :, :], E[:, :, P - 1:P].to_broadcast([P, SHEADS, HD]),
                                      ALU.mult).then_inc(S.Xs, 1)
                    dve.wait_ge(S.M, k + 1)
                    dve.wait_ge(S.St, k + 2)
                    add = psG[0:64, ST0:ST0 + SHEADS * HD].rearrange("p (h d) -> p h d", h=SHEADS)
                    if c == 0:
                        step(dve, dve.tensor_copy(state[:, 0, :, :], add), S.state, k + 2)
                    elif c < TILES - 1:
                        dve.wait_ge(S.dec, k + 2)
                        step(dve, dve.tensor_tensor(state[:, c % 2, :, :], state[:, (c - 1) % 2, :, :],
                                                    dec[:, :, P - 1:P].to_broadcast([64, SHEADS, HD]), ALU.mult),
                             S.decayed, 4 + b * 2 + c)
                        step(dve, dve.tensor_tensor(state[:, c % 2, :, :], state[:, c % 2, :, :], add, ALU.add), S.state, k + 2)
                    else:
                        dve.nop().then_inc(S.state, 1)
                    if c == 0 and not is_at(b, 0):
                        mean_squares(b - 1)
                        close(b - 1)
                    if c == 0 and ahead:
                        step_input(b + 1)
                    if c in (1, 2) and ahead:
                        convolve(b + 1, 2 * c - 2)
                dve.wait_ge(S.Y, b * TILES + (TILES + 1))
                for h in range(2):
                    dve.scalar_tensor_tensor(out=yg[:, h, :], in0=xc[:, q, 2 + h, :], scalar=Dcol[:, h:h + 1],
                                             in1=psY[:, h, :], op0=ALU.mult, op1=ALU.add).then_inc(S.skip, 1)
                dve.wait_ge(S.skip, b * 2 + 2)
                step(dve, dve.tensor_tensor(yg[:, :, :], yg[:, :, :], zs[:, q, :, :], ALU.mult), S.yg, b + 2)

            lead(dve, S.Xdt, 1)
            lead(dve, S.Btok, 1)
            lead(dve, S.Xs, 1)
            lead(dve, S.state, 1)
            lead(dve, S.yg, 1)
            step_input(0)
            step_sizes(0, 0)
            for g in range(GROUPS2):
                convolve(0, g)
            sequence_turns(dve, back)
            mean_squares(BATCH - 1)
            close(BATCH - 1)


def layout2(a, np):
    f = np.float32
    cw, cb = a["L1_attn_conv_w"], a["L1_attn_conv_b"]
    w = np.concatenate([cw, cb[:, None]], 1)
    zero = np.zeros((64, TAPS + 1), f)
    conv = np.concatenate([w[INNER:INNER + 64], zero, w[INNER + 64:], zero, w[:P], w[P:INNER]], 0)
    row = lambda v: np.tile(v[None], (P, 1))
    two = lambda v: v.reshape(2, P).T
    return {
        "m_in": a["L1_attn_W_in"].T,
        "m_small": np.concatenate([conv.reshape(GROUPS2, P, TAPS + 1).transpose(1, 0, 2).reshape(P, -1),
                                   row(a["L1_attn_dt_bias"]), row(a["L1_attn_A_log"]),
                                   two(np.repeat(a["L1_attn_D"], HD)), two(a["L1_attn_norm_w"])], 1),
        "m_out": a["L1_attn_W_out"].T.reshape(2, P, D).transpose(1, 0, 2),
        "m_tri": np.triu(np.ones((P, P), f)),
        "m_strict": np.tril(np.ones((P, P), f), -1),
    }


EXPERTS, FF = 8, 512
KF = FF // P
EC = 2 * FF + KF + 2


def stage3_route(nc, x_tok, xn_tok, con, centT, xT, gates):
    with ExitStack() as ctx:
        sb = lambda n, s: ctx.enter_context(nc.sbuf_tensor(f"g3_{n}", s, F32))
        S = semaphores(nc, ctx, "g3", "n0 n1 x0 x1 xt nt raw xT aff affs ex own")
        raw_in, norm_in = sb("raw_in", [P, 2, TILES, D]), sb("norm_in", [P, 2, TILES, D])
        rawT = sb("rawT", [P, 2, SEQ])
        aff, score = sb("aff", [P, NT, EXPERTS]), sb("score", [P, NT, EXPERTS])
        top, alpha = sb("top", [P, NT]), sb("alpha", [P, NT])
        pb = lambda n: ctx.enter_context(nc.psum_tensor(f"g3_{n}", [P, 2, 512], F32))
        ps_x, ps_n, ps_a = pb("ps_x"), pb("ps_n"), pb("ps_a")
        block = ctx.enter_context(nc.Block())

        @block.sync
        def _(sp):
            with sp.Fori(0, BATCH // 2) as i:
                for q in range(2):
                    b = 2 * i + q
                    sp.wait_ge(S.nt, b + 1)
                    sp.dma_start(raw_in[:, q, :, :], x_tok[:, bass.ds(b * TILES, TILES), :]).then_inc((S.x0, S.x1)[q], 16)
                    sp.dma_start(norm_in[:, q, :, :], xn_tok[:, bass.ds(b * TILES, TILES), :]).then_inc((S.n0, S.n1)[q], 16)

        @block.tensor
        def _(pe):
            lead(pe, S.nt, 2)
            with pe.Fori(0, BATCH // 2) as i:
                for q in range(2):
                    b = 2 * i + q
                    pe.wait_ge(S.xT, b + 1)
                    pe.wait_ge((S.x0, S.x1)[q], i * 16 + 16)
                    for j in range(TILES):
                        last = pe.transpose(ps_x[:, q, j * P:(j + 1) * P], raw_in[:, q, j, :], con["ident"])
                    last.then_inc(S.xt, 1)
                    pe.wait_ge((S.n0, S.n1)[q], i * 16 + 16)
                    for j in range(TILES):
                        last = pe.transpose(ps_n[:, q, j * P:(j + 1) * P], norm_in[:, q, j, :], con["ident"])
                    last.then_inc(S.nt, 1)
                    pe.wait_ge(S.raw, b + 1)
                    pe.wait_ge(S.affs, b + 1)
                    for j in range(TILES):
                        last = pe.matmul(ps_a[:, q, j * EXPERTS:(j + 1) * EXPERTS], rawT[:, q, j * P:(j + 1) * P], centT,
                                         start=True, stop=True, skip_group_check=True)
                    last.then_inc(S.aff, 1)

        @block.scalar
        def _(act):
            lead(act, S.xT, 2)
            with act.Fori(0, BATCH // 2) as i:
                for q in range(2):
                    b = 2 * i + q
                    act.wait_ge(S.xt, b + 1)
                    act.copy(rawT[:, q, :], ps_x[:, q, :]).then_inc(S.raw, 1)
                    act.wait_ge(S.nt, b + 3)
                    act.copy(xT[:, bass.ds(b * SEQ, SEQ)], ps_n[:, q, :]).then_inc(S.xT, 1)
            act.wait_ge(S.own, 1)
            act.activation(alpha[:, :], top[:, :], ACT.Exp, scale=-1.0).then_inc(S.ex, 1)

        @block.vector
        def _(dve):
            lead(dve, S.affs, 2)
            with dve.Fori(0, BATCH // 2) as i:
                for q in range(2):
                    b = 2 * i + q
                    dve.wait_ge(S.aff, b + 1)
                    dve.tensor_copy(aff[:, bass.ds(b * TILES, TILES), :],
                                    ps_a[:, q, 0:TILES * EXPERTS].rearrange("p (j e) -> p j e", j=TILES)).then_inc(S.affs, 1)
            dve.wait_ge(S.affs, 2 + BATCH)
            own = Order(dve, S.own)
            own(dve.tensor_reduce(top[:, :], aff[:, :, :], AX.X, ALU.max))
            own(dve.tensor_tensor(score[:, :, :], aff[:, :, :], spread(top[:, :], 2, EXPERTS), ALU.is_equal))
            own(dve.tensor_tensor(score[:, :, :], score[:, :, :], spread(con["countdown"], 1, NT), ALU.mult))
            dve.wait_ge(S.ex, 1)
            own(dve.tensor_reduce(top[:, :], score[:, :, :], AX.X, ALU.max))
            own(dve.tensor_tensor(score[:, :, :], score[:, :, :], spread(top[:, :], 2, EXPERTS), ALU.is_equal))
            own(dve.tensor_scalar(alpha[:, :], alpha[:, :], 1.0, None, ALU.add))
            own(dve.reciprocal(alpha[:, :], alpha[:, :]))
            own(dve.tensor_tensor(gates[:, :, :], score[:, :, :], spread(alpha[:, :], 2, EXPERTS), ALU.mult))


def edge_turns(eng, turn, n):
    turn(0)
    with eng.Fori(0, n - 2) as i:
        turn(i + 1)
    turn(n - 1)


def stage3_experts(nc, con, dram, xT, gates, acc):
    with ExitStack() as ctx:
        sb = lambda n, s: ctx.enter_context(nc.sbuf_tensor(f"e3_{n}", s, F32))
        S = semaphores(nc, ctx, "e3", " ".join(f"w{e}" for e in range(EXPERTS)) + " x up hA hV down acc own")
        wts = sb("wts", [P, EXPERTS, EC])
        xe = sb("xe", [P, 2, SEQ])
        hid = sb("hid", [P, 2, KF, SEQ])
        ps_u = ctx.enter_context(nc.psum_tensor("e3_ps_u", [P, KF, 512], F32))
        ps_d = ctx.enter_context(nc.psum_tensor("e3_ps_d", [P, 2, 512], F32))
        loaded = S[:EXPERTS]
        w1 = lambda e, f: wts[:, e, f * P:(f + 1) * P]
        w2 = lambda e, f: wts[:, e, FF + f * P:FF + (f + 1) * P]
        b1 = lambda e, f: wts[:, e, 2 * FF + f:2 * FF + f + 1]
        ACT_F = KF - 1
        block = ctx.enter_context(nc.Block())

        def following(b, e):
            if e + 1 < EXPERTS:
                return b, e + 1
            return None if is_at(b, BATCH - 1) else (b + 1, 0)

        def preceding(b, e):
            if e:
                return b, e - 1
            return None if is_at(b, 0) else (b - 1, EXPERTS - 1)

        @block.sync
        def _(sp):
            for e in range(EXPERTS):
                sp.dma_start(wts[:, e, :], dram["ew"][:, e, :]).then_inc(loaded[e], 16)

        @block.tensor
        def _(pe):
            def ups(b, e):
                m = b * EXPERTS + e
                pe.wait_ge(loaded[e], 16)
                pe.wait_ge(S.x, m + 1)
                pe.wait_ge(S.hA, m + 1)
                pe.wait_ge(S.hV, m + 1)
                for f in range(KF):
                    pe.matmul(ps_u[:, f, :], w1(e, f), xe[:, e % 2, :], start=True, stop=True).then_inc(S.up, 1)

            def turn(b):
                for e in range(EXPERTS):
                    m = b * EXPERTS + e
                    if following(b, e):
                        ups(*following(b, e))
                    else:
                        pe.wait_ge(S.hA, m + 2)
                        pe.wait_ge(S.hV, m + 2)
                    pe.wait_ge(S.acc, m + 1)
                    for j in range(TILES):
                        for f in range(KF):
                            last = pe.matmul(ps_d[:, e % 2, j * P:(j + 1) * P], hid[:, e % 2, f, j * P:(j + 1) * P], w2(e, f),
                                             start=f == 0, stop=f == KF - 1)
                    last.then_inc(S.down, 1)

            lead(pe, S.down, 2)
            ups(0, 0)
            edge_turns(pe, turn, BATCH)

        @block.scalar
        def _(act):
            def turn(b):
                for e in range(EXPERTS):
                    m = b * EXPERTS + e
                    act.wait_ge(S.down, m + 1)
                    for f in range(ACT_F):
                        act.wait_ge(S.up, m * KF + (f + 1))
                        last = act.activation(hid[:, e % 2, f, :], ps_u[:, f, :], ACT.Relu, bias=b1(e, f))
                    last.then_inc(S.hA, 1)

            lead(act, S.hA, 1)
            for e in range(EXPERTS):
                act.wait_ge(loaded[e], 16)
            edge_turns(act, turn, BATCH)

        @block.vector
        def _(dve):
            def affine(b, e):
                dve.tensor_scalar(xe[:, e % 2, :], xT[:, bass.ds(b * SEQ, SEQ)], wts[:, e, EC - 2:EC - 1],
                                  wts[:, e, EC - 1:EC], ALU.mult, ALU.add).then_inc(S.x, 1)

            def add(b, e):
                m = b * EXPERTS + e
                dve.wait_ge(S.down, m + 3)
                for j in range(TILES):
                    t = b * TILES + j
                    a = acc[:, bass.ds(t, 1), :].squeeze(1)
                    last = dve.scalar_tensor_tensor(out=a, in0=ps_d[:, e % 2, j * P:(j + 1) * P],
                                                    scalar=gates[:, bass.ds(t, 1), e], in1=a, op0=ALU.mult, op1=ALU.add)
                last.then_inc(S.acc, 1)
                dve.wait_ge(S.acc, m + 3)

            def turn(b):
                for e in range(EXPERTS):
                    m = b * EXPERTS + e
                    if following(b, e):
                        affine(*following(b, e))
                    dve.wait_ge(S.down, m + 1)
                    for f in range(ACT_F, KF):
                        dve.wait_ge(S.up, m * KF + (f + 1))
                        last = dve.tensor_scalar(hid[:, e % 2, f, :], ps_u[:, f, :], b1(e, f), 0.0, ALU.add, ALU.max)
                    last.then_inc(S.hV, 1)
                    if preceding(b, e):
                        add(*preceding(b, e))

            lead(dve, S.hV, 1)
            lead(dve, S.acc, 2)
            for e in range(EXPERTS):
                dve.wait_ge(loaded[e], 16)
            affine(0, 0)
            edge_turns(dve, turn, BATCH)
            add(BATCH - 1, EXPERTS - 1)


TB = P // EXPERTS


def stage3_biases(nc, con, gates, b2, x, y):
    with ExitStack() as ctx:
        S = semaphores(nc, ctx, "b3", "gt gT bias sum")
        gT = ctx.enter_context(nc.sbuf_tensor("b3_gT", [P, NT // TB, P], F32))
        ps_t = ctx.enter_context(nc.psum_tensor("b3_ps_t", [P, NT // TB, 512], F32))
        ps = ctx.enter_context(nc.psum_tensor("b3_ps", [P, TB // TILES, 512], F32))
        block = ctx.enter_context(nc.Block())

        @block.tensor
        def _(pe):
            for i in range(NT // TB):
                pe.transpose(ps_t[:, i, 0:P], gates[:, i * TB:(i + 1) * TB, :].rearrange("p t e -> p (t e)"),
                             con["ident"]).then_inc(S.gt, 1)
            for i in range(NT // TB):
                pe.wait_ge(S.gT, i + 1)
                for j in range(TB // TILES):
                    if i:
                        pe.wait_ge(S.sum, (i - 1) * (TB // TILES) + j + 1)
                    pe.matmul(ps[:, j, :], gT[:, i, :], b2[:, j * TILES:(j + 1) * TILES, :].rearrange("p t d -> p (t d)"),
                              start=True, stop=True).then_inc(S.bias, 1)

        @block.scalar
        def _(act):
            for i in range(NT // TB):
                act.wait_ge(S.gt, i + 1)
                act.copy(gT[:, i, :], ps_t[:, i, 0:P]).then_inc(S.gT, 1)

        @block.vector
        def _(dve):
            for i in range(NT // TILES):
                t = slice(i * TILES, (i + 1) * TILES)
                dve.wait_ge(S.bias, i + 1)
                dve.tensor_tensor(y[:, t, :], x[:, t, :], ps[:, i % (TB // TILES), :].rearrange("p (j d) -> p j d", j=TILES),
                                  ALU.add).then_inc(S.sum, 1)


def stage3(nc, xn_tok, y_tok, con, dram):
    with ExitStack() as ctx:
        sb = lambda n, s: ctx.enter_context(nc.sbuf_tensor(f"s3_{n}", s, F32))
        S = semaphores(nc, ctx, "s3", "load b2")
        small = sb("small", [P, EXPERTS])
        xT, gates = sb("xT", [P, BATCH * SEQ]), sb("gates", [P, NT, EXPERTS])
        twice = sb("twice", [P, NT, D])
        b2 = sb("b2", [P, TB, D])
        with nc.Block() as block:
            @block.sync
            def _(sp):
                sp.dma_start(small[:, :], dram["e_small"]).then_inc(S.load, 16)
                sp.dma_start(b2[:, :, :], dram["eb2"]).then_inc(S.b2, 16)
                sp.wait_ge(S.load, 16)
                sp.wait_ge(S.b2, 16)
        normalize(nc, "n3b", con, None, xn_tok, twice)
        stage3_route(nc, xn_tok, twice, con, small[:, 0:EXPERTS], xT, gates)
        stage3_biases(nc, con, gates, b2, xn_tok, y_tok)
        stage3_experts(nc, con, dram, xT, gates, y_tok)


def layout3(a, np):
    w1 = a["L1_ffn_w1"].transpose(1, 0, 2)
    b2 = np.zeros((TB, EXPERTS, TB, D), np.float32)
    b2[np.arange(TB), :, np.arange(TB), :] = a["L1_ffn_b2"][None]
    b2 = b2.reshape(P, TB, D)
    w2 = a["L1_ffn_w2"].reshape(EXPERTS, KF, P, D).transpose(2, 0, 1, 3).reshape(P, EXPERTS, FF)
    return {
        "ew": np.concatenate([w1, w2, a["L1_ffn_b1"].reshape(EXPERTS, KF, P).transpose(2, 0, 1),
                              a["L1_ffn_ln_g"].T[:, :, None], a["L1_ffn_ln_b"].T[:, :, None]], 2),
        "eb2": b2,
        "e_small": a["L1_ffn_centroids"].T,
    }

def host_layout(a, np):
    return {**layout1(a, np), **layout2(a, np), **layout3(a, np)}


def build(nc, x, consts, w0, out, extra):
    with ExitStack() as ctx:
        sb = lambda n, s, t=F32: ctx.enter_context(nc.sbuf_tensor(n, s, t))
        x_tok, xn_tok, y_tok = (sb(n, [P, NT, D]) for n in ("x_tok", "xn_tok", "y_tok"))
        kc = sb("con_sb", [P, 2 * P + 2 * 64 + 1 + 8])
        con = dict(ident=kc[:, 0:P], ones=kc[:, P:2 * P], half=kc[:, 2 * P:2 * P + 64],
                   mhalf=kc[:, 2 * P + 64:2 * P + 128], clamp_dt=kc[:, 2 * P + 128:2 * P + 129],
                   countdown=kc[:, 2 * P + 129:2 * P + 137])
        S = semaphores(nc, ctx, "io", "load store")
        tiles = lambda t: t.rearrange("b (j p) d -> p (b j) d", p=P)
        with nc.Block() as block:
            @block.sync
            def _(sp):
                sp.dma_start(kc[:, :], consts).then_inc(S.load, 16)
                sp.dma_start(x_tok[:, :, :], tiles(x)).then_inc(S.load, 16)
                sp.wait_ge(S.load, 32)
        y = None
        for stage in range(FIRST, STAGES):
            xn = y_tok if stage == 1 else xn_tok
            weights = ExitStack()
            if stage == 1:
                w1 = stage1_load(nc, weights, extra)
            normalize(nc, f"n{stage}", con, y, x_tok, xn)
            y = y_tok
            if stage == 0:
                stage0(nc, xn, y, con, w0)
            if stage == 1:
                stage1(nc, y, con, w1)
            if stage == 2:
                stage2(nc, xn, y, con, extra)
            if stage == 3:
                stage3(nc, xn, y, con, extra)
            weights.close()
        normalize(nc, "n4", con, y_tok, x_tok, None)
        with nc.Block() as block:
            @block.sync
            def _(sp):
                sp.dma_start(tiles(out), x_tok[:, :, :]).then_inc(S.store, 16)
                sp.wait_ge(S.store, 16)


def kernel(**inputs):
    import numpy as np
    import concourse.bacc as bacc
    from concourse.bass_utils import run_bass_kernel_spmd

    a = {k: np.asarray(v) for k, v in inputs.items()}
    f = np.float32
    c, r = (0.1 + 0.001) / 2, (0.1 - 0.001) / 2
    arrays = {
        "x": a["L0_attn_x"],
        "consts": np.concatenate([np.eye(P, dtype=f), np.ones((P, P), f), np.full((P, 64), 0.5, f),
                                  np.full((P, 64), -0.5, f), np.full((P, 1), -c * 0.5 / (r + 1e-8), f),
                                  np.tile(np.arange(8, 0, -1, dtype=f), (P, 1))], 1),
        "w0": np.concatenate([a["L0_attn_W_dt"].T, a["L0_attn_W_B"].T, a["L0_attn_W_C"].T, a["L0_attn_A_log"],
                              a["L0_attn_b_dt"][:, None], a["L0_attn_D_param"][:, None]], 1),
    }
    arrays.update(host_layout(a, np))
    arrays = {k: np.ascontiguousarray(v) for k, v in arrays.items()}
    nc = bacc.Bacc("TRN2", target_bir_lowering=False, num_devices=1)
    dram = {k: nc.dram_tensor(k, v.shape, mybir.dt.from_np(v.dtype), kind="ExternalInput").ap() for k, v in arrays.items()}
    out = nc.dram_tensor("out", a["L0_attn_x"].shape, F32, kind="ExternalOutput").ap()
    build(nc, dram.pop("x"), dram.pop("consts"), dram.pop("w0"), out, dram)
    result = run_bass_kernel_spmd(nc, [arrays], core_ids=[0])
    return result.results[0]["out"]
```
